# Optimizing a Trainium2 kernel written in Bass

```python
import numpy as np
import jax
import jax.numpy as jnp

def _softmax(x, axis=-1):
    return jax.nn.softmax(x, axis=axis)

def _gelu(x):
    return jax.nn.gelu(x, approximate=True)

def _silu(x):
    return jax.nn.silu(x)

def _sigmoid(x):
    return jax.nn.sigmoid(x)

def _layernorm(x, axis=-1, eps=1e-05):
    m = jnp.mean(x, axis=axis, keepdims=True)
    v = jnp.var(x, axis=axis, keepdims=True)
    return (x - m) / jnp.sqrt(v + eps)

def _scatter_add(tgt, idx, src, axis=0):
    return tgt.at[idx].add(src)

def _segment_sum(src, seg, n):
    return jax.ops.segment_sum(src, seg, n)
kernel_name = 'mk_adaln_d1_jaxref_r8_351b4a'

def setup_inputs(seed: int=0):
    np.random.seed(seed)
    _w = jnp.asarray

    def _L0_attn_setup():
        import jax, jax.numpy as jnp
        import numpy as np
        DIM = 128
        H = 16
        DH = DIM // H
        NF = 64
        EPS = 1e-06
        key = jax.random.key(seed)
        ks = jax.random.split(key, 10)
        B, L = (4, 512)
        s = 1.0 / np.sqrt(DIM)
        x = jax.random.normal(ks[0], (B, L, DIM), dtype=jnp.float32)
        Wq = jax.random.normal(ks[1], (DIM, DIM), dtype=jnp.float32) * s
        Wk = jax.random.normal(ks[2], (DIM, DIM), dtype=jnp.float32) * s
        Wv = jax.random.normal(ks[3], (DIM, DIM), dtype=jnp.float32) * s
        Wo = jax.random.normal(ks[4], (DIM, DIM), dtype=jnp.float32) * s
        bq = jax.random.normal(ks[5], (DIM,), dtype=jnp.float32) * s
        bk = jax.random.normal(ks[6], (DIM,), dtype=jnp.float32) * s
        bv = jax.random.normal(ks[7], (DIM,), dtype=jnp.float32) * s
        bo = jax.random.normal(ks[8], (DIM,), dtype=jnp.float32) * s
        Wrf = jax.random.normal(ks[9], (1, H, DH, NF), dtype=jnp.float32)
        return {'x': x, 'Wq': Wq, 'bq': bq, 'Wk': Wk, 'bk': bk, 'Wv': Wv, 'bv': bv, 'Wo': Wo, 'bo': bo, 'Wrf': Wrf}
    _L0_attn_in = _L0_attn_setup()

    def _L0_ffn_setup():
        import jax, jax.numpy as jnp
        import numpy as np
        DIM = 128
        DEPTH = 6
        HEADS = 16
        DIM_HEAD = 64
        WINDOW = 32
        INNER = HEADS * DIM_HEAD
        DIM_INNER = int(DIM * 4 * 2 / 3)
        QK_SCALE = 8.0

        def shift_tokens(t):
            a, s = jnp.split(t, 2, -1)
            s = jnp.pad(s, ((0, 0), (1, 0), (0, 0)))[:, :-1]
            return jnp.concatenate([a, s], -1)

        def l2norm(t):
            return t / jnp.maximum(jnp.linalg.norm(t, axis=-1, keepdims=True), 1e-12)

        def rotate_half(x):
            x1, x2 = jnp.split(x, 2, -1)
            return jnp.concatenate([-x2, x1], -1)

        def rotary_tables(n):
            half = jnp.arange(0, DIM_HEAD, 2, dtype=jnp.float32)
            inv_freq = 1.0 / 10000.0 ** (half / DIM_HEAD)
            t = jnp.arange(n, dtype=jnp.float32)
            freqs = t[:, None] * inv_freq[None, :]
            freqs = jnp.concatenate([freqs, freqs], -1)
            base_scale = (half + 0.4 * DIM_HEAD) / (1.4 * DIM_HEAD)
            power = (t - n // 2) / (WINDOW // 2)
            scale = base_scale[None, :] ** power[:, None]
            scale = jnp.concatenate([scale, scale], -1)
            return (freqs, scale)

        def local_attention(q, k, v):
            b, h, n, d = q.shape
            w = WINDOW
            nw = n // w
            bq = q.reshape(b, h, nw, w, d)
            bk = k.reshape(b, h, nw, w, d)
            bv = v.reshape(b, h, nw, w, d)

            def look(t):
                p = jnp.pad(t, ((0, 0), (0, 0), (1, 0), (0, 0), (0, 0)))
                return jnp.concatenate([p[:, :, :nw], p[:, :, 1:]], axis=3)
            bk2, bv2 = (look(bk), look(bv))
            seq = jnp.arange(n).reshape(nw, w)
            seq_p = jnp.pad(seq, ((1, 0), (0, 0)), constant_values=-1)
            jt = jnp.concatenate([seq_p[:nw], seq_p[1:]], axis=1)
            it = seq[:, :, None]
            jb = jt[:, None, :]
            mask = (it < jb) | (it > jb + w) | (jb == -1)
            sim = jnp.einsum('bhwie,bhwje->bhwij', bq, bk2) * QK_SCALE
            sim = jnp.where(mask, -jnp.finfo(sim.dtype).max, sim)
            attn = jax.nn.softmax(sim, -1)
            out = jnp.einsum('bhwij,bhwje->bhwie', attn, bv2)
            return out.reshape(b, h, n, d)

        def attn_layer(x, Wqkv, qs, ksc, Wo):
            b, n, _ = x.shape
            qkv = x @ Wqkv
            q, k, v = jnp.split(qkv, 3, -1)
            sh = lambda t: t.reshape(b, n, HEADS, DIM_HEAD).transpose(0, 2, 1, 3)
            q, k, v = (sh(q), sh(k), sh(v))
            q = l2norm(q) * qs
            k = l2norm(k) * ksc
            freqs, scale = rotary_tables(n)
            cos, sin = (jnp.cos(freqs), jnp.sin(freqs))
            q = q * cos * scale + rotate_half(q) * sin * scale
            inv = 1.0 / scale
            k = k * cos * inv + rotate_half(k) * sin * inv
            out = local_attention(q, k, v)
            out = out.transpose(0, 2, 1, 3).reshape(b, n, INNER)
            return out @ Wo

        def ffn_layer(x, g, bln, W1, b1, W2, b2):
            mu = x.mean(-1, keepdims=True)
            var = ((x - mu) ** 2).mean(-1, keepdims=True)
            xn = (x - mu) / jnp.sqrt(var + 1e-05) * g + bln
            hg = xn @ W1 + b1
            a, gate = jnp.split(hg, 2, -1)
            return a * jax.nn.gelu(gate, approximate=False) @ W2 + b2
        key = jax.random.key(seed)
        ks = jax.random.split(key, 8)
        B, N = (2, 256)
        init = lambda k, shape: jax.random.normal(k, shape, jnp.float32) * 0.02
        return {'x': jax.random.normal(ks[0], (B, N, DIM), jnp.float32), 'Wqkv': init(ks[1], (DEPTH, DIM, 3 * INNER)), 'q_scale': jnp.ones((DEPTH, DIM_HEAD), jnp.float32), 'k_scale': jnp.ones((DEPTH, DIM_HEAD), jnp.float32), 'Wo': init(ks[2], (DEPTH, INNER, DIM)), 'ln_g': jnp.ones((DEPTH, DIM), jnp.float32), 'ln_b': jnp.zeros((DEPTH, DIM), jnp.float32), 'W1': init(ks[3], (DEPTH, DIM, 2 * DIM_INNER)), 'b1': jnp.zeros((DEPTH, 2 * DIM_INNER), jnp.float32), 'W2': init(ks[4], (DEPTH, DIM_INNER, DIM)), 'b2': jnp.zeros((DEPTH, DIM), jnp.float32)}
    _L0_ffn_in = _L0_ffn_setup()
    _L0_c = _w((lambda *s: np.random.randn(*s).astype(np.float32) * 0.05)(4, 128))
    _L0_wmod = _w((lambda *s: np.random.randn(*s).astype(np.float32) * 0.05)(128, 6 * 128) * 128 ** (-0.5))
    _d = {'L0_attn_x': _L0_attn_in['x'], 'L0_attn_Wq': _L0_attn_in['Wq'], 'L0_attn_bq': _L0_attn_in['bq'], 'L0_attn_Wk': _L0_attn_in['Wk'], 'L0_attn_bk': _L0_attn_in['bk'], 'L0_attn_Wv': _L0_attn_in['Wv'], 'L0_attn_bv': _L0_attn_in['bv'], 'L0_attn_Wo': _L0_attn_in['Wo'], 'L0_attn_bo': _L0_attn_in['bo'], 'L0_attn_Wrf': _L0_attn_in['Wrf'], 'L0_ffn_Wqkv': _L0_ffn_in['Wqkv'], 'L0_ffn_q_scale': _L0_ffn_in['q_scale'], 'L0_ffn_k_scale': _L0_ffn_in['k_scale'], 'L0_ffn_Wo': _L0_ffn_in['Wo'], 'L0_ffn_ln_g': _L0_ffn_in['ln_g'], 'L0_ffn_ln_b': _L0_ffn_in['ln_b'], 'L0_ffn_W1': _L0_ffn_in['W1'], 'L0_ffn_b1': _L0_ffn_in['b1'], 'L0_ffn_W2': _L0_ffn_in['W2'], 'L0_ffn_b2': _L0_ffn_in['b2'], 'L0_c': _L0_c, 'L0_wmod': _L0_wmod}
    _x0 = _d['L0_attn_x']
    _d['L0_attn_x'] = jax.random.normal(jax.random.fold_in(jax.random.key(seed), 1), (4, 512, 128), dtype=_x0.dtype)
    del _x0
    return _d

def reference(L0_attn_x, L0_attn_Wq, L0_attn_bq, L0_attn_Wk, L0_attn_bk, L0_attn_Wv, L0_attn_bv, L0_attn_Wo, L0_attn_bo, L0_attn_Wrf, L0_ffn_Wqkv, L0_ffn_q_scale, L0_ffn_k_scale, L0_ffn_Wo, L0_ffn_ln_g, L0_ffn_ln_b, L0_ffn_W1, L0_ffn_b1, L0_ffn_W2, L0_ffn_b2, L0_c, L0_wmod):

    def _L0_attn_ref(x, Wq, bq, Wk, bk, Wv, bv, Wo, bo, Wrf):
        import jax, jax.numpy as jnp
        import numpy as np
        DIM = 128
        H = 16
        DH = DIM // H
        NF = 64
        EPS = 1e-06
        B, L, _ = x.shape
        W0 = Wrf[0]

        def split_heads(y):
            return y.reshape(B, L, H, DH).transpose(0, 2, 1, 3)
        q = split_heads(x @ Wq.T + bq)
        k = split_heads(x @ Wk.T + bk)
        v = split_heads(x @ Wv.T + bv)
        logits = jnp.einsum('bhld,hdf->bhlf', k, W0) - 0.5 * jnp.sum(k * k, axis=-1, keepdims=True)
        alpha = jax.nn.softmax(logits.reshape(B, H, L * NF), axis=2)
        alpha = alpha.reshape(B, H, L, NF)
        N = jnp.einsum('bhlf,bhld->bhfd', alpha, v)
        D = jnp.sum(alpha, axis=2)
        phi = jax.nn.softmax(jnp.einsum('bhld,hdf->bhlf', q, W0), axis=-1)
        num = jnp.einsum('bhlf,bhfd->bhld', phi, N)
        den = jnp.einsum('bhlf,bhf->bhl', phi, D)
        out = num / (den[..., None] + EPS)
        ctx = out.transpose(0, 2, 1, 3).reshape(B, L, DIM)
        return ctx @ Wo.T + bo

    def _L0_ffn_ref(x, Wqkv, q_scale, k_scale, Wo, ln_g, ln_b, W1, b1, W2, b2):
        import jax, jax.numpy as jnp
        import numpy as np
        DIM = 128
        DEPTH = 6
        HEADS = 16
        DIM_HEAD = 64
        WINDOW = 32
        INNER = HEADS * DIM_HEAD
        DIM_INNER = int(DIM * 4 * 2 / 3)
        QK_SCALE = 8.0

        def shift_tokens(t):
            a, s = jnp.split(t, 2, -1)
            s = jnp.pad(s, ((0, 0), (1, 0), (0, 0)))[:, :-1]
            return jnp.concatenate([a, s], -1)

        def l2norm(t):
            return t / jnp.maximum(jnp.linalg.norm(t, axis=-1, keepdims=True), 1e-12)

        def rotate_half(x):
            x1, x2 = jnp.split(x, 2, -1)
            return jnp.concatenate([-x2, x1], -1)

        def rotary_tables(n):
            half = jnp.arange(0, DIM_HEAD, 2, dtype=jnp.float32)
            inv_freq = 1.0 / 10000.0 ** (half / DIM_HEAD)
            t = jnp.arange(n, dtype=jnp.float32)
            freqs = t[:, None] * inv_freq[None, :]
            freqs = jnp.concatenate([freqs, freqs], -1)
            base_scale = (half + 0.4 * DIM_HEAD) / (1.4 * DIM_HEAD)
            power = (t - n // 2) / (WINDOW // 2)
            scale = base_scale[None, :] ** power[:, None]
            scale = jnp.concatenate([scale, scale], -1)
            return (freqs, scale)

        def local_attention(q, k, v):
            b, h, n, d = q.shape
            w = WINDOW
            nw = n // w
            bq = q.reshape(b, h, nw, w, d)
            bk = k.reshape(b, h, nw, w, d)
            bv = v.reshape(b, h, nw, w, d)

            def look(t):
                p = jnp.pad(t, ((0, 0), (0, 0), (1, 0), (0, 0), (0, 0)))
                return jnp.concatenate([p[:, :, :nw], p[:, :, 1:]], axis=3)
            bk2, bv2 = (look(bk), look(bv))
            seq = jnp.arange(n).reshape(nw, w)
            seq_p = jnp.pad(seq, ((1, 0), (0, 0)), constant_values=-1)
            jt = jnp.concatenate([seq_p[:nw], seq_p[1:]], axis=1)
            it = seq[:, :, None]
            jb = jt[:, None, :]
            mask = (it < jb) | (it > jb + w) | (jb == -1)
            sim = jnp.einsum('bhwie,bhwje->bhwij', bq, bk2) * QK_SCALE
            sim = jnp.where(mask, -jnp.finfo(sim.dtype).max, sim)
            attn = jax.nn.softmax(sim, -1)
            out = jnp.einsum('bhwij,bhwje->bhwie', attn, bv2)
            return out.reshape(b, h, n, d)

        def attn_layer(x, Wqkv, qs, ksc, Wo):
            b, n, _ = x.shape
            qkv = x @ Wqkv
            q, k, v = jnp.split(qkv, 3, -1)
            sh = lambda t: t.reshape(b, n, HEADS, DIM_HEAD).transpose(0, 2, 1, 3)
            q, k, v = (sh(q), sh(k), sh(v))
            q = l2norm(q) * qs
            k = l2norm(k) * ksc
            freqs, scale = rotary_tables(n)
            cos, sin = (jnp.cos(freqs), jnp.sin(freqs))
            q = q * cos * scale + rotate_half(q) * sin * scale
            inv = 1.0 / scale
            k = k * cos * inv + rotate_half(k) * sin * inv
            out = local_attention(q, k, v)
            out = out.transpose(0, 2, 1, 3).reshape(b, n, INNER)
            return out @ Wo

        def ffn_layer(x, g, bln, W1, b1, W2, b2):
            mu = x.mean(-1, keepdims=True)
            var = ((x - mu) ** 2).mean(-1, keepdims=True)
            xn = (x - mu) / jnp.sqrt(var + 1e-05) * g + bln
            hg = xn @ W1 + b1
            a, gate = jnp.split(hg, 2, -1)
            return a * jax.nn.gelu(gate, approximate=False) @ W2 + b2
        for i in range(DEPTH):
            x = attn_layer(shift_tokens(x), Wqkv[i], q_scale[i], k_scale[i], Wo[i]) + x
            x = ffn_layer(shift_tokens(x), ln_g[i], ln_b[i], W1[i], b1[i], W2[i], b2[i]) + x
        return x
    x = L0_attn_x
    mod = (_silu(L0_c) @ L0_wmod).reshape(L0_c.shape[0], 6, 1, -1)
    sa, ca, ga, sb, cb, gb = (mod[:, 0], mod[:, 1], mod[:, 2], mod[:, 3], mod[:, 4], mod[:, 5])
    ga = (2 * (ga >= 0) - 1) * jnp.maximum(jnp.abs(ga), 0.25)
    gb = (2 * (gb >= 0) - 1) * jnp.maximum(jnp.abs(gb), 0.25)
    h = _layernorm(x, axis=-1) * (1 + ca) + sa
    x = x + ga * _L0_attn_ref(h, L0_attn_Wq, L0_attn_bq, L0_attn_Wk, L0_attn_bk, L0_attn_Wv, L0_attn_bv, L0_attn_Wo, L0_attn_bo, L0_attn_Wrf)
    h = _layernorm(x, axis=-1) * (1 + cb) + sb
    x = x + gb * _L0_ffn_ref(h, L0_ffn_Wqkv, L0_ffn_q_scale, L0_ffn_k_scale, L0_ffn_Wo, L0_ffn_ln_g, L0_ffn_ln_b, L0_ffn_W1, L0_ffn_b1, L0_ffn_W2, L0_ffn_b2)
    return x

_drawn_inputs = setup_inputs


def setup_inputs(seed=0):
    import zlib

    import numpy as np

    out = dict(_drawn_inputs(seed))
    spreads = {'L0_ffn_q_scale': (1.0, 0.6),
     'L0_ffn_k_scale': (1.0, 0.6),
     'L0_ffn_ln_g': (1.0, 0.6),
     'L0_ffn_ln_b': (0.0, 0.8),
     'L0_ffn_b1': (0.0, 0.8),
     'L0_ffn_b2': (0.0, 0.645)}
    factors = {'L0_attn_bq': 7.03, 'L0_attn_bk': 7.442, 'L0_ffn_W1': 7.39, 'L0_ffn_W2': 7.253}
    for name, (base, spread) in spreads.items():
        noise = np.random.default_rng([zlib.crc32(name.encode()), seed]).standard_normal(out[name].shape)
        drawn = base * np.exp(spread * noise) if base else spread * noise
        out[name] = jnp.asarray(drawn.astype(out[name].dtype))
    for name, factor in factors.items():
        out[name] = (out[name] * factor).astype(out[name].dtype)
    return out
```

```python
from contextlib import ExitStack

import numpy as np

import concourse.bass as bass
from concourse import mybir

F32 = mybir.dt.float32
F32R = mybir.dt.float32r
BF16 = mybir.dt.bfloat16
I32 = mybir.dt.int32
ALU = mybir.AluOpType
ACT = mybir.ActivationFunctionType
AX = mybir.AxisListType

P = 128
B, L, D = 4, 512, 128
NT = L // P
H1, DH1, NF = 16, 8, 64
EPS1 = 1e-6
LN_EPS = 1e-5
DEPTH = 6
H, DH = 16, 64
HP = H // 2
INNER = H * DH
WIN = 32
WPT = P // WIN
NW = L // WIN
FF = int(D * 4 * 2 / 3)
FT = [(0, 128), (128, 128), (256, FF - 256)]
QK_SCALE = 8.0
MASKED = -1e30
HALF = 512
UNITS = 2 * NT
RSQRT_SEED = float(0x5F3759DF)
NORM_FLOOR2 = 1e-24


def wait_for(eng, sem, value, alone=None):
    eng.wait_ge(sem, value)
    if alone is not None:
        eng.sem_inc(alone, 1)


class Signal:

    def __init__(self, sem, per, base=0):
        self.sem, self.per, self.base = sem, per, base

    def wait(self, eng, turn, n, alone=None):
        wait_for(eng, self.sem, turn * self.per + (n + self.base), alone)


class Chain:

    def __init__(self, sem, per):
        self.sem, self.per, self.n = sem, per, 0

    def start(self, eng, turn):
        self.eng, self.turn, self.n = eng, turn, 0

    def step(self, ins, alone=None):
        self.n += 1
        ins.then_inc(self.sem, 1)
        wait_for(self.eng, self.sem, self.turn * self.per + self.n, alone)

    def end(self):
        assert self.n == self.per, (self.n, self.per)


RSQRT_STEPS = 12


def rsqrt_steps(nc, chain, y, half, tmp, x):
    chain.step(nc.vector.tensor_scalar(y.bitcast(I32), x.bitcast(I32), 1, None, ALU.logical_shift_right))
    chain.step(nc.vector.tensor_scalar(y.bitcast(I32), y.bitcast(I32), -1.0, RSQRT_SEED, ALU.mult, ALU.add))
    chain.step(nc.vector.tensor_scalar(half, x, -0.5, None, ALU.mult))
    for _ in range(3):
        chain.step(nc.vector.tensor_tensor(tmp, y, y, ALU.mult))
        chain.step(nc.vector.tensor_tensor(tmp, tmp, half, ALU.mult))
        chain.step(nc.vector.scalar_tensor_tensor(y, tmp, 1.5, y, ALU.add, ALU.mult))


def bcast(ap, n):
    return ap.unsqueeze(2).broadcast_to([ap.shape[0], ap.shape[1], n])


def over_heads(ap, n):
    return ap.unsqueeze(1).broadcast_to([ap.shape[0], n, ap.shape[1]])


def halves_swapped(t, part, heads):
    a = t.rearrange("p (h s d) -> p h s d", s=2, d=DH // 2)
    return a[:, :, ::-1, :]


def attention1_block(nc, a, xr, x1_dram, mod, consts):
    ident, identr, onesblk, ones = (consts[n] for n in ("ident", "identr", "onesblk", "ones"))
    with ExitStack() as ctx:
        def sb(name, shape, dt=F32):
            return ctx.enter_context(nc.sbuf_tensor(name, shape, dt))

        def sem(name):
            return ctx.enter_context(nc.semaphore(name))

        x0 = sb("x0", [P, B * NT, D])
        wq, wk, wv, wo = (sb(n, [P, D]) for n in ("wq", "wk", "wv", "wo"))
        w0bd = sb("w0bd", [P, H1 * NF])
        selneg = sb("selneg", [P, H1])
        bcol = sb("bcol", [P, 3])
        bvrow = sb("bvrow", [P, D])
        cT = sb("cT", [P, B])
        cexp = sb("cexp", [P, B])
        wmod = sb("wmod", [P, 6 * D])
        gab = sb("gab", [P, B])
        sgn = sb("sgn", [P, B])
        stats = sb("stats", [P, NT, 6])
        mv = sb("mv", [P, NT, 2])
        rs, rh, rt, rx = (sb(n, [P, NT]) for n in ("rs", "rh", "rt", "rx"))
        hn = sb("hn", [P, NT, D])
        hT = sb("hT", [P, L])
        qT, kT, ksq = (sb(n, [P, L]) for n in ("qT1", "kT1", "ksq1"))
        vext = sb("vext", [P, NT, H1, DH1 + 1])
        ksum = sb("ksum", [P, NT * H1])
        lg = sb("lg", [P, NT, H1 * NF])
        mk = sb("mk", [P, NT, H1])
        mkt = sb("mkt", [P, H1])
        mh = sb("mh", [H1, 1])
        dm = sb("dm", [H1, H1])
        negm = sb("negm", [P, H1])
        nxt = sb("nxt", [P, H1 // 2, 2, DH1 + 1])
        dcol = sb("dcol", [P, H1 // 2])
        m1 = sb("m1", [P, 8])
        nm1 = sb("nm1", [P, 2, 8], F32R)
        phi = sb("phi", [P, 2, HALF])
        phiT = sb("phiT", [P, 2, HALF])
        rd = sb("rd", [P, 8])
        cx = sb("cx", [P, 2, D])
        cxT = sb("cxT", [P, L])
        yT = sb("yT", [P, L])
        x1s = sb("x1s", [P, NT, D])
        bk = [ctx.enter_context(nc.psum_tensor(f"a{i}", [P, 512], F32)) for i in range(8)]

        in_x, in_w, bd, out_x1, zeroed = (sem(n) for n in ("in_x", "in_w", "bd_loaded", "x1_stored", "zeroed"))
        s_silu, s_silu2, s_mod, s_gate = sem("silu_exp"), sem("silu_done"), sem("mod_ps"), sem("mod_sb")
        ch0 = Chain(sem("setup_chain"), 13)
        tally = sem("tally1")
        ch = Chain(sem("dve_chain1"), 91)
        S = {}

        def sig(name, per, base=0):
            S[name] = Signal(sem(name), per, base)
            return S[name]

        hn_ready = sig("hn_ready", 2)
        hT_ps = sig("hT_ps", 2)
        hT_sb = sig("hT_sb", 2)
        qkv_ps = sig("qkv_ps", 1)
        qk_sb = sig("qk_sb", 1)
        v_sb = sig("v_sb", 1)
        ks_ps = sig("ks_ps", 1)
        lg_ps = sig("lg_ps", 2 * NT)
        lg_used = sig("lg_used", 2 * NT, 2)
        mk_ready = sig("mk_ready", 1)
        mkT_ps = sig("mkT_ps", 1)
        dm_ready = sig("dm_ready", 1)
        negm_ps = sig("negm_ps", 1)
        lg_sub = sig("lg_sub", NT)
        e_ready = sig("e_ready", NT)
        n_ps = sig("n_ps", 1)
        d_ready = sig("d_ready", 1)
        dsum_ps = sig("dsum_ps", 1)
        nxt_ready = sig("nxt_ready", 1)
        lq_ps = sig("lq_ps", 2 * NT)
        nm_ready = sig("nm1_ready", 2 * NT)
        lq_shift = sig("lq_shift", 2 * NT)
        phi_ready = sig("phi_ready", 2 * NT)
        phiT_ps = sig("phiT_ps", 2 * NT)
        phiT_sb = sig("phiT_sb", 2 * NT)
        num_ps = sig("num_ps", 2 * NT)
        cx_ready = sig("cx_ready", NT)
        cxT_ps = sig("cxT_ps", 1)
        cxT_sb = sig("cxT_sb", 1)
        wo_ps = sig("wo_ps", 1)
        y_sb = sig("y_sb", 1)
        yt_ps = sig("yt_ps", 1)
        x1_ready = sig("x1_ready", 1)
        xb_ps = sig("xb_ps", 1)
        xr_ready = sig("xr_ready", 1)
        block = ctx.enter_context(nc.Block())

        @block.sync
        def _(sp):
            for t, src in ((x0[:], a["x"].rearrange("b (t p) d -> p (b t) d", p=P)),):
                sp.dma_start(t, src).then_inc(in_x, 16)
            loads = [(cT, a["cT"]), (wmod, a["wmod"]), (ident, a["ident"]), (bcol, a["bcol"]), (wq, a["WqT"]),
                     (wk, a["WkT"]), (wv, a["WvT"]), (wo, a["WoT"]), (selneg, a["selneg"]), (onesblk, a["onesblk"])]
            for t, src in loads:
                sp.dma_start(t[:], src).then_inc(in_w, 16)
            sp.dma_start(bvrow[:], a["bv"].partition_broadcast(P)).then_inc(in_w, 16)
            sp.wait_ge(zeroed, 1)
            for h in range(H1):
                sp.dma_start(w0bd[DH1 * h:DH1 * (h + 1), NF * h:NF * (h + 1)], a["Wrf"][0, h]).then_inc(bd, 16)
            with sp.Fori(0, B) as b:
                x1_ready.wait(sp, b, 1)
                sp.dma_start(x1_dram[b], x1s[:]).then_inc(out_x1, 16)
            sp.wait_ge(out_x1, 16 * B)

        NLOADS = 11

        @block.gpsimd
        def _(pool):
            nc.gpsimd.memset(w0bd[:], 0.0).then_inc(zeroed, 1)
            nc.gpsimd.memset(nxt[:], 0.0).then_inc(zeroed, 1)
            nc.gpsimd.memset(ones[:], 1.0).then_inc(zeroed, 1)
            nc.gpsimd.memset(vext[:], 1.0).then_inc(zeroed, 1)

        @block.scalar
        def _(act):
            act.wait_ge(in_w, 16 * NLOADS)
            nc.scalar.activation(cexp[:], cT[:], ACT.Exp, scale=-1.0).then_inc(s_silu, 1)
            act.wait_ge(s_gate, 1)
            with act.Fori(0, B) as b:
                hT_ps.wait(act, b, 1)
                nc.scalar.activation(hT[:], bk[0][:], ACT.Identity, bias=mod[:, 0, bass.ds(b, 1)],
                                     scale=mod[:, 1, bass.ds(b, 1)]).then_inc(hT_sb.sem, 1)
                qkv_ps.wait(act, b, 1)
                nc.scalar.activation(qT[:], bk[1][:], ACT.Identity, bias=bcol[:, 0:1])
                nc.scalar.activation(kT[:], bk[2][:], ACT.Identity, bias=bcol[:, 1:2])
                nc.scalar.activation(ksq[:], bk[2][:], ACT.Square, bias=bcol[:, 1:2]).then_inc(qk_sb.sem, 1)
                for t in range(NT):
                    lg_sub.wait(act, b, t + 1)
                    nc.scalar.activation(lg[:, t], lg[:, t], ACT.Exp).then_inc(e_ready.sem, 1)
                for u in range(2 * NT):
                    lq_shift.wait(act, b, u + 1)
                    if u >= 2:
                        phiT_ps.wait(act, b, u - 1)
                    nc.scalar.activation(phi[:, u % 2], bk[4 + u % 2][:], ACT.Exp).then_inc(phi_ready.sem, 1)
                    phiT_ps.wait(act, b, u + 1)
                    if u >= 2:
                        num_ps.wait(act, b, u - 1)
                    nc.scalar.activation(phiT[:, u % 2], bk[6][:], ACT.Copy).then_inc(phiT_sb.sem, 1)
                cxT_ps.wait(act, b, 1)
                nc.scalar.activation(cxT[:], bk[3][:], ACT.Copy).then_inc(cxT_sb.sem, 1)
                wo_ps.wait(act, b, 1)
                nc.scalar.activation(yT[:], bk[0][:], ACT.Identity, bias=gab[:, bass.ds(b, 1)],
                                     scale=mod[:, 2, bass.ds(b, 1)]).then_inc(y_sb.sem, 1)
                hT_ps.wait(act, b, 2)
                nc.scalar.activation(hT[:], bk[2][:], ACT.Identity, bias=mod[:, 3, bass.ds(b, 1)],
                                     scale=mod[:, 4, bass.ds(b, 1)]).then_inc(hT_sb.sem, 1)

        @block.vector
        def _(dve):
            ch0.start(dve, 0)
            dve.wait_ge(s_silu, 1)
            ch0.step(nc.vector.tensor_scalar(cexp[:], cexp[:], 1.0, None, ALU.add))
            ch0.step(nc.vector.reciprocal(cexp[:], cexp[:]))
            nc.vector.tensor_tensor(cT[:], cT[:], cexp[:], ALU.mult).then_inc(s_silu2, 1)
            nc.vector.tensor_copy(identr[:], ident[:]).then_inc(s_silu2, 1)
            dve.wait_ge(s_mod, 1)
            ch0.step(nc.vector.tensor_copy(mod[:], bk[0][:, 0:6 * B].rearrange("p (j b) -> p j b", b=B)))
            for j in (1, 4):
                ch0.step(nc.vector.tensor_scalar(mod[:, j], mod[:, j], 1.0, None, ALU.add))
            for j in (2, 5):
                ch0.step(nc.vector.tensor_scalar(sgn[:], mod[:, j], 0.0, 2.0, ALU.is_ge, ALU.mult))
                ch0.step(nc.vector.tensor_scalar(sgn[:], sgn[:], -1.0, None, ALU.add))
                ch0.step(nc.vector.scalar_tensor_tensor(mod[:, j], mod[:, j], -1.0, mod[:, j], ALU.mult, ALU.max))
                ch0.step(nc.vector.scalar_tensor_tensor(mod[:, j], mod[:, j], 0.25, sgn[:], ALU.max, ALU.mult))
            nc.vector.tensor_scalar(gab[:], mod[:, 2], bcol[:, 2:3], None, ALU.mult).then_inc(s_gate, 1)
            nc.vector.sem_inc(lg_used.sem, 2)
            dve.wait_ge(in_x, 16)
            dve.wait_ge(zeroed, 4)
            with dve.Fori(0, B) as b:
                ch.start(dve, b)

                def layernorm(src):
                    for t in range(NT):
                        ch.step(nc.vector.bn_stats(stats[:, t], src(t)), alone=tally)
                    for t in range(NT):
                        ch.step(nc.vector.bn_aggr(mv[:, t], stats[:, t]), alone=tally)
                    ch.step(nc.vector.tensor_scalar(rx[:], mv[:, :, 1], LN_EPS, None, ALU.add))
                    rsqrt_steps(nc, ch, rs[:], rh[:], rt[:], rx[:])
                    for t in range(NT):
                        ins = nc.vector.tensor_scalar(hn[:, t], src(t), mv[:, t, 0:1], rs[:, t:t + 1],
                                                      ALU.subtract, ALU.mult)
                        if t < NT - 1:
                            ch.step(ins)
                    ins.then_inc(hn_ready.sem, 1)

                layernorm(lambda t: x0[:, bass.ds(b * NT + t, 1), :].rearrange("p a d -> p (a d)"))
                qkv_ps.wait(dve, b, 1)
                nc.vector.tensor_tensor(vext[:, :, :, 0:DH1],
                                        bk[3][:].rearrange("p (t h d) -> p t h d", t=NT, h=H1),
                                        bvrow[:].rearrange("p (h d) -> p h d", h=H1).unsqueeze(1)
                                        .broadcast_to([P, NT, H1, DH1]), ALU.add).then_inc(v_sb.sem, 1)
                ks_ps.wait(dve, b, 1)
                ch.step(nc.vector.tensor_copy(ksum[:], bk[0][:, 0:NT * H1]))
                for u in range(2 * NT):
                    t, c = divmod(u, 2)
                    lg_ps.wait(dve, b, u + 1)
                    part = lg[:, t, c * HALF:(c + 1) * HALF].rearrange("p (h f) -> p h f", f=NF)
                    h0 = t * H1 + c * 8
                    nc.vector.tensor_tensor(part, bk[4 + u % 2][:].rearrange("p (h f) -> p h f", f=NF),
                                            bcast(ksum[:, h0:h0 + 8], NF), ALU.add).then_inc(lg_used.sem, 1)
                    lg_used.wait(dve, b, u + 1)
                    ch.step(nc.vector.tensor_reduce(mk[:, t, c * 8:c * 8 + 8], part, AX.X, ALU.max))
                nc.vector.tensor_reduce(mkt[:], mk[:].rearrange("p t h -> p h t"), AX.X, ALU.max)\
                    .then_inc(mk_ready.sem, 1)
                mkT_ps.wait(dve, b, 1)
                ch.step(nc.vector.tensor_reduce(mh[:], bk[0][0:H1, 64:64 + P], AX.X, ALU.max))
                nc.vector.tensor_scalar(dm[:], ident[0:H1, 0:H1], mh[:], -1.0, ALU.mult, ALU.mult)\
                    .then_inc(dm_ready.sem, 1)
                negm_ps.wait(dve, b, 1)
                ch.step(nc.vector.tensor_copy(negm[:], bk[0][:, 256:256 + H1]))
                for t in range(NT):
                    part = lg[:, t].rearrange("p (h f) -> p h f", f=NF)
                    nc.vector.tensor_tensor(part, part, bcast(negm[:], NF), ALU.add).then_inc(lg_sub.sem, 1)
                n_ps.wait(dve, b, 1)
                nps = bk[0][:, 288:288 + 8 * 18].rearrange("p (g k c) -> p g k c", g=8, k=2)
                ch.step(nc.vector.tensor_copy(nxt[0:64, :, 0, :], nps[0:64, :, 0, :]))
                ch.step(nc.vector.tensor_copy(nxt[64:P, :, 1, :], nps[64:P, :, 1, :]))
                ch.step(nc.vector.tensor_copy(dcol[0:64, :], nps[0:64, :, 0, DH1]))
                nc.vector.tensor_copy(dcol[64:P, :], nps[64:P, :, 1, DH1]).then_inc(d_ready.sem, 1)
                dsum_ps.wait(dve, b, 1)
                ch.step(nc.vector.scalar_tensor_tensor(nxt[0:64, :, 0, DH1], bk[0][0:64, 440:448], EPS1,
                                                       dcol[0:64, :], ALU.mult, ALU.add))
                nc.vector.scalar_tensor_tensor(nxt[64:P, :, 1, DH1], bk[0][64:P, 440:448], EPS1,
                                               dcol[64:P, :], ALU.mult, ALU.add).then_inc(nxt_ready.sem, 1)

                def ctx_out(u):
                    t, c = divmod(u, 2)
                    num_ps.wait(dve, b, u + 1)
                    v = bk[(7, 0)[c]][:, 0:72].rearrange("p (h c) -> p h c", c=DH1 + 1)
                    ch.step(nc.vector.reciprocal(rd[:], v[:, :, DH1]))
                    ins = nc.vector.tensor_tensor(
                        cx[:, t % 2, c * 64:c * 64 + 64].rearrange("p (h d) -> p h d", d=DH1),
                        v[:, :, 0:DH1], bcast(rd[:], DH1), ALU.mult)
                    if c == 0:
                        ch.step(ins)
                    else:
                        ins.then_inc(cx_ready.sem, 1)

                for u in range(2 * NT):
                    lq_ps.wait(dve, b, u + 1)
                    if u >= 1:
                        nm_ready.wait(dve, b, u)
                    ch.step(nc.vector.tensor_reduce(m1[:], bk[4 + u % 2][:].rearrange("p (h f) -> p h f", f=NF),
                                                    AX.X, ALU.max))
                    if u >= 1:
                        lq_shift.wait(dve, b, u)
                    ch.step(nc.vector.tensor_scalar(nm1[:, 0], m1[:], -1.0, None, ALU.mult))
                    nc.vector.scalar_tensor_tensor(nm1[:, 1], m1[:], -1.0, nm1[:, 0].bitcast(F32), ALU.mult,
                                                   ALU.subtract).then_inc(nm_ready.sem, 1)
                    if u >= 1:
                        ctx_out(u - 1)
                ctx_out(2 * NT - 1)
                yt_ps.wait(dve, b, 1)
                nc.vector.tensor_tensor(x1s[:], x0[:, bass.ds(b * NT, NT), :],
                                        bk[1][:].rearrange("p (t d) -> p t d", d=D), ALU.add)\
                    .then_inc(x1_ready.sem, 1)
                x1_ready.wait(dve, b, 1, alone=tally)
                layernorm(lambda t: x1s[:, t])
                xb_ps.wait(dve, b, 1, alone=tally)
                nc.vector.tensor_copy(xr[:, bass.ds(b * NT, NT), :], bk[3][:].rearrange("p (t d) -> p t d", d=D))\
                    .then_inc(xr_ready.sem, 1)
                dve.wait_ge(out_x1, b * 16 + 16)
                ch.end()

        @block.tensor
        def _(pe):
            pe.wait_ge(in_w, 16 * NLOADS)
            pe.wait_ge(s_silu2, 2)
            for j in range(6):
                last = nc.tensor.matmul(bk[0][:, j * B:(j + 1) * B], wmod[:, j * D:(j + 1) * D], cT[:],
                                        start=True, stop=True)
            last.then_inc(s_mod, 1)
            pe.wait_ge(bd, 16 * H1)
            pe.wait_ge(zeroed, 4)
            pe.wait_ge(s_gate, 1)

            def transposes(dst, src, last_sig):
                for t in range(NT):
                    last = nc.tensor.transpose(dst[:, t * P:(t + 1) * P], src(t), ident[:])
                last.then_inc(last_sig.sem, 1)

            with pe.Fori(0, B) as b:
                hn_ready.wait(pe, b, 1)
                transposes(bk[0], lambda t: hn[:, t], hT_ps)
                hT_sb.wait(pe, b, 1)
                nc.tensor.matmul(bk[1][:], wq[:], hT[:], start=True, stop=True)
                nc.tensor.matmul(bk[2][:], wk[:], hT[:], start=True, stop=True)
                for t in range(NT):
                    last = nc.tensor.matmul(bk[3][:, t * D:(t + 1) * D], hT[:, t * P:(t + 1) * P], wv[:],
                                            start=True, stop=True)
                last.then_inc(qkv_ps.sem, 1)
                qk_sb.wait(pe, b, 1)
                for t in range(NT):
                    last = nc.tensor.matmul(bk[0][:, t * H1:(t + 1) * H1], ksq[:, t * P:(t + 1) * P], selneg[:],
                                            start=True, stop=True)
                last.then_inc(ks_ps.sem, 1)
                for u in range(2 * NT):
                    t, c = divmod(u, 2)
                    lg_used.wait(pe, b, u - 1)
                    nc.tensor.matmul(bk[4 + u % 2][:], kT[:, t * P:(t + 1) * P], w0bd[:, c * HALF:(c + 1) * HALF],
                                     start=True, stop=True).then_inc(lg_ps.sem, 1)
                mk_ready.wait(pe, b, 1)
                nc.tensor.transpose(bk[0][0:H1, 64:64 + P], mkt[:], ident[:]).then_inc(mkT_ps.sem, 1)
                dm_ready.wait(pe, b, 1)
                nc.tensor.matmul(bk[0][:, 256:256 + H1], ones[0:H1, :], dm[:], start=True, stop=True)\
                    .then_inc(negm_ps.sem, 1)
                v_sb.wait(pe, b, 1)
                for g in range(H1 // 2):
                    for t in range(NT):
                        if g == 0:
                            e_ready.wait(pe, b, t + 1)
                        last = nc.tensor.matmul(bk[0][:, 288 + 18 * g:306 + 18 * g], lg[:, t, g * P:(g + 1) * P],
                                                vext[:, t, 2 * g:2 * g + 2, :], start=(t == 0), stop=(t == NT - 1))
                last.then_inc(n_ps.sem, 1)
                d_ready.wait(pe, b, 1)
                nc.tensor.matmul(bk[0][:, 440:448], onesblk[:], dcol[:], start=True, stop=True)\
                    .then_inc(dsum_ps.sem, 1)
                lg_used.wait(pe, b, 2 * NT)
                nxt_ready.wait(pe, b, 1)

                def logits(u):
                    t, c = divmod(u, 2)
                    if u >= 2:
                        phi_ready.wait(pe, b, u - 1)
                    nc.tensor.matmul(bk[4 + u % 2][:], qT[:, t * P:(t + 1) * P], w0bd[:, c * HALF:(c + 1) * HALF],
                                     start=True, stop=True).then_inc(lq_ps.sem, 1)

                logits(0)
                for u in range(2 * NT):
                    t, c = divmod(u, 2)
                    if u + 1 < 2 * NT:
                        logits(u + 1)
                    nm_ready.wait(pe, b, u + 1)
                    dst = bk[4 + u % 2][:].rearrange("p (h f) -> p h f", f=NF)
                    nc.tensor.matmul(dst, identr[:], bcast(nm1[:, 0], NF), start=False, stop=True,
                                     skip_group_check=True)
                    nc.tensor.matmul(dst, identr[:], bcast(nm1[:, 1], NF), start=False, stop=True,
                                     skip_group_check=True).then_inc(lq_shift.sem, 1)
                    phi_ready.wait(pe, b, u + 1)
                    if u >= 1:
                        phiT_sb.wait(pe, b, u)
                    transposes(bk[6], lambda i: phi[:, u % 2, i * P:(i + 1) * P], phiT_ps)
                    phiT_sb.wait(pe, b, u + 1)
                    if c == 0 and t >= 1:
                        cx_ready.wait(pe, b, t)
                    for i in range(4):
                        last = nc.tensor.matmul(bk[(7, 0)[c]][:, 18 * i:18 * i + 18],
                                                phiT[:, u % 2, i * P:(i + 1) * P], nxt[:, 4 * c + i],
                                                start=True, stop=True)
                    last.then_inc(num_ps.sem, 1)
                    if c == 0 and t >= 1:
                        nc.tensor.transpose(bk[3][:, (t - 1) * P:t * P], cx[:, (t - 1) % 2], ident[:])
                cx_ready.wait(pe, b, NT)
                nc.tensor.transpose(bk[3][:, (NT - 1) * P:NT * P], cx[:, (NT - 1) % 2], ident[:])\
                    .then_inc(cxT_ps.sem, 1)
                cxT_sb.wait(pe, b, 1)
                nc.tensor.matmul(bk[0][:], wo[:], cxT[:], start=True, stop=True).then_inc(wo_ps.sem, 1)
                y_sb.wait(pe, b, 1)
                transposes(bk[1], lambda t: yT[:, t * P:(t + 1) * P], yt_ps)
                hn_ready.wait(pe, b, 2)
                transposes(bk[2], lambda t: hn[:, t], hT_ps)
                hT_sb.wait(pe, b, 2)
                transposes(bk[3], lambda t: hT[:, t * P:(t + 1) * P], xb_ps)
                xr_ready.wait(pe, b, 1)


def layers_block(nc, a, xr, consts):
    ident, identr = consts["ident"], consts["identr"]
    with ExitStack() as ctx:
        def sb(name, shape, dt=F32):
            return ctx.enter_context(nc.sbuf_tensor(name, shape, dt))

        def sem(name):
            return ctx.enter_context(nc.semaphore(name))

        S = {}

        def sig(name, per, base=0):
            S[name] = Signal(sem(name), per, base)
            return S[name]

        wraw = sb("wraw", [P, 3, HALF])
        whi, wlo = sb("whi", [P, 3 * INNER], F32R), sb("wlo", [P, 3 * INNER], F32R)
        wo = sb("wo2", [P, HP, D])
        w1 = sb("w1", [P, 2 * FF])
        w2 = sb("w2", [P, 3, D])
        b1c = sb("b1c", [P, 2, 3])
        b2r = sb("b2r", [P, D])
        lnc = sb("lnc", [P, 2])
        scr = sb("scr", [P, 4, DH])
        rot = sb("rot", [P, 4, NT, DH])
        tab = sb("tab", [P, 4, NT, DH])
        mask32 = sb("mask32", [P, 2, 2 * WIN])
        mask = sb("mask", [P, 2, 2 * WIN], BF16)
        identb = sb("identb", [P, P], BF16)
        xw = sb("xw", [P, NT, D])
        xs = sb("xs", [P, L + 1])
        xh, xl = sb("xh", [P, L], F32R), sb("xl", [P, L], F32R)
        raw = sb("raw", [P, 2, 2, INNER])
        sq = sb("sq", [P, 2, INNER])
        ss = sb("ss", [P, 2 * H])
        rs, rh, rt = (sb(n, [P, 2 * H]) for n in ("rs2", "rh2", "rt2"))
        t1 = sb("t1", [P, 2, INNER])
        t2 = sb("t2", [P, 2, INNER])
        vb = sb("vb", [P, 2, 2 * HALF])
        kT = sb("kT2", [P, HP, WIN + L])
        qT = sb("qT2", [P, 2, HP, P])
        vp = sb("vp", [P, NW, HALF])
        mx = sb("mx", [P, 8])
        nm = sb("nm", [P, 2, 8], F32R)
        pr = sb("pr", [P, 2, HALF])
        den = sb("den", [P, 2, 8])
        pT = sb("pT", [P, 2, HALF])
        ob = sb("ob", [P, 2, HALF])
        oT = sb("oT", [P, 2, HP, P])
        x1w = sb("x1w", [P, NT, D])
        xs2 = sb("xs2", [P, L + 1])
        stats = sb("stats2", [P, NT, 6])
        mv = sb("mv2", [P, NT, 2])
        fs, fh, ft, fx = (sb(n, [P, NT]) for n in ("fs", "fh", "ft", "fx"))
        xn = sb("xn", [P, NT, D])
        xnT = sb("xnT", [P, L])
        ge = pr
        uT = sb("uT", [P, 3, L])
        y2 = xn

        pA = [ctx.enter_context(nc.psum_tensor(f"pA{i}", [P, 512], F32)) for i in range(2)]
        pT_ = [ctx.enter_context(nc.psum_tensor(f"pT{i}", [P, 512], F32)) for i in range(2)]
        pS = [ctx.enter_context(nc.psum_tensor(f"pS{i}", [P, 512], F32)) for i in range(2)]
        pO = ctx.enter_context(nc.psum_tensor("pO", [P, 512], F32))
        pY = ctx.enter_context(nc.psum_tensor("pY", [P, 512], F32))

        ld_const, ld_s, ld_wo, ld_f = (sem(n) for n in ("ld_const", "ld_s", "ld_wo", "ld_f"))
        ld_w = [sem(f"ld_w{i}") for i in range(3)]
        consts_up = sem("consts_up")
        tally = sem("tally2")
        w_hi = sig("w_hi", 6)
        w_lo = sig("w_lo", 6, 3)
        tab_ready = sig("tab_ready", 4)
        w_free = sig("w_free", 1, 1)
        tab_free = sig("tab_free", 1, 1)
        wo_free = sig("wo_free", 1, 1)
        ffn_free = sig("ffn_free", 1, 1)
        xw_ready = sig("xw_ready", 1)
        NTP = 1 + 16 + 8 + 8 + 1 + 3 + 1
        tp_used = sig("tp_used", NTP, 2)
        xT_ps = sig("xT_ps", 1)
        xs_ready = sig("xs_ready", 1)
        xhl_ready = sig("xhl_ready", 2)
        a_ready = sig("a_ready", 6 * NT)
        a_used = sig("a_used", 6 * NT, 2)
        sq_ready = sig("sq_ready", 2 * NT)
        sq_read = sig("sq_read", 2 * NT, 2)
        v_ready = sig("v_ready", NT)
        v_moved = [sem(f"v_moved{t}") for t in range(NT)]
        qn_ready = sig("qn_ready", 2 * NT)
        t2_ready = sig("t2_ready", 2 * NT)
        t1_ready = sig("t1_ready", 2 * NT)
        rope_ready = sig("rope_ready", 2 * NT)
        r_ps = sig("r_ps", 4 * NT)
        qk_placed = sig("qk_placed", NT)
        s_ps = sig("s_ps", UNITS, 8)
        nm_ready = sig("nm_ready", UNITS)
        s_shift = sig("s_shift", UNITS)
        p_ready = sig("p_ready", UNITS, 2)
        den_ready = sig("den_ready", UNITS, 2)
        pt_ps = sig("pt_ps", UNITS, 2)
        pt_sb = sig("pt_sb", UNITS)
        o_ps = sig("o_ps", UNITS, 8)
        o_half = sig("o_half", UNITS)
        oa_ps = sig("oa_ps", 3)
        o_used = sig("o_used", UNITS + 3, 1)
        ob_ready = sig("ob_ready", UNITS)
        ot_ps = sig("ot_ps", UNITS, 2)
        ot_sb = sig("ot_sb", UNITS)
        wo_t = sig("wo_t", NT, 2)
        wo_ps = sig("wo_ps", 1)
        x1_ready = sig("x1w_ready", 1)
        x1T_ps = sig("x1T_ps", 1)
        xs2_ready = sig("xs2_ready", 1)
        xb_ps = sig("xb_ps2", 1)
        xn_ready = sig("xn_ready", 1)
        xnT_ps = sig("xnT_ps", 1)
        xnT_ready = sig("xnT_ready", 1)
        g_ps = sig("g_ps", 3)
        ge_ready = sig("ge_ready", 3)
        u_ready = sig("u_ready", 3)
        y_ps = sig("y_ps", 1)
        x_done = sig("x_done", 1)
        norm_ch = Chain(sem("norm_chain"), NT * (1 + RSQRT_STEPS))
        sm_ch = Chain(sem("softmax_chain"), 3 * UNITS)
        ffn_ch = Chain(sem("ffn_chain"), 2 * NT + 1 + RSQRT_STEPS + 1)
        ROPE0, PT0, OT0 = {}, {}, {}
        ORDER = [("proj", 0), ("proj", 1), ("rope", 0)]
        for u in range(UNITS + 2):
            t = u // 2
            if u < UNITS and u % 2 == 0 and t >= 1:
                ORDER.append(("rope", t))
            if u < UNITS:
                ORDER.append(("scores", u))
            if u >= 1 and u - 1 < UNITS:
                ORDER.append(("probs", u - 1))
            if u >= 2:
                ORDER.append(("out", u - 2))
            if u < UNITS and u % 2 == 0 and t + 2 < NT:
                ORDER.append(("proj", t + 2))
        at = 1
        for kind, i in ORDER:
            if kind == "rope":
                ROPE0[i], at = at, at + 4
            elif kind == "probs":
                PT0[i], at = at, at + 1
            elif kind == "out":
                OT0[i], at = at, at + 1
        X2_0, XN_0, G_0 = at, at + 1, at + 2
        assert G_0 + 3 == NTP


        block = ctx.enter_context(nc.Block())

        @block.sync
        def _(sp):
            for t, src in ((rot, a["rot"]), (mask32, a["mask"])):
                sp.dma_start(t[:], src).then_inc(ld_const, 16)
            with sp.Fori(0, DEPTH) as l:
                for c in range(6):
                    w_lo.wait(sp, l, c - 2, alone=tally)
                    sp.dma_start(wraw[:, c % 3], a["Wqkv"][l, :, c * HALF:(c + 1) * HALF])\
                        .then_inc(ld_w[c % 3], 16)
                tab_free.wait(sp, l, 0, alone=tally)
                for i, name in enumerate(("q_scale", "k_scale")):
                    sp.dma_start(scr[:, 2 * i, :], a[name][l, :].partition_broadcast(P)).then_inc(ld_s, 16)
                    for s in range(2):
                        sp.dma_start(scr[:, 2 * i + 1, s * 32:s * 32 + 32],
                                     a[name][l, (1 - s) * 32:(1 - s) * 32 + 32].partition_broadcast(P))\
                            .then_inc(ld_s, 16)
                wo_free.wait(sp, l, 0, alone=tally)
                for c in range(2):
                    for s in range(2):
                        sp.dma_start(wo[64 * c:64 * c + 64, 4 * s:4 * s + 4, :],
                                     a["Wo"][l].rearrange("(m c s d) n -> d c s m n", c=2, s=2, d=DH)[:, c, s])\
                            .then_inc(ld_wo, 16)
                ffn_free.wait(sp, l, 0, alone=tally)
                sp.dma_start(w1[:], a["W1"][l]).then_inc(ld_f, 16)
                for k, (f0, fn) in enumerate(FT):
                    sp.dma_start(w2[0:fn, k, :], a["W2"][l, f0:f0 + fn, :]).then_inc(ld_f, 16)
                    for s in range(2):
                        sp.dma_start(b1c[0:fn, s, k:k + 1],
                                     a["b1"][l, s * FF + f0:s * FF + f0 + fn].unsqueeze(1)).then_inc(ld_f, 16)
                sp.dma_start(b2r[:], a["b2"][l, :].partition_broadcast(P)).then_inc(ld_f, 16)
                sp.dma_start(lnc[:, 0:1], a["ln_g"][l, :].unsqueeze(1)).then_inc(ld_f, 16)
                sp.dma_start(lnc[:, 1:2], a["ln_b"][l, :].unsqueeze(1)).then_inc(ld_f, 16)
                with sp.Fori(0, B) as b:
                    n = sp.snap(l * B + b)
                    for t in range(NT):
                        v_ready.wait(sp, n, t + 1, alone=tally)
                        o_ps.wait(sp, n, min(UNITS, 2 * t + 4) - UNITS, alone=tally)
                        for j in range(WPT):
                            for s in range(2):
                                src = vb[WIN * j:WIN * j + WIN, t % 2, s * HALF:(s + 1) * HALF]
                                w = WPT * t + j
                                sp.dma_start(vp[64 * s + WIN:64 * s + 2 * WIN, w], src).then_inc(v_moved[t], 16)
                                if w + 1 < NW:
                                    sp.dma_start(vp[64 * s:64 * s + WIN, w + 1], src).then_inc(v_moved[t], 16)

        NLD_F = 1 + 3 * 3 + 3
        V_SENT = [16 * (4 * WPT - (2 if t == NT - 1 else 0)) for t in range(NT)]

        @block.gpsimd
        def _(pool):
            with pool.Fori(0, DEPTH) as l:
                pool.wait_ge(ld_const, 32)
                pool.wait_ge(ld_s, l * 96 + 96)
                tab_free.wait(pool, l, 0)
                for i in range(4):
                    nc.gpsimd.tensor_tensor(tab[:, i], rot[:, i], over_heads(scr[:, i], NT), ALU.mult)\
                        .then_inc(tab_ready.sem, 1)
                tab_ready.wait(pool, l, 4, alone=tally)
                with pool.Fori(0, B) as b:
                    n = pool.snap(l * B + b)
                    for t in range(NT):
                        for i in range(2):
                            qn_ready.wait(pool, n, 2 * t + i + 1)
                            src = raw[:, t % 2, i]
                            for hh in range(2):
                                part = slice(hh * HALF, (hh + 1) * HALF)
                                ins = nc.gpsimd.tensor_tensor(
                                    t2[:, i, part].rearrange("p (h s d) -> p h s d", s=2, d=32),
                                    halves_swapped(src[:, part], None, 8),
                                    tab[:, 2 * i + 1, t].rearrange("p (s d) -> p s d", s=2).unsqueeze(1)
                                    .broadcast_to([P, 8, 2, 32]), ALU.mult)
                            ins.then_inc(t2_ready.sem, 1)
                            t2_ready.wait(pool, n, 2 * t + i + 1)
                            t1_ready.wait(pool, n, 2 * t + i + 1)
                            nc.gpsimd.tensor_tensor(t1[:, i], t1[:, i], t2[:, i], ALU.add)\
                                .then_inc(rope_ready.sem, 1)

        @block.scalar
        def _(act):
            act.wait_ge(consts_up, 1)
            with act.Fori(0, DEPTH) as l:
                for c in range(6):
                    act.wait_ge(ld_w[c % 3], l * 32 + 16 * (1 + c // 3))
                    if c == 0:
                        w_free.wait(act, l, 0)
                    nc.scalar.activation(whi[:, c * HALF:(c + 1) * HALF], wraw[:, c % 3], ACT.Copy)\
                        .then_inc(w_hi.sem, 1)
                with act.Fori(0, B) as b:
                    n = act.snap(l * B + b)

                    def shifted(dst, src, ready, i):
                        nc.scalar.activation(dst[0:64, 0:L], src[0:64, :], ACT.Copy)
                        nc.scalar.activation(dst[64:P, 1:L + 1], src[64:P, :], ACT.Copy).then_inc(tp_used.sem, 1)
                        tp_used.wait(act, n, i + 1)
                        act.sem_inc(ready.sem, 1)

                    xT_ps.wait(act, n, 1)
                    shifted(xs, pT_[0], xs_ready, 0)

                    def evac_proj(t):
                        for c in range(6):
                            a_ready.wait(act, n, 6 * t + c + 1)
                            src = pA[c % 2][:]
                            if c < 4:
                                i, hh = divmod(c, 2)
                                part = slice(hh * HALF, (hh + 1) * HALF)
                                if hh == 0:
                                    sq_read.wait(act, n, 2 * t + i - 1)
                                    if t >= 2:
                                        rope_ready.wait(act, n, 2 * (t - 2) + i + 1)
                                nc.scalar.activation(raw[:, t % 2, i, part], src, ACT.Copy)
                                ins = nc.scalar.activation(sq[:, i, part], src, ACT.Square)
                                ins.then_inc(a_used.sem, 1)
                                if hh == 1:
                                    a_used.wait(act, n, 6 * t + c + 1)
                                    act.sem_inc(sq_ready.sem, 1)
                            else:
                                if c == 4 and t >= 2:
                                    act.wait_ge(v_moved[t - 2], n * V_SENT[t - 2] + V_SENT[t - 2])
                                nc.scalar.activation(vb[:, t % 2, (c - 4) * HALF:(c - 3) * HALF], src, ACT.Copy)\
                                    .then_inc(a_used.sem, 1)
                        a_used.wait(act, n, 6 * t + 6)
                        act.sem_inc(v_ready.sem, 1)

                    def evac_rope(t):
                        for g in range(4):
                            i, hh = divmod(g, 2)
                            r_ps.wait(act, n, 4 * t + g + 1)
                            src = pT_[(ROPE0[t] + g) % 2][:].rearrange("p (k c) -> p k c", c=P)
                            if i == 0:
                                s_ps.wait(act, n, 2 * t + 2 - 4)
                                dst = qT[:, t % 2, 4 * hh:4 * hh + 4, :]
                            else:
                                s_ps.wait(act, n, min(UNITS, 2 * t + 4) - UNITS)
                                dst = kT[:, 4 * hh:4 * hh + 4, WIN + t * P:WIN + (t + 1) * P]
                            nc.scalar.activation(dst, src, ACT.Copy).then_inc(tp_used.sem, 1)
                        tp_used.wait(act, n, ROPE0[t] + 4)
                        act.sem_inc(qk_placed.sem, 1)

                    def exps(u):
                        s_shift.wait(act, n, u + 1)
                        pt_ps.wait(act, n, u - 1)
                        den_ready.wait(act, n, u - 1)
                        nc.scalar.activation(pr[:, u % 2], pS[u % 2][:], ACT.Exp).then_inc(p_ready.sem, 1)

                    def evac_p(u):
                        pt_ps.wait(act, n, u + 1)
                        o_ps.wait(act, n, u - 1)
                        nc.scalar.activation(pT[:, u % 2], pT_[PT0[u] % 2][:], ACT.Copy).then_inc(tp_used.sem, 1)
                        tp_used.wait(act, n, PT0[u] + 1)
                        act.sem_inc(pt_sb.sem, 1)

                    def evac_o(u):
                        t, hh = divmod(u, 2)
                        ot_ps.wait(act, n, u + 1)
                        if hh == 0:
                            wo_t.wait(act, n, t - 1)
                        nc.scalar.activation(oT[:, t % 2, 4 * hh:4 * hh + 4, :],
                                             pT_[OT0[u] % 2][:].rearrange("p (k c) -> p k c", c=P), ACT.Copy)\
                            .then_inc(tp_used.sem, 1)
                        tp_used.wait(act, n, OT0[u] + 1)
                        act.sem_inc(ot_sb.sem, 1)

                    for kind, i in ORDER:
                        if kind == "proj":
                            evac_proj(i)
                        elif kind == "rope":
                            evac_rope(i)
                        elif kind == "scores":
                            exps(i)
                        elif kind == "probs":
                            evac_p(i)
                        elif kind == "out":
                            evac_o(i)
                    x1T_ps.wait(act, n, 1)
                    shifted(xs2, pT_[X2_0 % 2], xs2_ready, X2_0)
                    xnT_ps.wait(act, n, 1)
                    act.wait_ge(ld_f, l * (16 * NLD_F) + 16 * NLD_F)
                    nc.scalar.activation(xnT[:], pT_[XN_0 % 2][:], ACT.Identity, bias=lnc[:, 1:2], scale=lnc[:, 0:1])\
                        .then_inc(tp_used.sem, 1)
                    tp_used.wait(act, n, XN_0 + 1)
                    act.sem_inc(xnT_ready.sem, 1)
                    for k, (f0, fn) in enumerate(FT):
                        g_ps.wait(act, n, k + 1)
                        if k >= 2:
                            u_ready.wait(act, n, k - 1)
                        nc.scalar.activation(ge[0:fn, k % 2], pT_[(G_0 + k) % 2][0:fn, :], ACT.Gelu,
                                             bias=b1c[0:fn, 1, k:k + 1]).then_inc(tp_used.sem, 1)
                        tp_used.wait(act, n, G_0 + k + 1)
                        act.sem_inc(ge_ready.sem, 1)

        @block.vector
        def _(dve):
            dve.wait_ge(ld_const, 32)
            nc.vector.memset(xs[64:P, 0:1], 0.0)
            nc.vector.memset(xs2[64:P, 0:1], 0.0)
            nc.vector.memset(kT[:, :, 0:WIN], 0.0)
            nc.vector.memset(vp[0:WIN, 0, :], 0.0)
            nc.vector.memset(vp[64:64 + WIN, 0, :], 0.0)
            nc.vector.tensor_copy(mask[:], mask32[:])
            nc.vector.tensor_copy(identb[:], ident[:]).then_inc(consts_up, 1)
            nc.vector.sem_inc(sq_read.sem, 2)
            nc.vector.sem_inc(w_lo.sem, 3)
            nc.vector.sem_inc(den_ready.sem, 2)
            nc.vector.sem_inc(o_used.sem, 1)
            dve.wait_ge(consts_up, 1)
            with dve.Fori(0, DEPTH) as l:
                for c in range(6):
                    w_hi.wait(dve, l, c + 1)
                    part = slice(c * HALF, (c + 1) * HALF)
                    nc.vector.tensor_tensor(wlo[:, part], wraw[:, c % 3], whi[:, part].bitcast(F32), ALU.subtract)\
                        .then_inc(w_lo.sem, 1)
                with dve.Fori(0, B) as b:
                    n = dve.snap(l * B + b)
                    norm_ch.start(dve, n)
                    sm_ch.start(dve, n)
                    ffn_ch.start(dve, n)
                    nc.vector.tensor_copy(xw[:], xr[:, bass.ds(b * NT, NT), :]).then_inc(xw_ready.sem, 1)
                    xs_ready.wait(dve, n, 1)
                    nc.vector.tensor_copy(xh[:], xs[:, 0:L]).then_inc(xhl_ready.sem, 1)
                    xhl_ready.wait(dve, n, 1)
                    nc.vector.tensor_tensor(xl[:], xs[:, 0:L], xh[:].bitcast(F32), ALU.subtract)\
                        .then_inc(xhl_ready.sem, 1)

                    def normalize(t):
                        for i in range(2):
                            sq_ready.wait(dve, n, 2 * t + i + 1)
                            nc.vector.tensor_reduce(ss[:, i * H:(i + 1) * H],
                                                    sq[:, i].rearrange("p (h d) -> p h d", d=DH), AX.X, ALU.add)\
                                .then_inc(sq_read.sem, 1)
                        sq_read.wait(dve, n, 2 * t + 2)
                        norm_ch.step(nc.vector.tensor_scalar(ss[:], ss[:], NORM_FLOOR2, None, ALU.max))
                        rsqrt_steps(nc, norm_ch, rs[:], rh[:], rt[:], ss[:])
                        for i in range(2):
                            q = raw[:, t % 2, i].rearrange("p (h d) -> p h d", d=DH)
                            nc.vector.tensor_tensor(q, q, bcast(rs[:, i * H:(i + 1) * H], DH), ALU.mult)\
                                .then_inc(qn_ready.sem, 1)

                    def rotate(t):
                        tab_ready.wait(dve, l, 4)
                        for i in range(2):
                            q = raw[:, t % 2, i].rearrange("p (h d) -> p h d", d=DH)
                            qn_ready.wait(dve, n, 2 * t + i + 1)
                            if t >= 1:
                                r_ps.wait(dve, n, 4 * (t - 1) + 2 * i + 2)
                            nc.vector.tensor_tensor(t1[:, i].rearrange("p (h d) -> p h d", d=DH), q,
                                                    over_heads(tab[:, 2 * i, t], H), ALU.mult)\
                                .then_inc(t1_ready.sem, 1)

                    def row_max(u):
                        s_ps.wait(dve, n, u + 1)
                        if u >= 1:
                            nm_ready.wait(dve, n, u)
                        sm_ch.step(nc.vector.tensor_reduce(mx[:], pS[u % 2][:].rearrange("p (h c) -> p h c", c=64),
                                                           AX.X, ALU.max))
                        if u >= 1:
                            s_shift.wait(dve, n, u)
                        sm_ch.step(nc.vector.tensor_scalar(nm[:, 0], mx[:], -1.0, None, ALU.mult))
                        nc.vector.scalar_tensor_tensor(nm[:, 1], mx[:], -1.0, nm[:, 0].bitcast(F32), ALU.mult,
                                                       ALU.subtract).then_inc(nm_ready.sem, 1)

                    def row_sum(u):
                        p_ready.wait(dve, n, u + 1)
                        sm_ch.step(nc.vector.tensor_reduce(den[:, u % 2], pr[:, u % 2].rearrange("p (h c) -> p h c", c=64),
                                                           AX.X, ALU.add))
                        nc.vector.reciprocal(den[:, u % 2], den[:, u % 2]).then_inc(den_ready.sem, 1)

                    def normalized(u):
                        o_ps.wait(dve, n, u + 1)
                        den_ready.wait(dve, n, u + 1)
                        ot_ps.wait(dve, n, u - 1)
                        nc.vector.tensor_tensor(ob[:, u % 2].rearrange("p (h d) -> p h d", d=DH),
                                                pO[:].rearrange("p (h d) -> p h d", d=DH),
                                                bcast(den[:, u % 2], DH), ALU.mult).then_inc(o_used.sem, 1)
                        o_used.wait(dve, n, u + 1)
                        dve.sem_inc(ob_ready.sem, 1)

                    for kind, i in ORDER:
                        if kind == "proj":
                            normalize(i)
                            if i < 2:
                                rotate(i)
                        elif kind == "rope" and 2 <= i + 1 < NT:
                            rotate(i + 1)
                        elif kind == "scores":
                            row_max(i)
                        elif kind == "probs":
                            row_sum(i)
                        elif kind == "out":
                            normalized(i)
                    wo_ps.wait(dve, n, 1)
                    nc.vector.tensor_tensor(x1w[:], xw[:], pY[:].rearrange("p (t d) -> p t d", d=D), ALU.add)\
                        .then_inc(x1_ready.sem, 1)
                    xb_ps.wait(dve, n, 1, alone=tally)
                    for t in range(NT):
                        ffn_ch.step(nc.vector.bn_stats(stats[:, t], pY[:, t * D:(t + 1) * D]), alone=tally)
                    for t in range(NT):
                        ffn_ch.step(nc.vector.bn_aggr(mv[:, t], stats[:, t]), alone=tally)
                    ffn_ch.step(nc.vector.tensor_scalar(fx[:], mv[:, :, 1], LN_EPS, None, ALU.add))
                    rsqrt_steps(nc, ffn_ch, fs[:], fh[:], ft[:], fx[:])
                    for t in range(NT):
                        ins = nc.vector.tensor_scalar(xn[:, t], pY[:, t * D:(t + 1) * D], mv[:, t, 0:1],
                                                      fs[:, t:t + 1], ALU.subtract, ALU.mult)
                    ins.then_inc(xn_ready.sem, 1)
                    for k, (f0, fn) in enumerate(FT):
                        oa_ps.wait(dve, n, k + 1)
                        ge_ready.wait(dve, n, k + 1)
                        nc.vector.scalar_tensor_tensor(uT[0:fn, k], pO[0:fn, :], b1c[0:fn, 0, k:k + 1],
                                                       ge[0:fn, k % 2], ALU.add, ALU.mult).then_inc(o_used.sem, 1)
                        o_used.wait(dve, n, UNITS + k + 1)
                        dve.sem_inc(u_ready.sem, 1)
                    y_ps.wait(dve, n, 1)
                    ffn_ch.step(nc.vector.tensor_tensor(y2[:], pY[:].rearrange("p (t d) -> p t d", d=D),
                                                        b2r[:].unsqueeze(1).broadcast_to([P, NT, D]), ALU.add))
                    nc.vector.tensor_tensor(xr[:, bass.ds(b * NT, NT), :], y2[:], x1w[:], ALU.add)\
                        .then_inc(x_done.sem, 1)
                    x_done.wait(dve, n, 1, alone=tally)
                    norm_ch.end()
                    sm_ch.end()
                    ffn_ch.end()
                nc.vector.sem_inc(ffn_free.sem, 1)

        @block.tensor
        def _(pe):
            pe.wait_ge(consts_up, 1)
            nc.tensor.sem_inc(w_free.sem, 1)
            nc.tensor.sem_inc(tab_free.sem, 1)
            nc.tensor.sem_inc(wo_free.sem, 1)
            nc.tensor.sem_inc(ffn_free.sem, 1)
            for s, k in ((s_ps, 8), (o_ps, 8), (pt_ps, 2), (ot_ps, 2), (wo_t, 2), (tp_used, 2), (a_used, 2), (p_ready, 2)):
                nc.tensor.sem_inc(s.sem, k)
            with pe.Fori(0, DEPTH) as l:
                with pe.Fori(0, B) as b:
                    n = pe.snap(l * B + b)

                    def transposes(dst, src):
                        for t in range(4):
                            last = nc.tensor.transpose(dst[:, t * P:(t + 1) * P], src(t), ident[:])
                        return last

                    xw_ready.wait(pe, n, 1)
                    tp_used.wait(pe, n, 0 - 1)
                    transposes(pT_[0], lambda t: xw[:, t]).then_inc(xT_ps.sem, 1)
                    xhl_ready.wait(pe, n, 2)

                    def project(t):
                        xt = slice(t * P, (t + 1) * P)
                        for c in range(6):
                            if t == 0:
                                w_lo.wait(pe, l, c + 1)
                            a_used.wait(pe, n, 6 * t + c - 1)
                            for j, (x, w) in enumerate(((xh, whi), (xl, whi), (xh, wlo))):
                                if c < 4:
                                    rhs = w[:, c * HALF:(c + 1) * HALF]
                                else:
                                    rhs = w[:, 2 * INNER:].rearrange("p (m c d) -> p m c d", c=2, d=2 * DH)[:, :, c - 4, :]
                                last = nc.tensor.matmul(pA[c % 2][:], x[:, xt], rhs, start=(j == 0), stop=(j == 2))
                            last.then_inc(a_ready.sem, 1)

                    def rope(t):
                        for g in range(4):
                            i, hh = divmod(g, 2)
                            if hh == 0:
                                rope_ready.wait(pe, n, 2 * t + i + 1)
                            tp_used.wait(pe, n, ROPE0[t] + g - 1)
                            transposes(pT_[(ROPE0[t] + g) % 2],
                                       lambda j: t1[:, i, (4 * hh + j) * P:(4 * hh + j + 1) * P]).then_inc(r_ps.sem, 1)

                    def scores(u):
                        t, s = divmod(u, 2)
                        bank = pS[u % 2]
                        qk_placed.wait(pe, n, t + 1)
                        p_ready.wait(pe, n, u - 1)
                        nc.tensor.matmul(bank[:].rearrange("p (h c) -> p h c", c=64), identb[:],
                                         over_heads(mask[:, min(t, 1)], 8), start=True, stop=True)
                        part = slice(64 * s, 64 * s + 64)
                        for g in range(HP):
                            for j in range(WPT):
                                k0 = t * P + j * WIN
                                last = nc.tensor.matmul(bank[WIN * j:WIN * (j + 1), 64 * g:64 * (g + 1)],
                                                        qT[part, t % 2, g, WIN * j:WIN * (j + 1)],
                                                        kT[part, g, k0:k0 + 2 * WIN], start=False, stop=True,
                                                        skip_group_check=True)
                        last.then_inc(s_ps.sem, 1)

                    def shift(u):
                        dst = pS[u % 2][:].rearrange("p (h c) -> p h c", c=64)
                        nm_ready.wait(pe, n, u + 1)
                        for i in range(2):
                            last = nc.tensor.matmul(dst, identr[:], bcast(nm[:, i], 64), start=False, stop=True,
                                                    skip_group_check=True)
                        last.then_inc(s_shift.sem, 1)

                    def probs(u):
                        p_ready.wait(pe, n, u + 1)
                        tp_used.wait(pe, n, PT0[u] - 1)
                        transposes(pT_[PT0[u] % 2], lambda j: pr[:, u % 2, j * P:(j + 1) * P]).then_inc(pt_ps.sem, 1)

                    def values(u):
                        t, s = divmod(u, 2)
                        pt_sb.wait(pe, n, u + 1)
                        if s == 0:
                            pe.wait_ge(v_moved[t], n * V_SENT[t] + V_SENT[t])
                        o_used.wait(pe, n, u, alone=tally)
                        for c in range(2):
                            part = slice(64 * c, 64 * c + 64)
                            for m in range(4):
                                g, v = 2 * m + c, 2 * m + s
                                for j in range(WPT):
                                    last = nc.tensor.matmul(pO[WIN * j:WIN * (j + 1), 64 * g:64 * (g + 1)],
                                                            pT[part, u % 2, m * P + WIN * j:m * P + WIN * (j + 1)],
                                                            vp[part, WPT * t + j, 64 * v:64 * (v + 1)],
                                                            start=True, stop=True)
                            if c == 0:
                                last.then_inc(o_half.sem, 1)
                                o_half.wait(pe, n, u + 1, alone=tally)
                        last.then_inc(o_ps.sem, 1)

                    def out(u):
                        t, hh = divmod(u, 2)
                        ob_ready.wait(pe, n, u + 1)
                        tp_used.wait(pe, n, OT0[u] - 1)
                        transposes(pT_[OT0[u] % 2], lambda j: ob[:, u % 2, j * P:(j + 1) * P]).then_inc(ot_ps.sem, 1)

                    def project_out(t):
                        ot_sb.wait(pe, n, 2 * t + 2)
                        if t == 0:
                            pe.wait_ge(ld_wo, l * 64 + 64)
                        for g in range(HP):
                            last = nc.tensor.matmul(pY[:, t * D:(t + 1) * D], oT[:, t % 2, g, :], wo[:, g, :],
                                                    start=(g == 0), stop=(g == HP - 1))
                        last.then_inc(wo_t.sem, 1)
                        return last

                    for kind, i in ORDER:
                        if kind == "proj":
                            project(i)
                        elif kind == "rope":
                            rope(i)
                        elif kind == "scores":
                            scores(i)
                            if i >= 2:
                                values(i - 2)
                            shift(i)
                        elif kind == "probs":
                            if i + 1 >= UNITS:
                                values(i - 1)
                            probs(i)
                        elif kind == "out":
                            if i == UNITS - 1:
                                values(i)
                            if i >= 2 and i % 2 == 0:
                                project_out(i // 2 - 1)
                            out(i)
                    project_out(NT - 1)
                    wo_t.wait(pe, n, NT)
                    pe.sem_inc(wo_ps.sem, 1)
                    x1_ready.wait(pe, n, 1)
                    tp_used.wait(pe, n, X2_0 - 1)
                    transposes(pT_[X2_0 % 2], lambda t: x1w[:, t]).then_inc(x1T_ps.sem, 1)
                    xs2_ready.wait(pe, n, 1)
                    transposes(pY, lambda t: xs2[:, t * P:(t + 1) * P]).then_inc(xb_ps.sem, 1)
                    xn_ready.wait(pe, n, 1)
                    tp_used.wait(pe, n, XN_0 - 1)
                    transposes(pT_[XN_0 % 2], lambda t: xn[:, t]).then_inc(xnT_ps.sem, 1)
                    pe.wait_ge(ld_f, l * (16 * NLD_F) + 16 * NLD_F)
                    xnT_ready.wait(pe, n, 1)
                    for k, (f0, fn) in enumerate(FT):
                        tp_used.wait(pe, n, G_0 + k - 1)
                        nc.tensor.matmul(pT_[(G_0 + k) % 2][0:fn, :], w1[:, FF + f0:FF + f0 + fn], xnT[:],
                                         start=True, stop=True).then_inc(g_ps.sem, 1)
                        o_used.wait(pe, n, UNITS + k)
                        nc.tensor.matmul(pO[0:fn, :], w1[:, f0:f0 + fn], xnT[:], start=True, stop=True)\
                            .then_inc(oa_ps.sem, 1)
                    u_ready.wait(pe, n, 3)
                    for t in range(NT):
                        for k, (f0, fn) in enumerate(FT):
                            last = nc.tensor.matmul(pY[:, t * D:(t + 1) * D], uT[0:fn, k, t * P:(t + 1) * P],
                                                    w2[0:fn, k, :], start=(k == 0), stop=(k == 2))
                    last.then_inc(y_ps.sem, 1)
                    x_done.wait(pe, n, 1)
                pe.sem_inc(w_free.sem, 1)
                pe.sem_inc(tab_free.sem, 1)
                pe.sem_inc(wo_free.sem, 1)


def final_block(nc, xr, x1_dram, out, mod, consts):
    ident = consts["ident"]
    with ExitStack() as ctx:
        def sem(name):
            return ctx.enter_context(nc.semaphore(name))

        x1 = ctx.enter_context(nc.sbuf_tensor("x1f", [P, B, NT, D], F32))
        xc = ctx.enter_context(nc.sbuf_tensor("xcf", [P, B, NT, D], F32))
        gT = ctx.enter_context(nc.sbuf_tensor("gTf", [P, B, L], F32))
        res = ctx.enter_context(nc.sbuf_tensor("resf", [P, B, NT, D], F32))
        ps = [ctx.enter_context(nc.psum_tensor(f"f{i}", [P, 512], F32)) for i in range(8)]
        loaded, turned, gated, back, done, stored = (sem(n) for n in ("x1_loaded", "turned", "gated", "turned_back",
                                                                      "out_ready", "out_stored"))
        block = ctx.enter_context(nc.Block())

        @block.sync
        def _(sp):
            for b in range(B):
                sp.dma_start(x1[:, b], x1_dram[b]).then_inc(loaded, 16)
            for b in range(B):
                sp.wait_ge(done, b + 1)
                sp.dma_start(out[b].rearrange("(t p) d -> p t d", p=P), res[:, b]).then_inc(stored, 16)
            sp.wait_ge(stored, 16 * B)

        @block.tensor
        def _(pe):
            for b in range(B):
                for t in range(NT):
                    last = nc.tensor.transpose(ps[b][:, t * P:(t + 1) * P], xr[:, b * NT + t, :], ident[:])
                last.then_inc(turned, 1)
            for b in range(B):
                pe.wait_ge(gated, b + 1)
                for t in range(NT):
                    last = nc.tensor.transpose(ps[4 + b][:, t * P:(t + 1) * P], gT[:, b, t * P:(t + 1) * P], ident[:])
                last.then_inc(back, 1)

        @block.scalar
        def _(act):
            for b in range(B):
                act.wait_ge(turned, b + 1)
                nc.scalar.activation(gT[:, b], ps[b][:], ACT.Copy, scale=mod[:, 5, b:b + 1]).then_inc(gated, 1)

        @block.vector
        def _(dve):
            dve.wait_ge(loaded, 16 * B)
            for b in range(B):
                dve.wait_ge(back, b + 1)
                nc.vector.tensor_tensor(res[:, b], ps[4 + b][:].rearrange("p (t d) -> p t d", d=D), x1[:, b], ALU.add)\
                    .then_inc(done, 1)


def build(nc, a, out):
    with ExitStack() as ctx:
        xr = ctx.enter_context(nc.sbuf_tensor("xr", [P, B * NT, D], F32))
        mod = ctx.enter_context(nc.sbuf_tensor("mod", [P, 6, B], F32))
        consts = {n: ctx.enter_context(nc.sbuf_tensor(n, [P, P], F32)) for n in ("ident", "onesblk", "ones")}
        consts["identr"] = ctx.enter_context(nc.sbuf_tensor("identr", [P, P], F32R))
        x1_dram = nc.dram_tensor("x1_scratch", (B, P, NT, D), F32).ap()
        attention1_block(nc, a, xr, x1_dram, mod, consts)
        layers_block(nc, a, xr, consts)
        final_block(nc, xr, x1_dram, out, mod, consts)


def constants():
    f = np.float32
    half = np.arange(0, DH, 2, dtype=f)
    inv_freq = (f(1.0) / np.power(f(10000.0), half / f(DH), dtype=f)).astype(f)
    pos = np.arange(L, dtype=f)
    ang = pos[:, None] * inv_freq[None, :]
    base = ((half + f(0.4 * DH)) / f(1.4 * DH)).astype(f)
    power = ((pos - L // 2) / (WIN // 2)).astype(f)
    scale = np.power(base[None, :], power[:, None], dtype=f)
    cos, sin = np.cos(ang).astype(f), np.sin(ang).astype(f)
    rot = np.empty((4, L, DH), f)
    for i, (s, m) in enumerate(((scale, QK_SCALE), (f(1.0) / scale, 1.0))):
        rot[2 * i] = np.concatenate([cos * s, cos * s], -1) * f(m)
        rot[2 * i + 1] = np.concatenate([-sin * s, sin * s], -1) * f(m)
    rot = np.ascontiguousarray(rot.reshape(4, NT, P, DH).transpose(2, 0, 1, 3))
    mask = np.zeros((P, 2, 2 * WIN), f)
    i = np.arange(P)[:, None] % WIN
    j = np.arange(2 * WIN)[None, :] - WIN
    mask[:, :] = np.where((i < j) | (i > j + WIN), f(MASKED), f(0))[:, None]
    mask[0:WIN, 0, 0:WIN] = MASKED
    onesblk = np.kron(np.eye(2, dtype=f), np.ones((64, 64), f))
    selneg = np.kron(np.eye(H1, dtype=f), np.full((DH1, 1), -0.5, f))
    return {"rot": rot, "mask": mask, "ident": np.eye(P, dtype=f), "onesblk": onesblk, "selneg": selneg}


def kernel(**inputs):
    import concourse.bacc as bacc
    from concourse.bass_utils import run_bass_kernel_spmd

    x = {k: np.ascontiguousarray(v) for k, v in inputs.items()}
    arrays = {"x": x["L0_attn_x"], "Wrf": x["L0_attn_Wrf"], "bv": x["L0_attn_bv"], "wmod": x["L0_wmod"],
              "cT": np.ascontiguousarray(x["L0_c"].T)}
    for w in ("Wq", "Wk", "Wv", "Wo"):
        arrays[w + "T"] = np.ascontiguousarray(x["L0_attn_" + w].T)
    arrays["bcol"] = np.ascontiguousarray(np.stack([x["L0_attn_" + n] for n in ("bq", "bk", "bo")], 1))
    for w in ("Wqkv", "q_scale", "k_scale", "Wo", "ln_g", "ln_b", "W1", "b1", "W2", "b2"):
        arrays[w] = x["L0_ffn_" + w]
    arrays.update(constants())
    nc = bacc.Bacc("TRN2", target_bir_lowering=False, num_devices=1)
    a = {k: nc.dram_tensor("in_" + k, v.shape, mybir.dt.from_np(v.dtype), kind="ExternalInput").ap()
         for k, v in arrays.items()}
    out = nc.dram_tensor("out", (B, L, D), F32, kind="ExternalOutput").ap()
    build(nc, a, out)
    r = run_bass_kernel_spmd(nc, [{"in_" + k: v for k, v in arrays.items()}], core_ids=[0])
    return r.results[0]["out"]
```

```python
from contextlib import ExitStack

import numpy as np

import concourse.bass as bass
from concourse import mybir

F32 = mybir.dt.float32
F32R = mybir.dt.float32r
BF16 = mybir.dt.bfloat16
I32 = mybir.dt.int32
ALU = mybir.AluOpType
ACT = mybir.ActivationFunctionType
AX = mybir.AxisListType

P = 128
B, L, D = 4, 512, 128
NT = L // P
H1, DH1, NF = 16, 8, 64
EPS1 = 1e-6
LN_EPS = 1e-5
DEPTH = 6
H, DH = 16, 64
HP = H // 2
INNER = H * DH
WIN = 32
WPT = P // WIN
NW = L // WIN
FF = int(D * 4 * 2 / 3)
FT = [(0, 128), (128, 128), (256, FF - 256)]
QK_SCALE = 8.0
MASKED = -1e30
HALF = 512
UNITS = 2 * NT
RSQRT_SEED = float(0x5F3759DF)
NORM_FLOOR2 = 1e-24


def wait_for(eng, sem, value, alone=None):
    eng.wait_ge(sem, value)
    if alone is not None:
        eng.sem_inc(alone, 1)


class Signal:

    def __init__(self, sem, per, base=0):
        self.sem, self.per, self.base = sem, per, base

    def wait(self, eng, turn, n, alone=None):
        value = turn * self.per + (n + self.base)
        if not isinstance(value, int) or value > 0:
            wait_for(eng, self.sem, value, alone)


class Chain:

    def __init__(self, sem, per):
        self.sem, self.per, self.n = sem, per, 0

    def start(self, eng, turn, done=0):
        self.eng, self.turn, self.n = eng, turn, done

    def count(self, ins):
        self.n += 1
        assert self.n <= self.per
        ins.then_inc(self.sem, 1)

    def wait(self, alone=None):
        wait_for(self.eng, self.sem, self.turn * self.per + self.n, alone)

    def step(self, ins, alone=None):
        self.count(ins)
        self.wait(alone)

    def end(self):
        assert self.n == self.per, (self.n, self.per)


RSQRT_STEPS = 12


def rsqrt_steps(nc, chain, y, half, tmp, x):
    chain.step(nc.vector.tensor_scalar(y.bitcast(I32), x.bitcast(I32), 1, None, ALU.logical_shift_right))
    chain.step(nc.vector.tensor_scalar(y.bitcast(I32), y.bitcast(I32), -1.0, RSQRT_SEED, ALU.mult, ALU.add))
    chain.step(nc.vector.tensor_scalar(half, x, -0.5, None, ALU.mult))
    for _ in range(3):
        chain.step(nc.vector.tensor_tensor(tmp, y, y, ALU.mult))
        chain.step(nc.vector.tensor_tensor(tmp, tmp, half, ALU.mult))
        chain.step(nc.vector.scalar_tensor_tensor(y, tmp, 1.5, y, ALU.add, ALU.mult))


def bcast(ap, n):
    return ap.unsqueeze(2).broadcast_to([ap.shape[0], ap.shape[1], n])


def over_heads(ap, n):
    return ap.unsqueeze(1).broadcast_to([ap.shape[0], n, ap.shape[1]])


def halves_swapped(t):
    a = t.rearrange("p (h s d) -> p h s d", s=2, d=DH // 2)
    return a[:, :, ::-1, :]


def attention1_block(nc, a, xr, x1_dram, mod, consts):
    ident, identr, onesblk, ones = (consts[n] for n in ("ident", "identr", "onesblk", "ones"))
    with ExitStack() as ctx:
        def sb(name, shape, dt=F32):
            return ctx.enter_context(nc.sbuf_tensor(name, shape, dt))

        def sem(name):
            return ctx.enter_context(nc.semaphore(name))

        x0 = sb("x0", [P, B * NT, D])
        wq, wk, wv, wo = (sb(n, [P, D]) for n in ("wq", "wk", "wv", "wo"))
        w0bd = sb("w0bd", [P, H1 * NF])
        selneg = sb("selneg", [P, H1])
        bcol = sb("bcol", [P, 3])
        bvrow = sb("bvrow", [P, D])
        cT = sb("cT", [P, B])
        cexp = sb("cexp", [P, B])
        wmod = sb("wmod", [P, 6 * D])
        gab = sb("gab", [P, B])
        sgn = sb("sgn", [P, B])
        stats = sb("stats", [P, NT, 6])
        mv = sb("mv", [P, NT, 2])
        rs, rh, rt, rx = (sb(n, [P, NT]) for n in ("rs", "rh", "rt", "rx"))
        hn = sb("hn", [P, NT, D])
        hT = sb("hT", [P, L])
        qT, kT, ksq = (sb(n, [P, L]) for n in ("qT1", "kT1", "ksq1"))
        vext = sb("vext", [P, NT, H1, DH1 + 1])
        ksum = sb("ksum", [P, NT * H1])
        lg = sb("lg", [P, NT, H1 * NF])
        mk = sb("mk", [P, NT, H1])
        mkt = sb("mkt", [P, H1])
        mh = sb("mh", [H1, 1])
        dm = sb("dm", [H1, H1])
        negm = sb("negm", [P, H1])
        nxt = sb("nxt", [P, H1 // 2, 2, DH1 + 1])
        dcol = sb("dcol", [P, H1 // 2])
        m1 = sb("m1", [P, 8])
        nm1 = sb("nm1", [P, 2, 8], F32R)
        phi = sb("phi", [P, 2, HALF])
        phiT = sb("phiT", [P, 2, HALF])
        rd = sb("rd", [P, 8])
        cx = sb("cx", [P, 2, D])
        cxT = sb("cxT", [P, L])
        yT = sb("yT", [P, L])
        x1s = sb("x1s", [P, NT, D])
        bk = [ctx.enter_context(nc.psum_tensor(f"a{i}", [P, 512], F32)) for i in range(8)]

        in_x, in_w, bd, out_x1, zeroed = (sem(n) for n in ("in_x", "in_w", "bd_loaded", "x1_stored", "zeroed"))
        s_silu, s_silu2, s_mod, s_gate = sem("silu_exp"), sem("silu_done"), sem("mod_ps"), sem("mod_sb")
        ch0 = Chain(sem("setup_chain"), 13)
        tally = sem("tally1")
        ch = Chain(sem("dve_chain1"), 91)
        S = {}

        def sig(name, per, base=0):
            S[name] = Signal(sem(name), per, base)
            return S[name]

        hn_ready = sig("hn_ready", 2)
        hT_ps = sig("hT_ps", 2)
        hT_sb = sig("hT_sb", 2)
        qkv_ps = sig("qkv_ps", 1)
        qk_sb = sig("qk_sb", 1)
        v_sb = sig("v_sb", 1)
        ks_ps = sig("ks_ps", 1)
        lg_ps = sig("lg_ps", 2 * NT)
        lg_used = sig("lg_used", 2 * NT, 2)
        mk_ready = sig("mk_ready", 1)
        mkT_ps = sig("mkT_ps", 1)
        dm_ready = sig("dm_ready", 1)
        negm_ps = sig("negm_ps", 1)
        lg_sub = sig("lg_sub", NT)
        e_ready = sig("e_ready", NT)
        n_ps = sig("n_ps", 1)
        d_ready = sig("d_ready", 1)
        dsum_ps = sig("dsum_ps", 1)
        nxt_ready = sig("nxt_ready", 1)
        lq_ps = sig("lq_ps", 2 * NT)
        nm_ready = sig("nm1_ready", 2 * NT)
        lq_shift = sig("lq_shift", 2 * NT)
        phi_ready = sig("phi_ready", 2 * NT)
        phiT_ps = sig("phiT_ps", 2 * NT)
        phiT_sb = sig("phiT_sb", 2 * NT)
        num_ps = sig("num_ps", 2 * NT)
        cx_ready = sig("cx_ready", NT)
        cxT_ps = sig("cxT_ps", 1)
        cxT_sb = sig("cxT_sb", 1)
        wo_ps = sig("wo_ps", 1)
        y_sb = sig("y_sb", 1)
        yt_ps = sig("yt_ps", 1)
        x1_ready = sig("x1_ready", 1)
        xb_ps = sig("xb_ps", 1)
        xr_ready = sig("xr_ready", 1)
        block = ctx.enter_context(nc.Block())

        @block.sync
        def _(sp):
            for t, src in ((x0[:], a["x"].rearrange("b (t p) d -> p (b t) d", p=P)),):
                sp.dma_start(t, src).then_inc(in_x, 16)
            loads = [(cT, a["cT"]), (wmod, a["wmod"]), (ident, a["ident"]), (bcol, a["bcol"]), (wq, a["WqT"]),
                     (wk, a["WkT"]), (wv, a["WvT"]), (wo, a["WoT"]), (selneg, a["selneg"]), (onesblk, a["onesblk"])]
            for t, src in loads:
                sp.dma_start(t[:], src).then_inc(in_w, 16)
            sp.dma_start(bvrow[:], a["bv"].partition_broadcast(P)).then_inc(in_w, 16)
            sp.wait_ge(zeroed, 1)
            for h in range(H1):
                sp.dma_start(w0bd[DH1 * h:DH1 * (h + 1), NF * h:NF * (h + 1)], a["Wrf"][0, h]).then_inc(bd, 16)
            with sp.Fori(0, B) as b:
                x1_ready.wait(sp, b, 1)
                sp.dma_start(x1_dram[b], x1s[:]).then_inc(out_x1, 16)
            sp.wait_ge(out_x1, 16 * B)

        NLOADS = 11

        @block.gpsimd
        def _(pool):
            nc.gpsimd.memset(w0bd[:], 0.0).then_inc(zeroed, 1)
            nc.gpsimd.memset(nxt[:], 0.0).then_inc(zeroed, 1)
            nc.gpsimd.memset(ones[:], 1.0).then_inc(zeroed, 1)
            nc.gpsimd.memset(vext[:], 1.0).then_inc(zeroed, 1)

        @block.scalar
        def _(act):
            act.wait_ge(in_w, 16 * NLOADS)
            nc.scalar.activation(cexp[:], cT[:], ACT.Exp, scale=-1.0).then_inc(s_silu, 1)
            act.wait_ge(s_gate, 1)
            with act.Fori(0, B) as b:
                hT_ps.wait(act, b, 1)
                nc.scalar.activation(hT[:], bk[0][:], ACT.Identity, bias=mod[:, 0, bass.ds(b, 1)],
                                     scale=mod[:, 1, bass.ds(b, 1)]).then_inc(hT_sb.sem, 1)
                qkv_ps.wait(act, b, 1)
                nc.scalar.activation(qT[:], bk[1][:], ACT.Identity, bias=bcol[:, 0:1])
                nc.scalar.activation(kT[:], bk[2][:], ACT.Identity, bias=bcol[:, 1:2])
                nc.scalar.activation(ksq[:], bk[2][:], ACT.Square, bias=bcol[:, 1:2]).then_inc(qk_sb.sem, 1)
                for t in range(NT):
                    lg_sub.wait(act, b, t + 1)
                    nc.scalar.activation(lg[:, t], lg[:, t], ACT.Exp).then_inc(e_ready.sem, 1)
                for u in range(2 * NT):
                    lq_shift.wait(act, b, u + 1)
                    if u >= 2:
                        phiT_ps.wait(act, b, u - 1)
                    nc.scalar.activation(phi[:, u % 2], bk[4 + u % 2][:], ACT.Exp).then_inc(phi_ready.sem, 1)
                    phiT_ps.wait(act, b, u + 1)
                    if u >= 2:
                        num_ps.wait(act, b, u - 1)
                    nc.scalar.activation(phiT[:, u % 2], bk[6][:], ACT.Copy).then_inc(phiT_sb.sem, 1)
                cxT_ps.wait(act, b, 1)
                nc.scalar.activation(cxT[:], bk[3][:], ACT.Copy).then_inc(cxT_sb.sem, 1)
                wo_ps.wait(act, b, 1)
                nc.scalar.activation(yT[:], bk[0][:], ACT.Identity, bias=gab[:, bass.ds(b, 1)],
                                     scale=mod[:, 2, bass.ds(b, 1)]).then_inc(y_sb.sem, 1)
                hT_ps.wait(act, b, 2)
                nc.scalar.activation(hT[:], bk[2][:], ACT.Identity, bias=mod[:, 3, bass.ds(b, 1)],
                                     scale=mod[:, 4, bass.ds(b, 1)]).then_inc(hT_sb.sem, 1)

        @block.vector
        def _(dve):
            ch0.start(dve, 0)
            dve.wait_ge(s_silu, 1)
            ch0.step(nc.vector.tensor_scalar(cexp[:], cexp[:], 1.0, None, ALU.add))
            ch0.step(nc.vector.reciprocal(cexp[:], cexp[:]))
            nc.vector.tensor_tensor(cT[:], cT[:], cexp[:], ALU.mult).then_inc(s_silu2, 1)
            nc.vector.tensor_copy(identr[:], ident[:]).then_inc(s_silu2, 1)
            dve.wait_ge(s_mod, 1)
            ch0.step(nc.vector.tensor_copy(mod[:], bk[0][:, 0:6 * B].rearrange("p (j b) -> p j b", b=B)))
            for j in (1, 4):
                ch0.step(nc.vector.tensor_scalar(mod[:, j], mod[:, j], 1.0, None, ALU.add))
            for j in (2, 5):
                ch0.step(nc.vector.tensor_scalar(sgn[:], mod[:, j], 0.0, 2.0, ALU.is_ge, ALU.mult))
                ch0.step(nc.vector.tensor_scalar(sgn[:], sgn[:], -1.0, None, ALU.add))
                ch0.step(nc.vector.scalar_tensor_tensor(mod[:, j], mod[:, j], -1.0, mod[:, j], ALU.mult, ALU.max))
                ch0.step(nc.vector.scalar_tensor_tensor(mod[:, j], mod[:, j], 0.25, sgn[:], ALU.max, ALU.mult))
            nc.vector.tensor_scalar(gab[:], mod[:, 2], bcol[:, 2:3], None, ALU.mult).then_inc(s_gate, 1)
            nc.vector.sem_inc(lg_used.sem, 2)
            dve.wait_ge(in_x, 16)
            dve.wait_ge(zeroed, 4)
            with dve.Fori(0, B) as b:
                ch.start(dve, b)

                def layernorm(src):
                    for t in range(NT):
                        ch.step(nc.vector.bn_stats(stats[:, t], src(t)), alone=tally)
                    for t in range(NT):
                        ch.step(nc.vector.bn_aggr(mv[:, t], stats[:, t]), alone=tally)
                    ch.step(nc.vector.tensor_scalar(rx[:], mv[:, :, 1], LN_EPS, None, ALU.add))
                    rsqrt_steps(nc, ch, rs[:], rh[:], rt[:], rx[:])
                    for t in range(NT):
                        ins = nc.vector.tensor_scalar(hn[:, t], src(t), mv[:, t, 0:1], rs[:, t:t + 1],
                                                      ALU.subtract, ALU.mult)
                        if t < NT - 1:
                            ch.step(ins)
                    ins.then_inc(hn_ready.sem, 1)

                layernorm(lambda t: x0[:, bass.ds(b * NT + t, 1), :].rearrange("p a d -> p (a d)"))
                qkv_ps.wait(dve, b, 1)
                nc.vector.tensor_tensor(vext[:, :, :, 0:DH1],
                                        bk[3][:].rearrange("p (t h d) -> p t h d", t=NT, h=H1),
                                        bvrow[:].rearrange("p (h d) -> p h d", h=H1).unsqueeze(1)
                                        .broadcast_to([P, NT, H1, DH1]), ALU.add).then_inc(v_sb.sem, 1)
                ks_ps.wait(dve, b, 1)
                ch.step(nc.vector.tensor_copy(ksum[:], bk[0][:, 0:NT * H1]))
                for u in range(2 * NT):
                    t, c = divmod(u, 2)
                    lg_ps.wait(dve, b, u + 1)
                    part = lg[:, t, c * HALF:(c + 1) * HALF].rearrange("p (h f) -> p h f", f=NF)
                    h0 = t * H1 + c * 8
                    nc.vector.tensor_tensor(part, bk[4 + u % 2][:].rearrange("p (h f) -> p h f", f=NF),
                                            bcast(ksum[:, h0:h0 + 8], NF), ALU.add).then_inc(lg_used.sem, 1)
                    lg_used.wait(dve, b, u + 1)
                    ch.step(nc.vector.tensor_reduce(mk[:, t, c * 8:c * 8 + 8], part, AX.X, ALU.max))
                nc.vector.tensor_reduce(mkt[:], mk[:].rearrange("p t h -> p h t"), AX.X, ALU.max)\
                    .then_inc(mk_ready.sem, 1)
                mkT_ps.wait(dve, b, 1)
                ch.step(nc.vector.tensor_reduce(mh[:], bk[0][0:H1, 64:64 + P], AX.X, ALU.max))
                nc.vector.tensor_scalar(dm[:], ident[0:H1, 0:H1], mh[:], -1.0, ALU.mult, ALU.mult)\
                    .then_inc(dm_ready.sem, 1)
                negm_ps.wait(dve, b, 1)
                ch.step(nc.vector.tensor_copy(negm[:], bk[0][:, 256:256 + H1]))
                for t in range(NT):
                    part = lg[:, t].rearrange("p (h f) -> p h f", f=NF)
                    nc.vector.tensor_tensor(part, part, bcast(negm[:], NF), ALU.add).then_inc(lg_sub.sem, 1)
                n_ps.wait(dve, b, 1)
                nps = bk[0][:, 288:288 + 8 * 18].rearrange("p (g k c) -> p g k c", g=8, k=2)
                ch.step(nc.vector.tensor_copy(nxt[0:64, :, 0, :], nps[0:64, :, 0, :]))
                ch.step(nc.vector.tensor_copy(nxt[64:P, :, 1, :], nps[64:P, :, 1, :]))
                ch.step(nc.vector.tensor_copy(dcol[0:64, :], nps[0:64, :, 0, DH1]))
                nc.vector.tensor_copy(dcol[64:P, :], nps[64:P, :, 1, DH1]).then_inc(d_ready.sem, 1)
                dsum_ps.wait(dve, b, 1)
                ch.step(nc.vector.scalar_tensor_tensor(nxt[0:64, :, 0, DH1], bk[0][0:64, 440:448], EPS1,
                                                       dcol[0:64, :], ALU.mult, ALU.add))
                nc.vector.scalar_tensor_tensor(nxt[64:P, :, 1, DH1], bk[0][64:P, 440:448], EPS1,
                                               dcol[64:P, :], ALU.mult, ALU.add).then_inc(nxt_ready.sem, 1)

                def ctx_out(u):
                    t, c = divmod(u, 2)
                    num_ps.wait(dve, b, u + 1)
                    v = bk[(7, 0)[c]][:, 0:72].rearrange("p (h c) -> p h c", c=DH1 + 1)
                    ch.step(nc.vector.reciprocal(rd[:], v[:, :, DH1]))
                    ins = nc.vector.tensor_tensor(
                        cx[:, t % 2, c * 64:c * 64 + 64].rearrange("p (h d) -> p h d", d=DH1),
                        v[:, :, 0:DH1], bcast(rd[:], DH1), ALU.mult)
                    if c == 0:
                        ch.step(ins)
                    else:
                        ins.then_inc(cx_ready.sem, 1)

                for u in range(2 * NT):
                    lq_ps.wait(dve, b, u + 1)
                    if u >= 1:
                        nm_ready.wait(dve, b, u)
                    ch.step(nc.vector.tensor_reduce(m1[:], bk[4 + u % 2][:].rearrange("p (h f) -> p h f", f=NF),
                                                    AX.X, ALU.max))
                    if u >= 1:
                        lq_shift.wait(dve, b, u)
                    ch.step(nc.vector.tensor_scalar(nm1[:, 0], m1[:], -1.0, None, ALU.mult))
                    nc.vector.scalar_tensor_tensor(nm1[:, 1], m1[:], -1.0, nm1[:, 0].bitcast(F32), ALU.mult,
                                                   ALU.subtract).then_inc(nm_ready.sem, 1)
                    if u >= 1:
                        ctx_out(u - 1)
                ctx_out(2 * NT - 1)
                yt_ps.wait(dve, b, 1)
                nc.vector.tensor_tensor(x1s[:], x0[:, bass.ds(b * NT, NT), :],
                                        bk[1][:].rearrange("p (t d) -> p t d", d=D), ALU.add)\
                    .then_inc(x1_ready.sem, 1)
                x1_ready.wait(dve, b, 1, alone=tally)
                layernorm(lambda t: x1s[:, t])
                xb_ps.wait(dve, b, 1, alone=tally)
                nc.vector.tensor_copy(xr[:, bass.ds(b * NT, NT), :], bk[3][:].rearrange("p (t d) -> p t d", d=D))\
                    .then_inc(xr_ready.sem, 1)
                dve.wait_ge(out_x1, b * 16 + 16)
                ch.end()

        @block.tensor
        def _(pe):
            pe.wait_ge(in_w, 16 * NLOADS)
            pe.wait_ge(s_silu2, 2)
            for j in range(6):
                last = nc.tensor.matmul(bk[0][:, j * B:(j + 1) * B], wmod[:, j * D:(j + 1) * D], cT[:],
                                        start=True, stop=True)
            last.then_inc(s_mod, 1)
            pe.wait_ge(bd, 16 * H1)
            pe.wait_ge(zeroed, 4)
            pe.wait_ge(s_gate, 1)

            def transposes(dst, src, last_sig):
                for t in range(NT):
                    last = nc.tensor.transpose(dst[:, t * P:(t + 1) * P], src(t), ident[:])
                last.then_inc(last_sig.sem, 1)

            with pe.Fori(0, B) as b:
                hn_ready.wait(pe, b, 1)
                transposes(bk[0], lambda t: hn[:, t], hT_ps)
                hT_sb.wait(pe, b, 1)
                nc.tensor.matmul(bk[1][:], wq[:], hT[:], start=True, stop=True)
                nc.tensor.matmul(bk[2][:], wk[:], hT[:], start=True, stop=True)
                for t in range(NT):
                    last = nc.tensor.matmul(bk[3][:, t * D:(t + 1) * D], hT[:, t * P:(t + 1) * P], wv[:],
                                            start=True, stop=True)
                last.then_inc(qkv_ps.sem, 1)
                qk_sb.wait(pe, b, 1)
                for t in range(NT):
                    last = nc.tensor.matmul(bk[0][:, t * H1:(t + 1) * H1], ksq[:, t * P:(t + 1) * P], selneg[:],
                                            start=True, stop=True)
                last.then_inc(ks_ps.sem, 1)
                for u in range(2 * NT):
                    t, c = divmod(u, 2)
                    lg_used.wait(pe, b, u - 1)
                    nc.tensor.matmul(bk[4 + u % 2][:], kT[:, t * P:(t + 1) * P], w0bd[:, c * HALF:(c + 1) * HALF],
                                     start=True, stop=True).then_inc(lg_ps.sem, 1)
                mk_ready.wait(pe, b, 1)
                nc.tensor.transpose(bk[0][0:H1, 64:64 + P], mkt[:], ident[:]).then_inc(mkT_ps.sem, 1)
                dm_ready.wait(pe, b, 1)
                nc.tensor.matmul(bk[0][:, 256:256 + H1], ones[0:H1, :], dm[:], start=True, stop=True)\
                    .then_inc(negm_ps.sem, 1)
                v_sb.wait(pe, b, 1)
                for g in range(H1 // 2):
                    for t in range(NT):
                        if g == 0:
                            e_ready.wait(pe, b, t + 1)
                        last = nc.tensor.matmul(bk[0][:, 288 + 18 * g:306 + 18 * g], lg[:, t, g * P:(g + 1) * P],
                                                vext[:, t, 2 * g:2 * g + 2, :], start=(t == 0), stop=(t == NT - 1))
                last.then_inc(n_ps.sem, 1)
                d_ready.wait(pe, b, 1)
                nc.tensor.matmul(bk[0][:, 440:448], onesblk[:], dcol[:], start=True, stop=True)\
                    .then_inc(dsum_ps.sem, 1)
                lg_used.wait(pe, b, 2 * NT)
                nxt_ready.wait(pe, b, 1)

                def logits(u):
                    t, c = divmod(u, 2)
                    if u >= 2:
                        phi_ready.wait(pe, b, u - 1)
                    nc.tensor.matmul(bk[4 + u % 2][:], qT[:, t * P:(t + 1) * P], w0bd[:, c * HALF:(c + 1) * HALF],
                                     start=True, stop=True).then_inc(lq_ps.sem, 1)

                logits(0)
                for u in range(2 * NT):
                    t, c = divmod(u, 2)
                    if u + 1 < 2 * NT:
                        logits(u + 1)
                    nm_ready.wait(pe, b, u + 1)
                    dst = bk[4 + u % 2][:].rearrange("p (h f) -> p h f", f=NF)
                    nc.tensor.matmul(dst, identr[:], bcast(nm1[:, 0], NF), start=False, stop=True,
                                     skip_group_check=True)
                    nc.tensor.matmul(dst, identr[:], bcast(nm1[:, 1], NF), start=False, stop=True,
                                     skip_group_check=True).then_inc(lq_shift.sem, 1)
                    phi_ready.wait(pe, b, u + 1)
                    if u >= 1:
                        phiT_sb.wait(pe, b, u)
                    transposes(bk[6], lambda i: phi[:, u % 2, i * P:(i + 1) * P], phiT_ps)
                    phiT_sb.wait(pe, b, u + 1)
                    if c == 0 and t >= 1:
                        cx_ready.wait(pe, b, t)
                    for i in range(4):
                        last = nc.tensor.matmul(bk[(7, 0)[c]][:, 18 * i:18 * i + 18],
                                                phiT[:, u % 2, i * P:(i + 1) * P], nxt[:, 4 * c + i],
                                                start=True, stop=True)
                    last.then_inc(num_ps.sem, 1)
                    if c == 0 and t >= 1:
                        nc.tensor.transpose(bk[3][:, (t - 1) * P:t * P], cx[:, (t - 1) % 2], ident[:])
                cx_ready.wait(pe, b, NT)
                nc.tensor.transpose(bk[3][:, (NT - 1) * P:NT * P], cx[:, (NT - 1) % 2], ident[:])\
                    .then_inc(cxT_ps.sem, 1)
                cxT_sb.wait(pe, b, 1)
                nc.tensor.matmul(bk[0][:], wo[:], cxT[:], start=True, stop=True).then_inc(wo_ps.sem, 1)
                y_sb.wait(pe, b, 1)
                transposes(bk[1], lambda t: yT[:, t * P:(t + 1) * P], yt_ps)
                hn_ready.wait(pe, b, 2)
                transposes(bk[2], lambda t: hn[:, t], hT_ps)
                hT_sb.wait(pe, b, 2)
                transposes(bk[3], lambda t: hT[:, t * P:(t + 1) * P], xb_ps)
                xr_ready.wait(pe, b, 1)


def over_slots():
    steps = []

    def add(kind, i, of):
        steps.append((kind, i // of, i % of))

    for u in range(UNITS):
        t, s = divmod(u, 2)

        def proj(c):
            add("proj", (t + 2) * 6 + 3 * s + c, 6 * NT)

        add("scores", u, UNITS)
        if s == 0:
            add("rotate", t + 1, NT)
        if u == 3:
            add("x_turn", 1, 1)
        if u == 7:
            add("ffn_value", -1, 3)
        proj(0)
        add("values", u - 2, UNITS)
        if u == 6:
            add("ffn_gate", -1, 3)
        if s == 0:
            add("project_out", t - 2, NT)
        if u == 2:
            add("x1", -1, 1)
            add("x_copy", 1, 1)
        if u == 6:
            add("ffn_value", -3, 3)
        proj(1)
        add("shift", u, UNITS)
        add("probs", u - 1, UNITS)
        if s == 1:
            add("rope", 2 * (t + 1), 2 * NT)
        proj(2)
        if u == 6:
            add("ffn_value", -2, 3)
        if s == 1:
            add("rope", 2 * (t + 1) + 1, 2 * NT)
        add("out", u - 2, UNITS)
        add("norm", 2 * (t + 2) + s, 2 * NT)
        if u == 2:
            add("ffn_turn", -1, 1)
        if u == 3:
            add("x_split", 1, 1)
            add("ffn_norm", -1, 1)
        if u == 4:
            add("ffn_apply", -1, 1)
        if u == 5:
            add("ffn_turn2", -1, 1)
            add("ffn_gate", -3, 3)
            add("ffn_gate", -2, 3)
        if u == 7:
            add("ffn_down", -1, 1)
    return steps


STEPS = over_slots()


class Ring:

    def __init__(self, sem, banks, items):
        self.sem, self.banks = sem, banks
        self.place, self.per = {}, 0
        for kind, off, i in STEPS:
            if kind in items:
                self.place[kind, i] = (off, self.per)
                self.per += items[kind]
        self.items = items
        assert self.per % len(banks) == 0

    def bank(self, kind, i, k=0):
        return self.banks[(self.place[kind, i][1] + k) % len(self.banks)]

    def wait(self, eng, m, kind, i, n, alone=None):
        off, at = self.place[kind, i]
        turn = m - off + 1
        if not isinstance(turn, int) or turn * self.per + at + n > 0:
            wait_for(eng, self.sem, turn * self.per + at + n, alone)

    def free(self, eng, m, kind, i, k=0, alone=None):
        self.wait(eng, m, kind, i, k + 1 - len(self.banks), alone)

    def copied(self, eng, m, kind, i, k=0, alone=None):
        self.wait(eng, m, kind, i, k + 1, alone)

    def skip(self, eng, m, kind, i):
        if kind in self.items:
            self.wait(eng, m, kind, i, 0)
            eng.sem_inc(self.sem, self.items[kind])


def turns(eng, step, rings=()):

    def turn(n, offs):
        for kind, off, i in STEPS:
            if off in offs:
                step(kind, n + off, i)
            else:
                for ring in rings:
                    ring.skip(eng, n + off, kind, i)

    turn(-1, (1,))
    turn(0, (0, 1))
    with eng.Fori(1, DEPTH * B - 1) as n:
        turn(eng.snap(n), (-1, 0, 1))
    turn(DEPTH * B - 1, (-1, 0))
    turn(DEPTH * B, (-1,))


def batch_slot(m):
    return (m & (B - 1)) * NT


def layers_block(nc, a, xr, consts):
    ident, identr, ones = (consts[n] for n in ("ident", "identr", "ones"))
    with ExitStack() as ctx:
        def sb(name, shape, dt=F32):
            return ctx.enter_context(nc.sbuf_tensor(name, shape, dt))

        def sem(name):
            return ctx.enter_context(nc.semaphore(name))

        def sig(name, per):
            return Signal(sem(name), per)

        def psum(name):
            return ctx.enter_context(nc.psum_tensor(name, [P, 512], F32))

        wraw = sb("wraw", [P, 3 * INNER])
        whi, wlo = sb("whi", [P, 3 * INNER], F32R), sb("wlo", [P, 3 * INNER], F32R)
        wo = sb("wo2", [P, HP, D])
        w1 = sb("w1", [P, 2 * FF])
        w2 = sb("w2", [P, 3, D])
        b1c = sb("b1c", [P, 2, 3])
        b2r = sb("b2r", [P, D])
        lnc = sb("lnc", [P, 2])
        scr = sb("scr", [P, 4, DH])
        tab = sb("tab", [P, 4, NT, DH])
        mask32 = sb("mask32", [P, 2, 2 * WIN])
        mask = sb("mask", [P, 2, 2 * WIN], BF16)
        identb = sb("identb", [P, P], BF16)
        zero, warm = sb("zero", [P, 1]), sb("warm", [P, 1])
        xw = sb("xw", [P, NT, D])
        xs = sb("xs", [P, L + 1])
        xh, xl = sb("xh", [P, L], F32R), sb("xl", [P, L], F32R)
        raw = sb("raw", [P, 2, 2, INNER])
        sq = sb("sq", [P, 2, INNER])
        ss = sb("ss", [P, 2 * H])
        rs, rh, rt = (sb(n, [P, 2 * H]) for n in ("rs2", "rh2", "rt2"))
        t1 = sb("t1", [P, 2, INNER])
        t2 = sb("t2", [P, 2, INNER])
        vb = sb("vb", [P, 2, 2 * HALF])
        kT = sb("kT2", [P, HP, WIN + L])
        qT = sb("qT2", [P, 2, HP, P])
        vp = sb("vp", [P, NW, HALF])
        mx = sb("mx", [P, 8])
        nm = sb("nm", [P, 2, 8], F32R)
        pr = sb("pr", [P, 2, HALF])
        den = sb("den", [P, 2, 8])
        pT = sb("pT", [P, 2, HALF])
        ob = sb("ob", [P, 2, HALF])
        oT = sb("oT", [P, 2, HP, P])
        x1w = sb("x1w", [P, NT, D])
        xs2 = sb("xs2", [P, L + 1])
        stats = sb("stats2", [P, NT, 6])
        mv = sb("mv2", [P, NT, 2])
        fs, fh, ft, fx = (sb(n, [P, NT]) for n in ("fs", "fh", "ft", "fx"))
        xnT = sb("xnT", [P, L])
        uT = sb("uT", [P, 3, L])
        xb = xn = y2 = xw

        pA = [psum(f"pA{i}") for i in range(2)]
        pS = [psum(f"pS{i}") for i in range(2)]
        pY = psum("pY")
        tr = Ring(sem("tr_read"), [psum(f"pT{i}") for i in range(2)],
                  {"x_turn": 1, "probs": 1, "out": 1, "ffn_turn": 1,
                   "ffn_norm": 2, "ffn_turn2": 1, "ffn_gate": 1, "rope": 2})
        ou = Ring(sem("ou_read"), [psum("pO")], {"values": 1, "ffn_value": 1, "ffn_down": 1})

        ld_const, ld_s, ld_wo, ld_f = (sem(n) for n in ("ld_const", "ld_s", "ld_wo", "ld_f"))
        ld_w = [sem(f"ld_w{i}") for i in range(3)]
        consts_up, w0_split = sem("consts_up"), sem("pads_up")
        tally = sem("tally2")
        w_hi, w_lo = sig("w_hi", 6), sig("w_lo", 6)
        tab_ready = sig("tab_ready", 4)
        xw_ready = sig("xw_ready", 1)
        x_ps = sig("x_ps", 1)
        xhl_ready = sig("xhl_ready", 2)
        a_ready = sig("a_ready", 6 * NT)
        a_read = sig("a_read", 6 * NT)
        sq_read = sig("sq_read", 2 * NT)
        v_moved = [sem(f"v_moved{t}") for t in range(NT)]
        qn_ready = sig("qn_ready", 2 * NT)
        t2_ready = sig("t2_ready", 2 * NT)
        t1_ready = sig("t1_ready", 2 * NT)
        rope_ready = sig("rope_ready", 2 * NT)
        r_ps = sig("r_ps", 4 * NT)
        s_ps = sig("s_ps", UNITS)
        nm_ready = sig("nm_ready", UNITS)
        s_shift = sig("s_shift", UNITS)
        p_ready = sig("p_ready", UNITS)
        den_ready = sig("den_ready", UNITS)
        pt_ps = sig("pt_ps", UNITS)
        o_half = sig("o_half", UNITS)
        o_ps = sig("o_ps", UNITS)
        ot_ps = sig("ot_ps", UNITS)
        y_ps = sig("y_ps", NT)
        x1_ready = sig("x1w_ready", 1)
        x1T_ps = sig("x1T_ps", 1)
        xb_ps = sig("xb_ps2", 2)
        xn_ready = sig("xn_ready", 1)
        xnT_ps = sig("xnT_ps", 1)
        g_ps = sig("g_ps", 3)
        u_ps = sig("u_ps", 3)
        f_ps = Signal(sem("f_ps"), 1, 1)
        x_done = Signal(sem("x_done"), 1, 1)
        norm_ch = Chain(sem("norm_chain"), NT * (1 + RSQRT_STEPS))
        max_ch = Chain(sem("max_chain"), 2 * UNITS)
        sum_ch = Chain(sem("sum_chain"), UNITS)
        ffn_ch = Chain(sem("ffn_chain"), 2 * NT + 1 + RSQRT_STEPS)
        y_ch = Chain(sem("y_chain"), 1)

        NLD_F = 1 + 3 * 3 + 3
        LD_W = [16, 16, 32]
        V_SENT = [16 * (4 * WPT - (2 if t == NT - 1 else 0)) for t in range(NT)]

        block = ctx.enter_context(nc.Block())

        @block.sync
        def _(sp):
            for t, src in ((mask32, a["mask"]),):
                sp.dma_start(t[:], src).then_inc(ld_const, 16)

            def load_w(l):
                w_lo.wait(sp, l, 0, alone=tally)
                for j in range(3):
                    dst, src = wraw[:, j * INNER:(j + 1) * INNER], a["Wqkv"][l, :, j * INNER:(j + 1) * INNER]
                    if j == 2:
                        dst = dst.rearrange("p (c m d) -> p c m d", c=2, d=2 * DH)
                        src = src.rearrange("p (m c d) -> p c m d", c=2, d=2 * DH)
                    for c in range(1 if j < 2 else 2):
                        sp.dma_start(dst if j < 2 else dst[:, c], src if j < 2 else src[:, c]).then_inc(ld_w[j], 16)

            def load_tables(l):
                t1_ready.wait(sp, l * B, 0, alone=tally)
                t2_ready.wait(sp, l * B, 0, alone=tally)
                sp.dma_start(tab[:], a["rot"]).then_inc(ld_s, 16)
                for i, name in enumerate(("q_scale", "k_scale")):
                    sp.dma_start(scr[:, 2 * i, :], a[name][l, :].partition_broadcast(P)).then_inc(ld_s, 16)
                    for s in range(2):
                        sp.dma_start(scr[:, 2 * i + 1, s * 32:s * 32 + 32],
                                     a[name][l, (1 - s) * 32:(1 - s) * 32 + 32].partition_broadcast(P))\
                            .then_inc(ld_s, 16)

            def load_wo(l):
                y_ps.wait(sp, l * B, 0, alone=tally)
                for c in range(2):
                    for s in range(2):
                        sp.dma_start(wo[64 * c:64 * c + 64, 4 * s:4 * s + 4, :],
                                     a["Wo"][l].rearrange("(m c s d) n -> d c s m n", c=2, s=2, d=DH)[:, c, s])\
                            .then_inc(ld_wo, 16)

            def load_ffn(l):
                x_done.wait(sp, l * B, 0, alone=tally)
                sp.dma_start(w1[:], a["W1"][l]).then_inc(ld_f, 16)
                for k, (f0, fn) in enumerate(FT):
                    sp.dma_start(w2[0:fn, k, :], a["W2"][l, f0:f0 + fn, :]).then_inc(ld_f, 16)
                    for s in range(2):
                        sp.dma_start(b1c[0:fn, s, k:k + 1],
                                     a["b1"][l, s * FF + f0:s * FF + f0 + fn].unsqueeze(1)).then_inc(ld_f, 16)
                sp.dma_start(b2r[:], a["b2"][l, :].partition_broadcast(P)).then_inc(ld_f, 16)
                sp.dma_start(lnc[:, 0:1], a["ln_g"][l, :].unsqueeze(1)).then_inc(ld_f, 16)
                sp.dma_start(lnc[:, 1:2], a["ln_b"][l, :].unsqueeze(1)).then_inc(ld_f, 16)

            def move_v(m, t):
                a_read.wait(sp, m, 6 * t + 6, alone=tally)
                o_ps.wait(sp, m, min(UNITS, 2 * t + 4) - UNITS, alone=tally)
                for j in range(WPT):
                    for s in range(2):
                        src = vb[WIN * j:WIN * j + WIN, t % 2, s * HALF:(s + 1) * HALF]
                        w = WPT * t + j
                        sp.dma_start(vp[64 * s + WIN:64 * s + 2 * WIN, w], src).then_inc(v_moved[t], 16)
                        if w + 1 < NW:
                            sp.dma_start(vp[64 * s:64 * s + WIN, w + 1], src).then_inc(v_moved[t], 16)

            def move_all(m):
                for t in range(NT):
                    move_v(m, t)

            load_w(0)
            load_tables(0)
            sp.wait_ge(w0_split, 1)
            move_v(0, 0)
            move_v(0, 1)
            load_wo(0)
            move_v(0, 2)
            move_v(0, 3)
            load_ffn(0)
            move_all(1)
            with sp.Fori(1, DEPTH) as l:
                move_all(sp.snap(l * B - 2))
                m = sp.snap(l * B - 1)
                move_v(m, 0)
                move_v(m, 1)
                load_w(l)
                move_v(m, 2)
                move_v(m, 3)
                load_tables(l)
                m = sp.snap(l * B)
                move_v(m, 0)
                move_v(m, 1)
                load_wo(l)
                move_v(m, 2)
                move_v(m, 3)
                m = sp.snap(l * B + 1)
                move_v(m, 0)
                move_v(m, 1)
                load_ffn(l)
                move_v(m, 2)
                move_v(m, 3)
            with sp.Fori(DEPTH * B - 2, DEPTH * B) as m:
                move_all(sp.snap(m))

        @block.gpsimd
        def _(pool):
            def split_w(l, chunks):
                for c in chunks:
                    pool.wait_ge(ld_w[c // 2], LD_W[c // 2] * (l + 1))
                    a_ready.wait(pool, l * B, c + 1 - 6, alone=tally)
                    part = slice(c * HALF, (c + 1) * HALF)
                    nc.gpsimd.tensor_tensor(whi[:, part], wraw[:, part], ones[:, 0:1].broadcast_to([P, HALF]), ALU.mult)\
                        .then_inc(w_hi.sem, 1)
                    w_hi.wait(pool, l, c + 1)
                    nc.gpsimd.tensor_tensor(wlo[:, part], wraw[:, part], whi[:, part].bitcast(F32), ALU.subtract)\
                        .then_inc(w_lo.sem, 1)

            def tables(l):
                pool.wait_ge(ld_s, l * 112 + 112)
                for i in range(4):
                    nc.gpsimd.tensor_tensor(tab[:, i], tab[:, i], over_heads(scr[:, i], NT), ALU.mult)\
                        .then_inc(tab_ready.sem, 1)
                tab_ready.wait(pool, l, 4, alone=tally)

            def rotate(m, t, i):
                qn_ready.wait(pool, m, 2 * t + i + 1)
                src = raw[:, t % 2, i]
                if i == 0:
                    rope_ready.wait(pool, m, 2 * t)
                for hh in range(2):
                    part = slice(hh * HALF, (hh + 1) * HALF)
                    ins = nc.gpsimd.tensor_tensor(
                        t2[:, i, part].rearrange("p (h s d) -> p h s d", s=2, d=32),
                        halves_swapped(src[:, part]),
                        tab[:, 2 * i + 1, t].rearrange("p (s d) -> p s d", s=2).unsqueeze(1)
                        .broadcast_to([P, 8, 2, 32]), ALU.mult)
                ins.then_inc(t2_ready.sem, 1)
                t2_ready.wait(pool, m, 2 * t + i + 1)
                t1_ready.wait(pool, m, 2 * t + i + 1)
                nc.gpsimd.tensor_tensor(t1[:, i], t1[:, i], t2[:, i], ALU.add).then_inc(rope_ready.sem, 1)

            def rotate_tiles(m, tiles):
                for t in tiles:
                    for i in range(2):
                        rotate(m, t, i)

            split_w(0, range(6))
            tables(0)
            with pool.Fori(1, DEPTH) as l:
                with pool.Fori((l - 1) * B, l * B - 1) as m:
                    rotate_tiles(pool.snap(m), range(NT))
                m = pool.snap(l * B - 1)
                rotate_tiles(m, range(3))
                split_w(l, range(3))
                rotate(m, 3, 0)
                split_w(l, range(3, 6))
                rotate(m, 3, 1)
                tables(l)
            with pool.Fori((DEPTH - 1) * B, DEPTH * B) as m:
                rotate_tiles(pool.snap(m), range(NT))

        @block.scalar
        def _(act):
            def shifted(dst, src):
                nc.scalar.activation(dst[0:64, 0:L], src[0:64, :], ACT.Copy)
                nc.scalar.activation(dst[64:P, 1:L + 1], src[64:P, :], ACT.Copy).then_inc(tr.sem, 1)

            def step(kind, m, i):
                t, s = divmod(i, 2)
                if kind == "x_turn":
                    x_ps.wait(act, m, 1)
                    xhl_ready.wait(act, m, 0)
                    shifted(xs, tr.bank(kind, i))
                elif kind == "proj":
                    t, c = divmod(i, 6)
                    a_ready.wait(act, m, i + 1)
                    src = pA[c % 2][:]
                    if c < 4:
                        j, hh = divmod(c, 2)
                        part = slice(hh * HALF, (hh + 1) * HALF)
                        if hh == 0:
                            sq_read.wait(act, m, 2 * t + j - 1)
                            rope_ready.wait(act, m, 2 * (t - 2) + j + 1)
                        nc.scalar.activation(raw[:, t % 2, j, part], src, ACT.Copy)
                        nc.scalar.activation(sq[:, j, part], src, ACT.Square).then_inc(a_read.sem, 1)
                    else:
                        if c == 4:
                            k = (t - 2) % NT
                            times = m + 1 if t >= 2 else m
                            if not isinstance(times, int) or times > 0:
                                act.wait_ge(v_moved[k], times * V_SENT[k])
                        nc.scalar.activation(vb[:, t % 2, (c - 4) * HALF:(c - 3) * HALF], src, ACT.Copy)\
                            .then_inc(a_read.sem, 1)
                elif kind == "rope":
                    for hh in range(2):
                        r_ps.wait(act, m, 2 * i + hh + 1)
                        src = tr.bank(kind, i, hh)[:].rearrange("p (k c) -> p k c", c=P)
                        if s == 0:
                            s_ps.wait(act, m, 2 * t + 2 - 4)
                            dst = qT[:, t % 2, 4 * hh:4 * hh + 4, :]
                        else:
                            s_ps.wait(act, m, min(UNITS, 2 * t + 4) - UNITS)
                            dst = kT[:, 4 * hh:4 * hh + 4, WIN + t * P:WIN + (t + 1) * P]
                        nc.scalar.activation(dst, src, ACT.Copy).then_inc(tr.sem, 1)
                elif kind == "shift":
                    s_shift.wait(act, m, i + 1)
                    pt_ps.wait(act, m, i - 1)
                    den_ready.wait(act, m, i - 1)
                    nc.scalar.activation(pr[:, i % 2], pS[i % 2][:], ACT.Exp).then_inc(p_ready.sem, 1)
                elif kind == "probs":
                    pt_ps.wait(act, m, i + 1)
                    o_ps.wait(act, m, i - 1)
                    nc.scalar.activation(pT[:, i % 2], tr.bank(kind, i)[:], ACT.Copy).then_inc(tr.sem, 1)
                elif kind == "out":
                    ot_ps.wait(act, m, i + 1)
                    if s == 0:
                        y_ps.wait(act, m, t - 1)
                    nc.scalar.activation(oT[:, t % 2, 4 * s:4 * s + 4, :],
                                         tr.bank(kind, i)[:].rearrange("p (k c) -> p k c", c=P), ACT.Copy)\
                        .then_inc(tr.sem, 1)
                elif kind == "ffn_turn":
                    x1T_ps.wait(act, m, 1)
                    shifted(xs2, tr.bank(kind, i))
                elif kind == "ffn_norm":
                    for k in range(2):
                        xb_ps.wait(act, m, k + 1)
                        nc.scalar.activation(xb[:, 2 * k:2 * k + 2], tr.bank(kind, i, k)[:, 0:2 * D].rearrange(
                            "p (t d) -> p t d", d=D), ACT.Copy).then_inc(tr.sem, 1)
                elif kind == "ffn_turn2":
                    xnT_ps.wait(act, m, 1)
                    act.wait_ge(ld_f, (m >> 2) * (16 * NLD_F) + 16 * NLD_F)
                    nc.scalar.activation(xnT[:], tr.bank(kind, i)[:], ACT.Identity, bias=lnc[:, 1:2],
                                         scale=lnc[:, 0:1]).then_inc(tr.sem, 1)
                elif kind == "ffn_gate":
                    fn = FT[i][1]
                    g_ps.wait(act, m, i + 1)
                    f_ps.wait(act, m, 0)
                    nc.scalar.activation(uT[0:fn, i], tr.bank(kind, i)[0:fn, :], ACT.Gelu,
                                         bias=b1c[0:fn, 1, i:i + 1]).then_inc(tr.sem, 1)
                    if i == 2:
                        nc.scalar.activation(warm[:], zero[:], ACT.Exp)

            act.sem_inc(f_ps.sem, 1)
            act.wait_ge(consts_up, 1)
            turns(act, step, [tr])

        @block.vector
        def _(dve):
            dve.wait_ge(ld_const, 16)
            nc.vector.memset(zero[:], 0.0)
            nc.vector.memset(xs[64:P, 0:1], 0.0)
            nc.vector.memset(xs2[64:P, 0:1], 0.0)
            nc.vector.memset(kT[:, :, 0:WIN], 0.0)
            nc.vector.memset(vp[0:WIN, 0, :], 0.0)
            nc.vector.memset(vp[64:64 + WIN, 0, :], 0.0).then_inc(w0_split, 1)
            nc.vector.tensor_copy(mask[:], mask32[:])
            nc.vector.tensor_copy(identb[:], ident[:]).then_inc(consts_up, 1)
            dve.wait_ge(consts_up, 1)

            def step(kind, m, i):
                t, s = divmod(i, 2)
                if kind == "x_copy":
                    x_ps.wait(dve, m, 0, alone=tally)
                    x_done.wait(dve, m, -2, alone=tally)
                    nc.vector.tensor_copy(xw[:], xr[:, bass.ds(batch_slot(m), NT), :]).then_inc(xw_ready.sem, 1)
                elif kind == "x_split":
                    tr.copied(dve, m, "x_turn", 0)
                    a_ready.wait(dve, m, 0)
                    nc.vector.tensor_copy(xh[:], xs[:, 0:L]).then_inc(xhl_ready.sem, 1)
                    xhl_ready.wait(dve, m, 1)
                    nc.vector.tensor_tensor(xl[:], xs[:, 0:L], xh[:].bitcast(F32), ALU.subtract)\
                        .then_inc(xhl_ready.sem, 1)
                elif kind == "norm":
                    a_read.wait(dve, m, 6 * t + 2 * s + 2)
                    nc.vector.tensor_reduce(ss[:, s * H:(s + 1) * H],
                                            sq[:, s].rearrange("p (h d) -> p h d", d=DH), AX.X, ALU.add)\
                        .then_inc(sq_read.sem, 1)
                    if s == 0:
                        return
                    sq_read.wait(dve, m, 2 * t + 2)
                    norm_ch.start(dve, m, t * (1 + RSQRT_STEPS))
                    norm_ch.step(nc.vector.tensor_scalar(ss[:], ss[:], NORM_FLOOR2, None, ALU.max))
                    rsqrt_steps(nc, norm_ch, rs[:], rh[:], rt[:], ss[:])
                    for j in range(2):
                        q = raw[:, t % 2, j].rearrange("p (h d) -> p h d", d=DH)
                        nc.vector.tensor_tensor(q, q, bcast(rs[:, j * H:(j + 1) * H], DH), ALU.mult)\
                            .then_inc(qn_ready.sem, 1)
                elif kind == "rotate":
                    wait_for(dve, tab_ready.sem, (m >> 2) * 4 + 4)
                    for j in range(2):
                        q = raw[:, i % 2, j].rearrange("p (h d) -> p h d", d=DH)
                        qn_ready.wait(dve, m, 2 * i + j + 1)
                        r_ps.wait(dve, m, 4 * (i - 1) + 2 * j + 2)
                        nc.vector.tensor_tensor(t1[:, j].rearrange("p (h d) -> p h d", d=DH), q,
                                                over_heads(tab[:, 2 * j, i], H), ALU.mult).then_inc(t1_ready.sem, 1)
                elif kind == "scores":
                    max_ch.start(dve, m, 2 * i)
                    s_ps.wait(dve, m, i + 1)
                    nm_ready.wait(dve, m, i)
                    max_ch.step(nc.vector.tensor_reduce(mx[:], pS[i % 2][:].rearrange("p (h c) -> p h c", c=64),
                                                        AX.X, ALU.max))
                    s_shift.wait(dve, m, i)
                    max_ch.step(nc.vector.tensor_scalar(nm[:, 0], mx[:], -1.0, None, ALU.mult))
                    nc.vector.scalar_tensor_tensor(nm[:, 1], mx[:], -1.0, nm[:, 0].bitcast(F32), ALU.mult,
                                                   ALU.subtract).then_inc(nm_ready.sem, 1)
                elif kind == "probs":
                    sum_ch.start(dve, m, i)
                    p_ready.wait(dve, m, i + 1)
                    sum_ch.step(nc.vector.tensor_reduce(den[:, i % 2], pr[:, i % 2].rearrange("p (h c) -> p h c", c=64),
                                                        AX.X, ALU.add))
                    nc.vector.reciprocal(den[:, i % 2], den[:, i % 2]).then_inc(den_ready.sem, 1)
                elif kind == "values":
                    o_ps.wait(dve, m, i + 1)
                    den_ready.wait(dve, m, i + 1)
                    ot_ps.wait(dve, m, i - 1)
                    nc.vector.tensor_tensor(ob[:, i % 2].rearrange("p (h d) -> p h d", d=DH),
                                            ou.bank(kind, i)[:].rearrange("p (h d) -> p h d", d=DH),
                                            bcast(den[:, i % 2], DH), ALU.mult).then_inc(ou.sem, 1)
                elif kind == "x1":
                    y_ps.wait(dve, m, NT)
                    nc.vector.tensor_tensor(x1w[:], xr[:, bass.ds(batch_slot(m), NT), :],
                                            pY[:].rearrange("p (t d) -> p t d", d=D), ALU.add).then_inc(x1_ready.sem, 1)
                elif kind == "ffn_norm":
                    ffn_ch.start(dve, m)
                    tr.copied(dve, m, kind, i, 1, alone=tally)
                    for j in range(NT):
                        ffn_ch.count(nc.vector.bn_stats(stats[:, j], xb[:, j]))
                    ffn_ch.wait(alone=tally)
                    for j in range(NT):
                        ffn_ch.count(nc.vector.bn_aggr(mv[:, j], stats[:, j]))
                elif kind == "ffn_apply":
                    ffn_ch.start(dve, m, 2 * NT)
                    ffn_ch.wait()
                    ffn_ch.step(nc.vector.tensor_scalar(fx[:], mv[:, :, 1], LN_EPS, None, ALU.add))
                    rsqrt_steps(nc, ffn_ch, fs[:], fh[:], ft[:], fx[:])
                    for j in range(NT):
                        ins = nc.vector.tensor_scalar(xn[:, j], xb[:, j], mv[:, j, 0:1], fs[:, j:j + 1],
                                                      ALU.subtract, ALU.mult)
                    ins.then_inc(xn_ready.sem, 1)
                elif kind == "ffn_value":
                    fn = FT[i][1]
                    u_ps.wait(dve, m, i + 1)
                    tr.copied(dve, m, "ffn_gate", i)
                    nc.vector.scalar_tensor_tensor(uT[0:fn, i], ou.bank(kind, i)[0:fn, :], b1c[0:fn, 0, i:i + 1],
                                                   uT[0:fn, i], ALU.add, ALU.mult).then_inc(ou.sem, 1)
                elif kind == "ffn_down":
                    f_ps.wait(dve, m, 1)
                    y_ch.start(dve, m)
                    ou.copied(dve, m, "ffn_value", 2)
                    nc.vector.tensor_tensor(y2[:], ou.bank(kind, i)[:].rearrange("p (t d) -> p t d", d=D),
                                            b2r[:].unsqueeze(1).broadcast_to([P, NT, D]), ALU.add).then_inc(ou.sem, 1)
                    ou.copied(dve, m, kind, i)
                    nc.vector.tensor_tensor(xr[:, bass.ds(batch_slot(m), NT), :], y2[:], x1w[:], ALU.add)\
                        .then_inc(x_done.sem, 1)

            dve.sem_inc(x_done.sem, 1)
            turns(dve, step, [ou])

        @block.tensor
        def _(pe):
            def transposes(dst, src):
                for t in range(4):
                    last = nc.tensor.transpose(dst[:, t * P:(t + 1) * P], src(t), ident[:])
                return last

            def step(kind, m, i):
                t, s = divmod(i, 2)
                if kind == "x_turn":
                    xw_ready.wait(pe, m, 1)
                    tr.free(pe, m, kind, i)
                    transposes(tr.bank(kind, i), lambda j: xw[:, j]).then_inc(x_ps.sem, 1)
                elif kind == "proj":
                    t, c = divmod(i, 6)
                    xt = slice(t * P, (t + 1) * P)
                    if i == 0:
                        xhl_ready.wait(pe, m, 2)
                    if t == 0:
                        wait_for(pe, w_lo.sem, (m >> 2) * 6 + c + 1)
                    a_read.wait(pe, m, i - 1)
                    for j, (x, w) in enumerate(((xh, whi), (xl, whi), (xh, wlo))):
                        last = nc.tensor.matmul(pA[c % 2][:], x[:, xt], w[:, c * HALF:(c + 1) * HALF],
                                                start=(j == 0), stop=(j == 2))
                    last.then_inc(a_ready.sem, 1)
                elif kind == "rope":
                    rope_ready.wait(pe, m, i + 1)
                    for hh in range(2):
                        tr.free(pe, m, kind, i, hh)
                        transposes(tr.bank(kind, i, hh),
                                   lambda k: t1[:, s, (4 * hh + k) * P:(4 * hh + k + 1) * P]).then_inc(r_ps.sem, 1)
                elif kind == "scores":
                    bank = pS[i % 2]
                    if s == 0:
                        tr.copied(pe, m, "rope", 2 * t + 1, 1)
                    p_ready.wait(pe, m, i - 1)
                    nc.tensor.matmul(bank[:].rearrange("p (h c) -> p h c", c=64), identb[:],
                                     over_heads(mask[:, min(t, 1)], 8), start=True, stop=True)
                    part = slice(64 * s, 64 * s + 64)
                    for g in range(HP):
                        for j in range(WPT):
                            k0 = t * P + j * WIN
                            last = nc.tensor.matmul(bank[WIN * j:WIN * (j + 1), 64 * g:64 * (g + 1)],
                                                    qT[part, t % 2, g, WIN * j:WIN * (j + 1)],
                                                    kT[part, g, k0:k0 + 2 * WIN], start=False, stop=True,
                                                    skip_group_check=True)
                    last.then_inc(s_ps.sem, 1)
                elif kind == "shift":
                    dst = pS[i % 2][:].rearrange("p (h c) -> p h c", c=64)
                    nm_ready.wait(pe, m, i + 1)
                    for j in range(2):
                        last = nc.tensor.matmul(dst, identr[:], bcast(nm[:, j], 64), start=False, stop=True,
                                                skip_group_check=True)
                    last.then_inc(s_shift.sem, 1)
                elif kind == "probs":
                    p_ready.wait(pe, m, i + 1)
                    tr.free(pe, m, kind, i)
                    transposes(tr.bank(kind, i), lambda j: pr[:, i % 2, j * P:(j + 1) * P]).then_inc(pt_ps.sem, 1)
                elif kind == "values":
                    bank = ou.bank(kind, i)
                    tr.copied(pe, m, "probs", i)
                    if s == 0:
                        pe.wait_ge(v_moved[t], m * V_SENT[t] + V_SENT[t])
                    ou.free(pe, m, kind, i, alone=tally)
                    for c in range(2):
                        part = slice(64 * c, 64 * c + 64)
                        for k in range(4):
                            g, v = 2 * k + c, 2 * k + s
                            for j in range(WPT):
                                last = nc.tensor.matmul(bank[WIN * j:WIN * (j + 1), 64 * g:64 * (g + 1)],
                                                        pT[part, i % 2, k * P + WIN * j:k * P + WIN * (j + 1)],
                                                        vp[part, WPT * t + j, 64 * v:64 * (v + 1)],
                                                        start=True, stop=True)
                        if c == 0:
                            last.then_inc(o_half.sem, 1)
                            o_half.wait(pe, m, i + 1, alone=tally)
                    last.then_inc(o_ps.sem, 1)
                elif kind == "out":
                    ou.copied(pe, m, "values", i)
                    tr.free(pe, m, kind, i)
                    transposes(tr.bank(kind, i), lambda j: ob[:, i % 2, j * P:(j + 1) * P]).then_inc(ot_ps.sem, 1)
                elif kind == "project_out":
                    tr.copied(pe, m, "out", 2 * i + 1)
                    if i == 0:
                        pe.wait_ge(ld_wo, (m >> 2) * 64 + 64)
                        x1_ready.wait(pe, m, 0)
                    for g in range(HP):
                        last = nc.tensor.matmul(pY[:, i * D:(i + 1) * D], oT[:, i % 2, g, :], wo[:, g, :],
                                                start=(g == 0), stop=(g == HP - 1))
                    last.then_inc(y_ps.sem, 1)
                elif kind == "ffn_turn":
                    x1_ready.wait(pe, m, 1)
                    tr.free(pe, m, kind, i)
                    transposes(tr.bank(kind, i), lambda j: x1w[:, j]).then_inc(x1T_ps.sem, 1)
                elif kind == "ffn_norm":
                    tr.copied(pe, m, "ffn_turn", 0)
                    for k in range(2):
                        tr.free(pe, m, kind, i, k)
                        for j in range(2):
                            last = nc.tensor.transpose(tr.bank(kind, i, k)[:, j * P:(j + 1) * P],
                                                       xs2[:, (2 * k + j) * P:(2 * k + j + 1) * P], ident[:])
                        last.then_inc(xb_ps.sem, 1)
                elif kind == "ffn_turn2":
                    xn_ready.wait(pe, m, 1)
                    tr.free(pe, m, kind, i)
                    transposes(tr.bank(kind, i), lambda j: xn[:, j]).then_inc(xnT_ps.sem, 1)
                elif kind == "ffn_gate":
                    f0, fn = FT[i]
                    if i == 0:
                        pe.wait_ge(ld_f, (m >> 2) * (16 * NLD_F) + 16 * NLD_F)
                        tr.copied(pe, m, "ffn_turn2", 0)
                    tr.free(pe, m, kind, i)
                    nc.tensor.matmul(tr.bank(kind, i)[0:fn, :], w1[:, FF + f0:FF + f0 + fn], xnT[:],
                                     start=True, stop=True).then_inc(g_ps.sem, 1)
                elif kind == "ffn_value":
                    f0, fn = FT[i]
                    ou.free(pe, m, kind, i)
                    nc.tensor.matmul(ou.bank(kind, i)[0:fn, :], w1[:, f0:f0 + fn], xnT[:], start=True, stop=True)\
                        .then_inc(u_ps.sem, 1)
                elif kind == "ffn_down":
                    ou.free(pe, m, kind, i)
                    for j in range(NT):
                        for k, (f0, fn) in enumerate(FT):
                            last = nc.tensor.matmul(ou.bank(kind, i)[:, j * D:(j + 1) * D],
                                                    uT[0:fn, k, j * P:(j + 1) * P], w2[0:fn, k, :],
                                                    start=(k == 0), stop=(k == 2))
                    last.then_inc(f_ps.sem, 1)

            pe.wait_ge(consts_up, 1)
            turns(pe, step)


def final_block(nc, xr, x1_dram, out, mod, consts):
    ident = consts["ident"]
    with ExitStack() as ctx:
        def sem(name):
            return ctx.enter_context(nc.semaphore(name))

        x1 = ctx.enter_context(nc.sbuf_tensor("x1f", [P, B, NT, D], F32))
        xc = ctx.enter_context(nc.sbuf_tensor("xcf", [P, B, NT, D], F32))
        gT = ctx.enter_context(nc.sbuf_tensor("gTf", [P, B, L], F32))
        res = ctx.enter_context(nc.sbuf_tensor("resf", [P, B, NT, D], F32))
        ps = [ctx.enter_context(nc.psum_tensor(f"f{i}", [P, 512], F32)) for i in range(8)]
        loaded, turned, gated, back, done, stored = (sem(n) for n in ("x1_loaded", "turned", "gated", "turned_back",
                                                                      "out_ready", "out_stored"))
        block = ctx.enter_context(nc.Block())

        @block.sync
        def _(sp):
            for b in range(B):
                sp.dma_start(x1[:, b], x1_dram[b]).then_inc(loaded, 16)
            for b in range(B):
                sp.wait_ge(done, b + 1)
                sp.dma_start(out[b].rearrange("(t p) d -> p t d", p=P), res[:, b]).then_inc(stored, 16)
            sp.wait_ge(stored, 16 * B)

        @block.tensor
        def _(pe):
            for b in range(B):
                for t in range(NT):
                    last = nc.tensor.transpose(ps[b][:, t * P:(t + 1) * P], xr[:, b * NT + t, :], ident[:])
                last.then_inc(turned, 1)
            for b in range(B):
                pe.wait_ge(gated, b + 1)
                for t in range(NT):
                    last = nc.tensor.transpose(ps[4 + b][:, t * P:(t + 1) * P], gT[:, b, t * P:(t + 1) * P], ident[:])
                last.then_inc(back, 1)

        @block.scalar
        def _(act):
            for b in range(B):
                act.wait_ge(turned, b + 1)
                nc.scalar.activation(gT[:, b], ps[b][:], ACT.Copy, scale=mod[:, 5, b:b + 1]).then_inc(gated, 1)

        @block.vector
        def _(dve):
            dve.wait_ge(loaded, 16 * B)
            for b in range(B):
                dve.wait_ge(back, b + 1)
                nc.vector.tensor_tensor(res[:, b], ps[4 + b][:].rearrange("p (t d) -> p t d", d=D), x1[:, b], ALU.add)\
                    .then_inc(done, 1)


def build(nc, a, out):
    with ExitStack() as ctx:
        xr = ctx.enter_context(nc.sbuf_tensor("xr", [P, B * NT, D], F32))
        mod = ctx.enter_context(nc.sbuf_tensor("mod", [P, 6, B], F32))
        consts = {n: ctx.enter_context(nc.sbuf_tensor(n, [P, P], F32)) for n in ("ident", "onesblk", "ones")}
        consts["identr"] = ctx.enter_context(nc.sbuf_tensor("identr", [P, P], F32R))
        x1_dram = nc.dram_tensor("x1_scratch", (B, P, NT, D), F32).ap()
        attention1_block(nc, a, xr, x1_dram, mod, consts)
        layers_block(nc, a, xr, consts)
        final_block(nc, xr, x1_dram, out, mod, consts)


def constants():
    f = np.float32
    half = np.arange(0, DH, 2, dtype=f)
    inv_freq = (f(1.0) / np.power(f(10000.0), half / f(DH), dtype=f)).astype(f)
    pos = np.arange(L, dtype=f)
    ang = pos[:, None] * inv_freq[None, :]
    base = ((half + f(0.4 * DH)) / f(1.4 * DH)).astype(f)
    power = ((pos - L // 2) / (WIN // 2)).astype(f)
    scale = np.power(base[None, :], power[:, None], dtype=f)
    cos, sin = np.cos(ang).astype(f), np.sin(ang).astype(f)
    rot = np.empty((4, L, DH), f)
    for i, (s, m) in enumerate(((scale, QK_SCALE), (f(1.0) / scale, 1.0))):
        rot[2 * i] = np.concatenate([cos * s, cos * s], -1) * f(m)
        rot[2 * i + 1] = np.concatenate([-sin * s, sin * s], -1) * f(m)
    rot = np.ascontiguousarray(rot.reshape(4, NT, P, DH).transpose(2, 0, 1, 3))
    mask = np.zeros((P, 2, 2 * WIN), f)
    i = np.arange(P)[:, None] % WIN
    j = np.arange(2 * WIN)[None, :] - WIN
    mask[:, :] = np.where((i < j) | (i > j + WIN), f(MASKED), f(0))[:, None]
    mask[0:WIN, 0, 0:WIN] = MASKED
    onesblk = np.kron(np.eye(2, dtype=f), np.ones((64, 64), f))
    selneg = np.kron(np.eye(H1, dtype=f), np.full((DH1, 1), -0.5, f))
    return {"rot": rot, "mask": mask, "ident": np.eye(P, dtype=f), "onesblk": onesblk, "selneg": selneg}


def kernel(**inputs):
    import concourse.bacc as bacc
    from concourse.bass_utils import run_bass_kernel_spmd

    x = {k: np.ascontiguousarray(v) for k, v in inputs.items()}
    arrays = {"x": x["L0_attn_x"], "Wrf": x["L0_attn_Wrf"], "bv": x["L0_attn_bv"], "wmod": x["L0_wmod"],
              "cT": np.ascontiguousarray(x["L0_c"].T)}
    for w in ("Wq", "Wk", "Wv", "Wo"):
        arrays[w + "T"] = np.ascontiguousarray(x["L0_attn_" + w].T)
    arrays["bcol"] = np.ascontiguousarray(np.stack([x["L0_attn_" + n] for n in ("bq", "bk", "bo")], 1))
    for w in ("Wqkv", "q_scale", "k_scale", "Wo", "ln_g", "ln_b", "W1", "b1", "W2", "b2"):
        arrays[w] = x["L0_ffn_" + w]
    arrays.update(constants())
    nc = bacc.Bacc("TRN2", target_bir_lowering=False, num_devices=1)
    a = {k: nc.dram_tensor("in_" + k, v.shape, mybir.dt.from_np(v.dtype), kind="ExternalInput").ap()
         for k, v in arrays.items()}
    out = nc.dram_tensor("out", (B, L, D), F32, kind="ExternalOutput").ap()
    build(nc, a, out)
    r = run_bass_kernel_spmd(nc, [{"in_" + k: v for k, v in arrays.items()}], core_ids=[0])
    return r.results[0]["out"]
```

```python
from contextlib import ExitStack

import numpy as np

import concourse.bass as bass
from concourse import mybir

F32 = mybir.dt.float32
F32R = mybir.dt.float32r
BF16 = mybir.dt.bfloat16
I32 = mybir.dt.int32
ALU = mybir.AluOpType
ACT = mybir.ActivationFunctionType
AX = mybir.AxisListType

P = 128
B, L, D = 4, 512, 128
NT = L // P
H1, DH1, NF = 16, 8, 64
EPS1 = 1e-6
LN_EPS = 1e-5
DEPTH = 6
H, DH = 16, 64
HP = H // 2
INNER = H * DH
WIN = 32
WPT = P // WIN
NW = L // WIN
FF = int(D * 4 * 2 / 3)
FT = [(0, 128), (128, 128), (256, FF - 256)]
QK_SCALE = 8.0
MASKED = -1e30
HALF = 512
UNITS = 2 * NT
RSQRT_SEED = float(0x5F3759DF + 0x3FC00000)
NORM_FLOOR2 = 1e-24


def wait_for(eng, sem, value, alone=None):
    eng.wait_ge(sem, value)
    if alone is not None:
        eng.sem_inc(alone, 1)


class Signal:

    def __init__(self, sem, per, base=0):
        self.sem, self.per, self.base = sem, per, base

    def wait(self, eng, turn, n, alone=None):
        value = turn * self.per + (n + self.base)
        if not isinstance(value, int) or value > 0:
            wait_for(eng, self.sem, value, alone)


class Chain:

    def __init__(self, sem, per):
        self.sem, self.per, self.n = sem, per, 0

    def start(self, eng, turn, done=0):
        self.eng, self.turn, self.n = eng, turn, done

    def count(self, ins):
        self.n += 1
        assert self.n <= self.per
        ins.then_inc(self.sem, 1)

    def wait(self, alone=None):
        wait_for(self.eng, self.sem, self.turn * self.per + self.n, alone)

    def step(self, ins, alone=None):
        self.count(ins)
        self.wait(alone)

    def end(self):
        assert self.n == self.per, (self.n, self.per)


RSQRT_STEPS = 12


def rsqrt_steps(nc, chain, y, half, tmp, x, shift, op):
    chain.step(nc.vector.tensor_scalar(half, x, shift, -0.5, op, ALU.mult))
    chain.step(nc.vector.tensor_scalar(y.bitcast(I32), half.bitcast(I32), 1, None, ALU.logical_shift_right))
    chain.step(nc.vector.tensor_scalar(y.bitcast(I32), y.bitcast(I32), -1.0, RSQRT_SEED, ALU.mult, ALU.add))
    for _ in range(3):
        chain.step(nc.vector.tensor_tensor(tmp, y, y, ALU.mult))
        chain.step(nc.vector.tensor_tensor(tmp, tmp, half, ALU.mult))
        chain.step(nc.vector.scalar_tensor_tensor(y, tmp, 1.5, y, ALU.add, ALU.mult))


def bcast(ap, n):
    return ap.unsqueeze(2).broadcast_to([ap.shape[0], ap.shape[1], n])


def over_heads(ap, n):
    return ap.unsqueeze(1).broadcast_to([ap.shape[0], n, ap.shape[1]])


def halves_swapped(t):
    a = t.rearrange("p (h s d) -> p h s d", s=2, d=DH // 2)
    return a[:, :, ::-1, :]


class Ring:

    def __init__(self, sem, banks, items, steps):
        self.sem, self.banks, self.items = sem, banks, items
        self.place, self.per = {}, 0
        for kind, off, i in steps:
            if kind in items:
                self.place[kind, i] = (off, self.per)
                self.per += self.of(kind, i)
        assert self.per % len(banks) == 0

    def of(self, kind, i):
        n = self.items.get(kind, 0)
        return n if isinstance(n, int) else n[i % len(n)]

    def bank(self, kind, i, k=0):
        return self.banks[(self.place[kind, i][1] + k) % len(self.banks)]

    def wait(self, eng, m, kind, i, n, alone=None):
        off, at = self.place[kind, i]
        turn = m - off + 1
        if not isinstance(turn, int) or turn * self.per + at + n > 0:
            wait_for(eng, self.sem, turn * self.per + at + n, alone)

    def free(self, eng, m, kind, i, k=0, alone=None):
        self.wait(eng, m, kind, i, k + 1 - len(self.banks), alone)

    def copied(self, eng, m, kind, i, k=0, alone=None):
        self.wait(eng, m, kind, i, k + 1, alone)

    def skip(self, eng, m, kind, i):
        if self.of(kind, i):
            self.wait(eng, m, kind, i, 0)
            eng.sem_inc(self.sem, self.of(kind, i))


def turns(eng, steps, batches, step, rings=()):

    def turn(n, offs):
        for kind, off, i in steps:
            if off in offs:
                step(kind, n + off, i)
            else:
                for ring in rings:
                    ring.skip(eng, n + off, kind, i)

    turn(-1, (1,))
    turn(0, (0, 1))
    with eng.Fori(1, batches - 1) as n:
        turn(eng.snap(n), (-1, 0, 1))
    turn(batches - 1, (-1, 0))
    turn(batches, (-1,))


def first_steps():
    steps = []
    add = lambda kind, off, i=0: steps.append((kind, off, i))
    for u in range(10):
        q = u - 2
        if q >= 0:
            add("q_logits", -1, q)
        if u < 8:
            add("k_logits", 0, u)
        if u == 0:
            add("k_norm", -1)
            add("proj_v", 0)
            add("proj_q", 0)
        if u == 1:
            add("h_apply", 1)
        if u == 2:
            add("h_turn", 1)
        if u == 8:
            add("head_tokens", 0)
            add("head_max", 0)
            add("proj_k", 1)
        if q >= 1:
            add("q_turn", -1, q - 1)
        if q >= 2:
            add("q_num", -1, q - 2)
            if q in (4, 6):
                add("ctx_turn", -1, q // 2 - 2)
        if u == 8:
            add("head_spread", 0)
        if q >= 0:
            add("q_shift", -1, q)
        if u == 9:
            add("k_sum", 0, 0)
        if u == 8:
            add("k_sub", 0, 0)
            add("k_sub", 0, 1)
            add("key_norm", 1)
    add("k_sub", 0, 2)
    add("q_turn", -1, 7)
    add("k_sub", 0, 3)
    add("q_num", -1, 6)
    add("k_sum", 0, 1)
    add("ctx_turn", -1, 2)
    add("q_num", -1, 7)
    add("q_move", 0)
    add("k_sum", 0, 2)
    add("k_sum", 0, 3)
    add("ctx_turn", -1, 3)
    return steps


FIRST_STEPS = first_steps()


def attention1_block(nc, a, xr, x1_dram, mod, consts):
    ident, identr = consts["ident"], consts["identr"]
    with ExitStack() as ctx:
        def sb(name, shape, dt=F32):
            return ctx.enter_context(nc.sbuf_tensor(name, shape, dt))

        def sem(name):
            return ctx.enter_context(nc.semaphore(name))

        def sig(name, per, base=0):
            return Signal(sem(name), per, base)

        def psum(name):
            return ctx.enter_context(nc.psum_tensor(name, [P, 512], F32))

        onesblk, ones = sb("onesblk", [P, P]), sb("ones", [P, P])
        x0 = sb("x0", [P, B * NT, D])
        wq, wk, wv, wo = (sb(n, [P, D]) for n in ("wq", "wk", "wv", "wo"))
        w0bd = sb("w0bd", [P, H1 * NF])
        selneg = sb("selneg", [P, H1])
        bcol = sb("bcol", [P, 3])
        bvrow = sb("bvrow", [P, D])
        cT = sb("cT", [P, B])
        cexp = sb("cexp", [P, B])
        wmod = sb("wmod", [P, 6 * D])
        gab = sb("gab", [P, B])
        sgn = sb("sgn", [P, B])
        stats = sb("stats", [P, B * NT, 6])
        mv = sb("mv", [P, B * NT, 2])
        rs, rh, rt = (sb(n, [P, B * NT]) for n in ("rs", "rh", "rt"))
        hn = sb("hn", [P, NT, D])
        hn2 = sb("hn2", [P, B * NT, D])
        hT = sb("hT", [P, L])
        qT, qTn, kT, ksq = (sb(n, [P, L]) for n in ("qT1", "qTn1", "kT1", "ksq1"))
        vext = sb("vext", [P, NT, H1, DH1 + 1])
        ksum = sb("ksum", [P, NT * H1])
        lg = sb("lg", [P, NT, H1 * NF])
        mk = sb("mk", [P, NT, H1])
        mkt = sb("mkt", [P, H1])
        mh = sb("mh", [H1, 1])
        dm = sb("dm", [H1, H1])
        negm = sb("negm", [P, H1])
        nxt = sb("nxt", [P, H1 // 2, 2, DH1 + 1])
        dcol = sb("dcol", [P, H1 // 2])
        m1 = sb("m1", [P, 8])
        nm1 = sb("nm1", [P, 2, 8], F32R)
        phi = sb("phi", [P, 2, HALF])
        phiT = sb("phiT", [P, 2, HALF])
        rd = sb("rd", [P, 8])
        cx = sb("cx", [P, 2, D])
        cxT = sb("cxT", [P, B * NT, P])
        yT = sb("yT", [P, 2, L])
        h2T = sb("h2T", [P, 2, L])
        x1s = sb("x1s", [P, B * NT, D])
        pK = [psum(f"pK{i}") for i in range(2)]
        pQ = [psum(f"pQ{i}") for i in range(2)]
        pN = psum("pN")
        tr = Ring(sem("tr1_read"), [psum(f"pU{i}") for i in range(2)],
                  {"h_turn": 2, "proj_q": 1, "proj_k": 1, "q_turn": 1, "ctx_turn": 1}, FIRST_STEPS)
        ac = Ring(sem("ac_read"), [psum("pC")],
                  {"key_norm": 1, "proj_v": 1, "head_max": 1, "head_spread": 1, "k_sum": (0, 0, 0, 1), "k_norm": 1}, FIRST_STEPS)

        in_x, in_w, bd, out_x1, zeroed = (sem(n) for n in ("in_x", "in_w", "bd_loaded", "x1_stored", "zeroed"))
        s_silu, s_silu2, s_mod, s_gate = sem("silu_exp"), sem("silu_done"), sem("mod_ps"), sem("mod_sb")
        ch0 = Chain(sem("setup_chain"), 13)
        tally = sem("tally1")
        hn_ready = sig("hn_ready", 1)
        qT_ready = sig("qT_ready", 1)
        h_ps = sig("h_ps", 2)
        q_ps, k_ps, v_ps, ks_ps = (sig(n, 1) for n in ("q_ps", "k_ps", "v_ps", "ks_ps"))
        ksq_ready = sig("ksq_ready", 1)
        ksum_ready = sig("ksum_ready", 1)
        lg_ps = sig("lg_ps", 2 * NT)
        lg_used = sig("lg_used", 2 * NT)
        mk_part = sig("mk_part", 2 * NT)
        mk_ready = sig("mk_ready", 1)
        mkT_ps = sig("mkT_ps", 1)
        mh_ready = sig("mh_ready", 1)
        negm_ps = sig("negm_ps", 1)
        lg_sub, lg_sub_odd = sig("lg_sub", NT // 2), sig("lg_sub_odd", NT // 2)
        e_ready = sig("e_ready", NT)
        n_ps = sig("n_ps", 1)
        dsum_ps = sig("dsum_ps", 1)
        lq_ps = sig("lq_ps", 2 * NT, 2)
        q_max = sig("q_max", 4 * NT, 2)
        nm_ready = sig("nm1_ready", 2 * NT, 2)
        lq_shift = sig("lq_shift", 2 * NT, 2)
        phi_ready = sig("phi_ready", 2 * NT, 2)
        phiT_ps = sig("phiT_ps", 2 * NT, 2)
        num_ps = sig("num_ps", 2 * NT, 2)
        rd_ready = sig("rd_ready", 2 * NT, 2)
        cx_part = sig("cx_part", 2 * NT, 2)
        cxT_ps = sig("cxT_ps", NT, 2)
        wo_ps, y_sb, yt_ps, x1_ready, h2_ps, h2_sb, xb_ps, xr_ready = (
            sem(n) for n in ("wo_ps", "y_sb", "yt_ps", "x1_ready", "h2_ps", "h2_sb", "xb_ps", "xr_ready"))
        hn2_ready = sem("hn2_ready")
        norms = [Chain(sem(f"norm_chain{i}"), 2 * B * NT + RSQRT_STEPS) for i in range(2)]
        block = ctx.enter_context(nc.Block())

        @block.sync
        def _(sp):
            for b in range(B):
                sp.dma_start(x0[:, b * NT:(b + 1) * NT], a["x"][b].rearrange("(t p) d -> p t d", p=P)).then_inc(in_x, 16)
            loads = [(cT, a["cT"]), (wmod, a["wmod"]), (ident, a["ident"]), (bcol, a["bcol"]), (wq, a["WqT"]),
                     (wk, a["WkT"]), (wv, a["WvT"]), (wo, a["WoT"]), (selneg, a["selneg"]), (onesblk, a["onesblk"])]
            for t, src in loads:
                sp.dma_start(t[:], src).then_inc(in_w, 16)
            sp.dma_start(bvrow[:], a["bv"].partition_broadcast(P)).then_inc(in_w, 16)
            sp.wait_ge(zeroed, 1)
            for h in range(H1):
                sp.dma_start(w0bd[DH1 * h:DH1 * (h + 1), NF * h:NF * (h + 1)], a["Wrf"][0, h]).then_inc(bd, 16)
            for b in range(B):
                sp.wait_ge(x1_ready, b + 1)
                sp.dma_start(x1_dram[b], x1s[:, b * NT:(b + 1) * NT]).then_inc(out_x1, 16)
            sp.wait_ge(out_x1, 16 * B)

        NLOADS = 11

        @block.gpsimd
        def _(pool):
            nc.gpsimd.memset(w0bd[:], 0.0).then_inc(zeroed, 1)
            nc.gpsimd.memset(nxt[:], 0.0).then_inc(zeroed, 1)
            nc.gpsimd.memset(ones[:], 1.0).then_inc(zeroed, 1)
            nc.gpsimd.memset(vext[:], 1.0).then_inc(zeroed, 1)
            with pool.Fori(0, B) as b:
                b = pool.snap(b)
                ac.copied(pool, b, "head_spread", 0, alone=tally)
                for i in (1, 3):
                    part = lg[:, i].rearrange("p (h f) -> p h f", f=NF)
                    nc.gpsimd.tensor_tensor(part, part, bcast(negm[:], NF), ALU.add).then_inc(lg_sub_odd.sem, 1)

        @block.scalar
        def _(act):
            act.wait_ge(in_w, 16 * NLOADS)
            nc.scalar.activation(cexp[:], cT[:], ACT.Exp, scale=-1.0).then_inc(s_silu, 1)
            act.wait_ge(s_gate, 1)

            def step(kind, m, i):
                if kind == "h_turn":
                    for k in range(2):
                        h_ps.wait(act, m, k + 1, alone=tally)
                        if k == 0:
                            v_ps.wait(act, m, 0, alone=tally)
                            q_ps.wait(act, m, 0, alone=tally)
                        nc.scalar.activation(hT[:, 2 * P * k:2 * P * (k + 1)], tr.bank(kind, i, k)[:, 0:2 * P],
                                             ACT.Identity, bias=mod[:, 0, bass.ds(m, 1)],
                                             scale=mod[:, 1, bass.ds(m, 1)]).then_inc(tr.sem, 1)
                elif kind == "proj_q":
                    q_ps.wait(act, m, 1)
                    qT_ready.wait(act, m, 0)
                    nc.scalar.activation(qTn[:], tr.bank(kind, i)[:], ACT.Identity, bias=bcol[:, 0:1])\
                        .then_inc(tr.sem, 1)
                elif kind == "proj_k":
                    k_ps.wait(act, m, 1)
                    lg_ps.wait(act, m, 0)
                    ks_ps.wait(act, m, 0)
                    nc.scalar.activation(kT[:], tr.bank(kind, i)[:], ACT.Identity, bias=bcol[:, 1:2])
                    nc.scalar.activation(ksq[:], tr.bank(kind, i)[:], ACT.Square, bias=bcol[:, 1:2])\
                        .then_inc(tr.sem, 1)
                elif kind == "k_sub":
                    (lg_sub, lg_sub_odd)[i % 2].wait(act, m, i // 2 + 1)
                    nc.scalar.activation(lg[:, i], lg[:, i], ACT.Exp).then_inc(e_ready.sem, 1)
                elif kind == "q_shift":
                    lq_shift.wait(act, m, i + 1)
                    phiT_ps.wait(act, m, i - 1)
                    nc.scalar.activation(phi[:, i % 2], pQ[i % 2][:], ACT.Exp).then_inc(phi_ready.sem, 1)
                elif kind == "q_turn":
                    phiT_ps.wait(act, m, i + 1)
                    num_ps.wait(act, m, i - 1)
                    nc.scalar.activation(phiT[:, i % 2], tr.bank(kind, i)[:], ACT.Copy).then_inc(tr.sem, 1)
                elif kind == "ctx_turn":
                    cxT_ps.wait(act, m, i + 1, alone=tally)
                    nc.scalar.activation(cxT[:, bass.ds(m * NT + i, 1), :].rearrange("p a d -> p (a d)"),
                                         tr.bank(kind, i)[:, 0:P], ACT.Copy).then_inc(tr.sem, 1)

            turns(act, FIRST_STEPS, B, step, [tr])
            for b in range(B):
                act.wait_ge(wo_ps, b + 1)
                if b >= 2:
                    act.wait_ge(yt_ps, b - 1)
                nc.scalar.activation(yT[:, b % 2], pK[b % 2][:], ACT.Identity, bias=gab[:, b:b + 1],
                                     scale=mod[:, 2, b:b + 1]).then_inc(y_sb, 1)
            for b in range(B):
                act.wait_ge(h2_ps, b + 1)
                if b >= 2:
                    act.wait_ge(xb_ps, b - 1)
                nc.scalar.activation(h2T[:, b % 2], pK[b % 2][:], ACT.Identity, bias=mod[:, 3, b:b + 1],
                                     scale=mod[:, 4, b:b + 1]).then_inc(h2_sb, 1)

        @block.vector
        def _(dve):
            def statistics(ch, src, b):
                for t in range(b * NT, (b + 1) * NT):
                    ch.count(nc.vector.bn_stats(stats[:, t], src[:, t]))

            def deviations(ch):
                ch.wait()
                for t in range(B * NT):
                    ch.count(nc.vector.bn_aggr(mv[:, t], stats[:, t]))
                ch.wait()
                rsqrt_steps(nc, ch, rs[:], rh[:], rt[:], mv[:, :, 1], LN_EPS, ALU.add)
                ch.end()

            norms[0].start(dve, 0)
            dve.wait_ge(in_x, 16 * B)
            for b in range(B):
                statistics(norms[0], x0, b)
            deviations(norms[0])
            ch0.start(dve, 0)
            dve.wait_ge(s_silu, 1)
            ch0.step(nc.vector.tensor_scalar(cexp[:], cexp[:], 1.0, None, ALU.add))
            ch0.step(nc.vector.reciprocal(cexp[:], cexp[:]))
            nc.vector.tensor_tensor(cT[:], cT[:], cexp[:], ALU.mult).then_inc(s_silu2, 1)
            nc.vector.tensor_copy(identr[:], ident[:]).then_inc(s_silu2, 1)
            dve.wait_ge(s_mod, 1)
            ch0.step(nc.vector.tensor_copy(mod[:], pK[0][:, 0:6 * B].rearrange("p (j b) -> p j b", b=B)))
            for j in (1, 4):
                ch0.step(nc.vector.tensor_scalar(mod[:, j], mod[:, j], 1.0, None, ALU.add))
            for j in (2, 5):
                ch0.step(nc.vector.tensor_scalar(sgn[:], mod[:, j], 0.0, 2.0, ALU.is_ge, ALU.mult))
                ch0.step(nc.vector.tensor_scalar(sgn[:], sgn[:], -1.0, None, ALU.add))
                ch0.step(nc.vector.scalar_tensor_tensor(mod[:, j], mod[:, j], -1.0, mod[:, j], ALU.mult, ALU.max))
                ch0.step(nc.vector.scalar_tensor_tensor(mod[:, j], mod[:, j], 0.25, sgn[:], ALU.max, ALU.mult))
            nc.vector.tensor_scalar(gab[:], mod[:, 2], bcol[:, 2:3], None, ALU.mult).then_inc(s_gate, 1)
            dve.wait_ge(zeroed, 4)
            for signal in (lq_ps, q_max, nm_ready, lq_shift, phi_ready, phiT_ps, num_ps, rd_ready, cx_part, cxT_ps):
                dve.sem_inc(signal.sem, signal.base)

            def step(kind, m, i):
                t, c = divmod(i, 2)
                if kind == "h_apply":
                    h_ps.wait(dve, m, 0)
                    for j in range(NT):
                        tile = bass.ds(m * NT + j, 1)
                        ins = nc.vector.tensor_scalar(hn[:, j], x0[:, tile, :].rearrange("p a d -> p (a d)"),
                                                      mv[:, tile, 0:1].rearrange("p a d -> p (a d)"),
                                                      rs[:, tile], ALU.subtract, ALU.mult)
                    ins.then_inc(hn_ready.sem, 1)
                elif kind == "proj_v":
                    v_ps.wait(dve, m, 1)
                    n_ps.wait(dve, m, 0)
                    nc.vector.tensor_tensor(vext[:, :, :, 0:DH1],
                                            ac.bank(kind, i)[:].rearrange("p (t h d) -> p t h d", t=NT, h=H1),
                                            bvrow[:].rearrange("p (h d) -> p h d", h=H1).unsqueeze(1)
                                            .broadcast_to([P, NT, H1, DH1]), ALU.add).then_inc(ac.sem, 1)
                elif kind == "key_norm":
                    ks_ps.wait(dve, m, 1, alone=tally)
                    lg_used.wait(dve, m, 0, alone=tally)
                    nc.vector.tensor_copy(ksum[:], ac.bank(kind, i)[:, 0:NT * H1]).then_inc(ac.sem, 1)
                elif kind == "k_logits":
                    lg_ps.wait(dve, m, i + 1)
                    if i == 0:
                        ac.copied(dve, m, "key_norm", 0)
                        n_ps.wait(dve, m, 0)
                        mk_ready.wait(dve, m, 0)
                    part = lg[:, t, c * HALF:(c + 1) * HALF].rearrange("p (h f) -> p h f", f=NF)
                    h0 = t * H1 + c * 8
                    nc.vector.tensor_tensor(part, pK[c][:].rearrange("p (h f) -> p h f", f=NF),
                                            bcast(ksum[:, h0:h0 + 8], NF), ALU.add).then_inc(lg_used.sem, 1)
                    lg_used.wait(dve, m, i + 1)
                    nc.vector.tensor_reduce(mk[:, t, c * 8:c * 8 + 8], part, AX.X, ALU.max).then_inc(mk_part.sem, 1)
                elif kind == "head_tokens":
                    mk_part.wait(dve, m, 2 * NT)
                    mkT_ps.wait(dve, m, 0)
                    nc.vector.tensor_reduce(mkt[:], mk[:].rearrange("p t h -> p h t"), AX.X, ALU.max)\
                        .then_inc(mk_ready.sem, 1)
                elif kind == "head_max":
                    mkT_ps.wait(dve, m, 1)
                    negm_ps.wait(dve, m, 0)
                    nc.vector.tensor_reduce(mh[:], ac.bank(kind, i)[0:H1, 0:P], AX.X, ALU.max).then_inc(ac.sem, 1)
                    ac.copied(dve, m, kind, i)
                    nc.vector.tensor_scalar(dm[:], ident[0:H1, 0:H1], mh[:], -1.0, ALU.mult, ALU.mult)\
                        .then_inc(mh_ready.sem, 1)
                elif kind == "head_spread":
                    negm_ps.wait(dve, m, 1, alone=tally)
                    lg_sub.wait(dve, m, 0, alone=tally)
                    lg_sub_odd.wait(dve, m, 0, alone=tally)
                    nc.vector.tensor_copy(negm[:], ac.bank(kind, i)[:, 0:H1]).then_inc(ac.sem, 1)
                elif kind == "k_sub":
                    if i % 2 == 1:
                        return
                    if i == 0:
                        ac.copied(dve, m, "head_spread", 0)
                    part = lg[:, i].rearrange("p (h f) -> p h f", f=NF)
                    nc.vector.tensor_tensor(part, part, bcast(negm[:], NF), ALU.add).then_inc(lg_sub.sem, 1)
                elif kind == "q_move":
                    tr.copied(dve, m, "proj_q", 0, alone=tally)
                    lq_ps.wait(dve, m, 0, alone=tally)
                    nc.vector.tensor_copy(qT[:], qTn[:]).then_inc(qT_ready.sem, 1)
                elif kind == "k_sum" and i == NT - 1:
                    n_ps.wait(dve, m, 1, alone=tally)
                    num_ps.wait(dve, m, 0, alone=tally)
                    dsum_ps.wait(dve, m, 0, alone=tally)
                    nps = ac.bank(kind, i)[:, 0:8 * 18].rearrange("p (g k c) -> p g k c", g=8, k=2)
                    nc.vector.tensor_copy(nxt[0:64, :, 0, :], nps[0:64, :, 0, :])
                    nc.vector.tensor_copy(nxt[64:P, :, 1, :], nps[64:P, :, 1, :])
                    nc.vector.tensor_copy(dcol[0:64, :], nps[0:64, :, 0, DH1])
                    nc.vector.tensor_copy(dcol[64:P, :], nps[64:P, :, 1, DH1]).then_inc(ac.sem, 1)
                elif kind == "k_norm":
                    dsum_ps.wait(dve, m, 1)
                    ac.copied(dve, m, "k_sum", NT - 1)
                    dps = ac.bank(kind, i)
                    nc.vector.scalar_tensor_tensor(nxt[0:64, :, 0, DH1], dps[0:64, 0:8], EPS1, dcol[0:64, :],
                                                   ALU.mult, ALU.add)
                    nc.vector.scalar_tensor_tensor(nxt[64:P, :, 1, DH1], dps[64:P, 0:8], EPS1, dcol[64:P, :],
                                                   ALU.mult, ALU.add).then_inc(ac.sem, 1)
                elif kind == "q_logits":
                    lq_ps.wait(dve, m, i + 1)
                    nm_ready.wait(dve, m, i)
                    nc.vector.tensor_reduce(m1[:], pQ[c][:].rearrange("p (h f) -> p h f", f=NF), AX.X, ALU.max)\
                        .then_inc(q_max.sem, 1)
                    q_max.wait(dve, m, 2 * i + 1)
                    lq_shift.wait(dve, m, i)
                    nc.vector.tensor_scalar(nm1[:, 0], m1[:], -1.0, None, ALU.mult).then_inc(q_max.sem, 1)
                    q_max.wait(dve, m, 2 * i + 2)
                    nc.vector.scalar_tensor_tensor(nm1[:, 1], m1[:], -1.0, nm1[:, 0].bitcast(F32), ALU.mult,
                                                   ALU.subtract).then_inc(nm_ready.sem, 1)
                elif kind == "q_num":
                    num_ps.wait(dve, m, i + 1)
                    cx_part.wait(dve, m, i)
                    v = pN[:, 0:72].rearrange("p (h c) -> p h c", c=DH1 + 1)
                    nc.vector.reciprocal(rd[:], v[:, :, DH1]).then_inc(rd_ready.sem, 1)
                    rd_ready.wait(dve, m, i + 1)
                    if c == 0:
                        cxT_ps.wait(dve, m, t - 1)
                    nc.vector.tensor_tensor(cx[:, t % 2, c * 64:c * 64 + 64].rearrange("p (h d) -> p h d", d=DH1),
                                            v[:, :, 0:DH1], bcast(rd[:], DH1), ALU.mult).then_inc(cx_part.sem, 1)

            turns(dve, FIRST_STEPS, B, step, [ac])
            ch = norms[1]
            ch.start(dve, 0)
            for b in range(B):
                tiles = slice(b * NT, (b + 1) * NT)
                dve.wait_ge(yt_ps, b + 1)
                nc.vector.tensor_tensor(x1s[:, tiles], x0[:, tiles],
                                        pQ[b % 2][:].rearrange("p (t d) -> p t d", d=D), ALU.add)\
                    .then_inc(x1_ready, 1)
                dve.wait_ge(x1_ready, b + 1)
                statistics(ch, x1s, b)
            hn_ready.wait(dve, B, 0)
            deviations(ch)
            for t in range(B * NT):
                ins = nc.vector.tensor_scalar(hn2[:, t], x1s[:, t], mv[:, t, 0:1], rs[:, t:t + 1],
                                              ALU.subtract, ALU.mult)
                if t % NT == NT - 1:
                    ins.then_inc(hn2_ready, 1)
            for b in range(B):
                dve.wait_ge(xb_ps, b + 1)
                nc.vector.tensor_copy(xr[:, b * NT:(b + 1) * NT], pQ[b % 2][:].rearrange("p (t d) -> p t d", d=D))\
                    .then_inc(xr_ready, 1)

        @block.tensor
        def _(pe):
            pe.wait_ge(in_w, 16 * NLOADS)
            pe.wait_ge(s_silu2, 2)
            for j in range(6):
                last = nc.tensor.matmul(pK[0][:, j * B:(j + 1) * B], wmod[:, j * D:(j + 1) * D], cT[:],
                                        start=True, stop=True)
            last.then_inc(s_mod, 1)
            pe.wait_ge(bd, 16 * H1)
            pe.wait_ge(zeroed, 4)
            pe.wait_ge(s_gate, 1)

            def transposes(dst, src):
                for t in range(NT):
                    last = nc.tensor.transpose(dst[:, t * P:(t + 1) * P], src(t), ident[:])
                return last

            def step(kind, m, i):
                t, c = divmod(i, 2)
                if kind == "h_turn":
                    hn_ready.wait(pe, m, 1)
                    for k in range(2):
                        tr.free(pe, m, kind, i, k)
                        for j in range(2):
                            last = nc.tensor.transpose(tr.bank(kind, i, k)[:, j * P:(j + 1) * P],
                                                       hn[:, 2 * k + j], ident[:])
                        last.then_inc(h_ps.sem, 1)
                elif kind == "proj_q":
                    tr.copied(pe, m, "h_turn", 0, 1)
                    tr.free(pe, m, kind, i)
                    nc.tensor.matmul(tr.bank(kind, i)[:], wq[:], hT[:], start=True, stop=True).then_inc(q_ps.sem, 1)
                elif kind == "proj_k":
                    tr.copied(pe, m, "h_turn", 0, 1)
                    tr.free(pe, m, kind, i)
                    nc.tensor.matmul(tr.bank(kind, i)[:], wk[:], hT[:], start=True, stop=True).then_inc(k_ps.sem, 1)
                elif kind == "proj_v":
                    tr.copied(pe, m, "h_turn", 0, 1)
                    ac.free(pe, m, kind, i)
                    for j in range(NT):
                        last = nc.tensor.matmul(ac.bank(kind, i)[:, j * D:(j + 1) * D], hT[:, j * P:(j + 1) * P],
                                                wv[:], start=True, stop=True)
                    last.then_inc(v_ps.sem, 1)
                elif kind == "key_norm":
                    tr.copied(pe, m, "proj_k", 0)
                    ac.free(pe, m, kind, i)
                    for j in range(NT):
                        last = nc.tensor.matmul(ac.bank(kind, i)[:, j * H1:(j + 1) * H1], ksq[:, j * P:(j + 1) * P],
                                                selneg[:], start=True, stop=True)
                    last.then_inc(ks_ps.sem, 1)
                elif kind == "k_logits":
                    if i == 0:
                        tr.copied(pe, m, "proj_k", 0)
                    lg_used.wait(pe, m, i - 1)
                    nc.tensor.matmul(pK[c][:], kT[:, t * P:(t + 1) * P], w0bd[:, c * HALF:(c + 1) * HALF],
                                     start=True, stop=True).then_inc(lg_ps.sem, 1)
                elif kind == "head_max":
                    mk_ready.wait(pe, m, 1)
                    ac.free(pe, m, kind, i)
                    nc.tensor.transpose(ac.bank(kind, i)[0:H1, 0:P], mkt[:], ident[:]).then_inc(mkT_ps.sem, 1)
                elif kind == "head_spread":
                    mh_ready.wait(pe, m, 1)
                    ac.free(pe, m, kind, i)
                    nc.tensor.matmul(ac.bank(kind, i)[:, 0:H1], ones[0:H1, :], dm[:], start=True, stop=True)\
                        .then_inc(negm_ps.sem, 1)
                elif kind == "k_sum":
                    if i == 0:
                        ac.wait(pe, m, kind, i, 0)
                        nc.tensor.matmul(ac.bank(kind, i)[:, 0:8 * 18], ident[0:32, :], w0bd[0:32, HALF:HALF + 8 * 18],
                                         start=True, stop=True)
                    e_ready.wait(pe, m, i + 1)
                    for g in range(H1 // 2):
                        last = nc.tensor.matmul(ac.bank(kind, i)[:, 18 * g:18 * (g + 1)], lg[:, i, g * P:(g + 1) * P],
                                                vext[:, i, 2 * g:2 * g + 2, :], start=False, stop=True,
                                                skip_group_check=True)
                    if i == NT - 1:
                        last.then_inc(n_ps.sem, 1)
                elif kind == "k_norm":
                    ac.copied(pe, m, "k_sum", NT - 1)
                    ac.free(pe, m, kind, i)
                    nc.tensor.matmul(ac.bank(kind, i)[:, 0:8], onesblk[:], dcol[:], start=True, stop=True)\
                        .then_inc(dsum_ps.sem, 1)
                elif kind == "q_logits":
                    if i == 0:
                        qT_ready.wait(pe, m, 1)
                    phi_ready.wait(pe, m, i - 1)
                    nc.tensor.matmul(pQ[c][:], qT[:, t * P:(t + 1) * P], w0bd[:, c * HALF:(c + 1) * HALF],
                                     start=True, stop=True).then_inc(lq_ps.sem, 1)
                elif kind == "q_shift":
                    nm_ready.wait(pe, m, i + 1)
                    dst = pQ[c][:].rearrange("p (h f) -> p h f", f=NF)
                    for j in range(2):
                        last = nc.tensor.matmul(dst, identr[:], bcast(nm1[:, j], NF), start=False, stop=True,
                                                skip_group_check=True)
                    last.then_inc(lq_shift.sem, 1)
                elif kind == "q_turn":
                    phi_ready.wait(pe, m, i + 1)
                    tr.free(pe, m, kind, i)
                    transposes(tr.bank(kind, i), lambda j: phi[:, c, j * P:(j + 1) * P]).then_inc(phiT_ps.sem, 1)
                elif kind == "q_num":
                    if i == 0:
                        ac.copied(pe, m, "k_norm", 0)
                    tr.copied(pe, m, "q_turn", i)
                    cx_part.wait(pe, m, i)
                    for j in range(4):
                        last = nc.tensor.matmul(pN[:, 18 * j:18 * j + 18], phiT[:, c, j * P:(j + 1) * P],
                                                nxt[:, 4 * c + j], start=True, stop=True)
                    last.then_inc(num_ps.sem, 1)
                elif kind == "ctx_turn":
                    cx_part.wait(pe, m, 2 * i + 2)
                    tr.free(pe, m, kind, i)
                    nc.tensor.transpose(tr.bank(kind, i)[:, 0:P], cx[:, i % 2], ident[:]).then_inc(cxT_ps.sem, 1)

            turns(pe, FIRST_STEPS, B, step)
            for b in range(B + 1):
                if b < B:
                    tr.copied(pe, b, "ctx_turn", NT - 1)
                    if b >= 2:
                        pe.wait_ge(y_sb, b - 1)
                    nc.tensor.matmul(pK[b % 2][:], wo[:], cxT[:, b * NT:(b + 1) * NT].rearrange("p t d -> p (t d)"),
                                     start=True, stop=True).then_inc(wo_ps, 1)
                if b >= 1:
                    pe.wait_ge(y_sb, b)
                    if b >= 3:
                        pe.wait_ge(x1_ready, b - 2)
                    transposes(pQ[(b - 1) % 2], lambda t: yT[:, (b - 1) % 2, t * P:(t + 1) * P]).then_inc(yt_ps, 1)
            for b in range(B + 1):
                if b < B:
                    pe.wait_ge(hn2_ready, b + 1)
                    if b >= 2:
                        pe.wait_ge(h2_sb, b - 1)
                    transposes(pK[b % 2], lambda t: hn2[:, b * NT + t]).then_inc(h2_ps, 1)
                if b >= 1:
                    pe.wait_ge(h2_sb, b)
                    if b == 1:
                        pe.wait_ge(x1_ready, B)
                    if b >= 3:
                        pe.wait_ge(xr_ready, b - 2)
                    transposes(pQ[(b - 1) % 2], lambda t: h2T[:, (b - 1) % 2, t * P:(t + 1) * P]).then_inc(xb_ps, 1)


def over_slots():
    steps = []

    def add(kind, i, of):
        steps.append((kind, i // of, i % of))

    for u in range(UNITS):
        t, s = divmod(u, 2)

        def proj(c):
            add("proj", (t + 2) * 6 + 3 * s + c, 6 * NT)

        add("scores", u, UNITS)
        if s == 0:
            add("rotate", t + 1, NT)
        if u == 3:
            add("ffn_norm", -2, 2)
        if u != 4:
            proj(0)
        if u == 3:
            add("ffn_norm", -1, 2)
        if u == 5:
            add("ffn_turn2", -1, 1)
        add("values", 2 * (u - 2), 2 * UNITS)
        if u == 4:
            proj(0)
        if u == 6:
            add("ffn_gate", -1, 3)
        if s == 0:
            proj(1)
        else:
            add("rope", 4 * (t + 1), 4 * NT)
            add("norm", 2 * (t + 2) + 1, 2 * NT)
        add("values", 2 * (u - 2) + 1, 2 * UNITS)
        if u == 3:
            add("ffn_stats", -1, 1)
            add("x_turn", 1, 1)
        if s == 0:
            add("project_out", t - 2, NT)
        else:
            add("rope", 4 * (t + 1) + 1, 4 * NT)
            proj(1)
        if u == 2:
            add("x1", -1, 1)
            add("x_copy", 1, 1)
        if u == 6:
            add("ffn_value", -3, 3)
        add("shift", u, UNITS)
        if s == 1:
            add("rope", 4 * (t + 1) + 2, 4 * NT)
        if u == 3:
            proj(2)
        add("probs", u - 1, UNITS)
        if u == 7:
            add("ffn_value", -1, 3)
        if u == 3:
            add("x_split", 1, 1)
        if s == 1:
            add("scale", t + 2, NT)
        if u == 4:
            add("ffn_apply", -1, 1)
        if u != 3:
            proj(2)
        if s == 1:
            add("rope", 4 * (t + 1) + 3, 4 * NT)
        if u == 6:
            add("ffn_value", -2, 3)
        add("out", u - 2, UNITS)
        if s == 0:
            add("norm", 2 * (t + 2), 2 * NT)
        if u == 2:
            add("ffn_turn", -1, 1)
        if u == 5:
            add("ffn_gate", -3, 3)
            add("ffn_gate", -2, 3)
        if u == 7:
            add("ffn_down", -1, 1)
    return steps


STEPS = over_slots()


def batch_slot(m):
    return (m & (B - 1)) * NT


def layers_block(nc, a, xr, consts):
    ident, identr = consts["ident"], consts["identr"]
    with ExitStack() as ctx:
        def sb(name, shape, dt=F32):
            return ctx.enter_context(nc.sbuf_tensor(name, shape, dt))

        def sem(name):
            return ctx.enter_context(nc.semaphore(name))

        def sig(name, per):
            return Signal(sem(name), per)

        def psum(name):
            return ctx.enter_context(nc.psum_tensor(name, [P, 512], F32))

        wraw = sb("wraw", [P, 3 * INNER])
        whi, wlo = sb("whi", [P, 3 * INNER], F32R), sb("wlo", [P, 3 * INNER], F32R)
        wo = sb("wo2", [P, HP, D])
        w1 = sb("w1", [P, 2 * FF])
        w2 = sb("w2", [P, 3, D])
        b1c = sb("b1c", [P, 2, 3])
        b2r = sb("b2r", [P, D])
        lnc = sb("lnc", [P, 2])
        scr = sb("scr", [P, 4, DH])
        tab = sb("tab", [P, 4, NT, DH])
        mask = sb("mask", [P, 2, 2 * WIN], BF16)
        identb = sb("identb", [P, P], BF16)
        zow = sb("zow", [P, 3])
        zero, one, warm = (zow[:, i:i + 1] for i in range(3))
        xw = sb("xw", [P, NT, D])
        xs = sb("xs", [P, L + 1])
        xh, xl = sb("xh", [P, L], F32R), sb("xl", [P, L], F32R)
        raw = sb("raw", [P, 2, 2, INNER])
        sq = sb("sq", [P, 2, INNER])
        ss, rs, rh, rt = (sb(n, [P, 2 * H + NT]) for n in ("ss2", "rs2", "rh2", "rt2"))
        t1 = sb("t1", [P, 2, INNER])
        t2 = sb("t2", [P, 2, INNER])
        vb = sb("vb", [P, 2, 2 * HALF])
        kT = sb("kT2", [P, HP, WIN + L])
        qT = sb("qT2", [P, 2, HP, P])
        vp = sb("vp", [P, NW, HALF])
        mx = sb("mx", [P, 8])
        nm = sb("nm", [P, 2, 8], F32R)
        pr = sb("pr", [P, 2, HALF])
        mask32 = pr[:, 0, 0:4 * WIN].rearrange("p (t c) -> p t c", t=2)
        den = sb("den", [P, 2, 8])
        pT = sb("pT", [P, 2, HALF])
        ob = sb("ob", [P, 2, HALF])
        oT = sb("oT", [P, 2, HP, P])
        x1w = sb("x1w", [P, NT, D])
        xs2 = sb("xs2", [P, L + 1])
        stats = sb("stats2", [P, NT, 6])
        mv = sb("mv2", [P, NT, 2])
        xnT = sb("xnT", [P, L])
        uT = sb("uT", [P, 3, L])
        xb = sb("xb", [P, NT, D])
        xn = y2 = xb

        pA = [psum(f"pA{i}") for i in range(2)]
        pS = [psum(f"pS{i}") for i in range(2)]
        pY = psum("pY")
        tr = Ring(sem("tr_read"), [psum(f"pT{i}") for i in range(2)],
                  {"x_turn": 1, "probs": 1, "out": 1, "ffn_turn": 1,
                   "ffn_norm": 1, "ffn_turn2": 1, "ffn_gate": 1, "rope": 1}, STEPS)
        ou = Ring(sem("ou_read"), [psum("pO")], {"values": (0, 1), "ffn_value": 1, "ffn_down": 1}, STEPS)

        ld_const, ld_s, ld_wo, ld_f = (sem(n) for n in ("ld_const", "ld_s", "ld_wo", "ld_f"))
        ld_w = [sem(f"ld_w{i}") for i in range(3)]
        consts_up, pads_up = sem("consts_up"), sem("pads_up")
        tally = sem("tally2")
        w_hi, w_lo = sig("w_hi", 6), sig("w_lo", 6)
        tab_ready = sig("tab_ready", 4)
        xw_ready = sig("xw_ready", 1)
        x_ps = sig("x_ps", 1)
        xhl_ready = sig("xhl_ready", 2)
        a_ready = sig("a_ready", 6 * NT)
        a_read = sig("a_read", 6 * NT)
        sq_read = sig("sq_read", 2 * NT)
        v_moved = [sem(f"v_moved{t}") for t in range(NT)]
        qn_ready = sig("qn_ready", 2 * NT)
        t2_ready = sig("t2_ready", 2 * NT)
        t1_ready = sig("t1_ready", 2 * NT)
        rope_ready = sig("rope_ready", 2 * NT)
        r_ps = sig("r_ps", 4 * NT)
        s_ps = sig("s_ps", UNITS)
        nm_ready = sig("nm_ready", UNITS)
        s_shift = sig("s_shift", UNITS)
        p_ready = sig("p_ready", UNITS)
        den_ready = sig("den_ready", UNITS)
        pt_ps = sig("pt_ps", UNITS)
        o_half = sig("o_half", UNITS)
        o_ps = sig("o_ps", UNITS)
        ot_ps = sig("ot_ps", UNITS)
        y_ps = sig("y_ps", NT)
        x1_ready = sig("x1w_ready", 1)
        x1T_ps = sig("x1T_ps", 1)
        xb_ps = sig("xb_ps2", 2)
        xn_ready = sig("xn_ready", 1)
        xnT_ps = sig("xnT_ps", 1)
        g_ps = sig("g_ps", 3)
        u_ps = sig("u_ps", 3)
        f_ps = Signal(sem("f_ps"), 1, 1)
        x_done = Signal(sem("x_done"), 1, 1)
        norm_ch = Chain(sem("norm_chain"), NT * RSQRT_STEPS)
        max_ch = Chain(sem("max_chain"), 2 * UNITS)
        sum_ch = Chain(sem("sum_chain"), UNITS)
        ffn_ch = Chain(sem("ffn_chain"), 2 * NT + 1)
        last_ch = Chain(sem("last_chain"), RSQRT_STEPS)

        NLD_F = 1 + 3 * 3 + 3
        LD_W = [16, 16, 32]
        V_SENT = [16 * (4 * WPT - (2 if t == NT - 1 else 0)) for t in range(NT)]

        block = ctx.enter_context(nc.Block())

        @block.sync
        def _(sp):
            sp.dma_start(mask32, a["mask"]).then_inc(ld_const, 16)

            def load_w(l):
                w_lo.wait(sp, l, 0, alone=tally)
                for j in range(3):
                    dst, src = wraw[:, j * INNER:(j + 1) * INNER], a["Wqkv"][l, :, j * INNER:(j + 1) * INNER]
                    if j == 2:
                        dst = dst.rearrange("p (c m d) -> p c m d", c=2, d=2 * DH)
                        src = src.rearrange("p (m c d) -> p c m d", c=2, d=2 * DH)
                    for c in range(1 if j < 2 else 2):
                        sp.dma_start(dst if j < 2 else dst[:, c], src if j < 2 else src[:, c]).then_inc(ld_w[j], 16)

            def load_tables(l):
                t1_ready.wait(sp, l * B, 0, alone=tally)
                t2_ready.wait(sp, l * B, 0, alone=tally)
                sp.dma_start(tab[:], a["rot"]).then_inc(ld_s, 16)
                for i, name in enumerate(("q_scale", "k_scale")):
                    sp.dma_start(scr[:, 2 * i, :], a[name][l, :].partition_broadcast(P)).then_inc(ld_s, 16)
                    for s in range(2):
                        sp.dma_start(scr[:, 2 * i + 1, s * 32:s * 32 + 32],
                                     a[name][l, (1 - s) * 32:(1 - s) * 32 + 32].partition_broadcast(P))\
                            .then_inc(ld_s, 16)

            def load_wo(l):
                y_ps.wait(sp, l * B, 0, alone=tally)
                for c in range(2):
                    for s in range(2):
                        sp.dma_start(wo[64 * c:64 * c + 64, 4 * s:4 * s + 4, :],
                                     a["Wo"][l].rearrange("(m c s d) n -> d c s m n", c=2, s=2, d=DH)[:, c, s])\
                            .then_inc(ld_wo, 16)

            def load_ffn(l):
                x_done.wait(sp, l * B, 0, alone=tally)
                sp.dma_start(w1[:], a["W1"][l]).then_inc(ld_f, 16)
                for k, (f0, fn) in enumerate(FT):
                    sp.dma_start(w2[0:fn, k, :], a["W2"][l, f0:f0 + fn, :]).then_inc(ld_f, 16)
                    for s in range(2):
                        sp.dma_start(b1c[0:fn, s, k:k + 1],
                                     a["b1"][l, s * FF + f0:s * FF + f0 + fn].unsqueeze(1)).then_inc(ld_f, 16)
                sp.dma_start(b2r[:], a["b2"][l, :].partition_broadcast(P)).then_inc(ld_f, 16)
                sp.dma_start(lnc[:, 0:1], a["ln_g"][l, :].unsqueeze(1)).then_inc(ld_f, 16)
                sp.dma_start(lnc[:, 1:2], a["ln_b"][l, :].unsqueeze(1)).then_inc(ld_f, 16)

            def move_v(m, t):
                a_read.wait(sp, m, 6 * t + 6, alone=tally)
                o_ps.wait(sp, m, min(UNITS, 2 * t + 4) - UNITS, alone=tally)
                for j in range(WPT):
                    for s in range(2):
                        src = vb[WIN * j:WIN * j + WIN, t % 2, s * HALF:(s + 1) * HALF]
                        w = WPT * t + j
                        sp.dma_start(vp[64 * s + WIN:64 * s + 2 * WIN, w], src).then_inc(v_moved[t], 16)
                        if w + 1 < NW:
                            sp.dma_start(vp[64 * s:64 * s + WIN, w + 1], src).then_inc(v_moved[t], 16)

            def move_all(m):
                for t in range(NT):
                    move_v(m, t)

            load_w(0)
            load_tables(0)
            sp.wait_ge(pads_up, 1)
            move_v(0, 0)
            move_v(0, 1)
            load_wo(0)
            move_v(0, 2)
            move_v(0, 3)
            load_ffn(0)
            move_all(1)
            with sp.Fori(1, DEPTH) as l:
                move_all(sp.snap(l * B - 2))
                m = sp.snap(l * B - 1)
                move_v(m, 0)
                move_v(m, 1)
                load_w(l)
                move_v(m, 2)
                move_v(m, 3)
                load_tables(l)
                m = sp.snap(l * B)
                move_v(m, 0)
                move_v(m, 1)
                load_wo(l)
                move_v(m, 2)
                move_v(m, 3)
                m = sp.snap(l * B + 1)
                move_v(m, 0)
                move_v(m, 1)
                load_ffn(l)
                move_v(m, 2)
                move_v(m, 3)
            with sp.Fori(DEPTH * B - 2, DEPTH * B) as m:
                move_all(sp.snap(m))

        @block.gpsimd
        def _(pool):
            def split_w(l, chunks):
                for c in chunks:
                    pool.wait_ge(ld_w[c // 2], LD_W[c // 2] * (l + 1))
                    a_ready.wait(pool, l * B, c + 1 - 6, alone=tally)
                    part = slice(c * HALF, (c + 1) * HALF)
                    nc.gpsimd.tensor_tensor(whi[:, part], wraw[:, part], one.broadcast_to([P, HALF]), ALU.mult)\
                        .then_inc(w_hi.sem, 1)
                    w_hi.wait(pool, l, c + 1)
                    nc.gpsimd.tensor_tensor(wlo[:, part], wraw[:, part], whi[:, part].bitcast(F32), ALU.subtract)\
                        .then_inc(w_lo.sem, 1)

            def tables(l):
                pool.wait_ge(ld_s, l * 112 + 112)
                for i in range(4):
                    nc.gpsimd.tensor_tensor(tab[:, i], tab[:, i], over_heads(scr[:, i], NT), ALU.mult)\
                        .then_inc(tab_ready.sem, 1)
                tab_ready.wait(pool, l, 4, alone=tally)

            def rotate(m, t, i):
                qn_ready.wait(pool, m, 2 * t + i + 1)
                src = raw[:, t % 2, i]
                if i == 0:
                    rope_ready.wait(pool, m, 2 * t)
                for hh in range(2):
                    part = slice(hh * HALF, (hh + 1) * HALF)
                    ins = nc.gpsimd.tensor_tensor(
                        t2[:, i, part].rearrange("p (h s d) -> p h s d", s=2, d=32),
                        halves_swapped(src[:, part]),
                        tab[:, 2 * i + 1, t].rearrange("p (s d) -> p s d", s=2).unsqueeze(1)
                        .broadcast_to([P, 8, 2, 32]), ALU.mult)
                ins.then_inc(t2_ready.sem, 1)
                t2_ready.wait(pool, m, 2 * t + i + 1)
                t1_ready.wait(pool, m, 2 * t + i + 1)
                nc.gpsimd.tensor_tensor(t1[:, i], t1[:, i], t2[:, i], ALU.add).then_inc(rope_ready.sem, 1)

            def rotate_tiles(m, tiles):
                for t in tiles:
                    for i in range(2):
                        rotate(m, t, i)

            pool.wait_ge(consts_up, 1)
            split_w(0, range(6))
            tables(0)
            with pool.Fori(1, DEPTH) as l:
                with pool.Fori((l - 1) * B, l * B - 1) as m:
                    rotate_tiles(pool.snap(m), range(NT))
                m = pool.snap(l * B - 1)
                rotate_tiles(m, range(3))
                split_w(l, range(4))
                rotate(m, 3, 0)
                split_w(l, (4,))
                rotate(m, 3, 1)
                split_w(l, (5,))
                tables(l)
            with pool.Fori((DEPTH - 1) * B, DEPTH * B) as m:
                rotate_tiles(pool.snap(m), range(NT))

        @block.scalar
        def _(act):
            def shifted(dst, src):
                nc.scalar.activation(dst[0:64, 0:L], src[0:64, :], ACT.Copy)
                nc.scalar.activation(dst[64:P, 1:L + 1], src[64:P, :], ACT.Copy).then_inc(tr.sem, 1)

            def step(kind, m, i):
                t, s = divmod(i, 2)
                if kind == "x_turn":
                    x_ps.wait(act, m, 1)
                    xhl_ready.wait(act, m, 0)
                    shifted(xs, tr.bank(kind, i))
                elif kind == "proj":
                    t, c = divmod(i, 6)
                    a_ready.wait(act, m, i + 1)
                    src = pA[c % 2][:]
                    if c < 4:
                        j, hh = divmod(c, 2)
                        part = slice(hh * HALF, (hh + 1) * HALF)
                        if hh == 0:
                            sq_read.wait(act, m, 2 * t + j - 1)
                            rope_ready.wait(act, m, 2 * (t - 2) + j + 1)
                        nc.scalar.activation(raw[:, t % 2, j, part], src, ACT.Copy)
                        nc.scalar.activation(sq[:, j, part], src, ACT.Square).then_inc(a_read.sem, 1)
                    else:
                        if c == 4:
                            k = (t - 2) % NT
                            times = m + 1 if t >= 2 else m
                            if not isinstance(times, int) or times > 0:
                                act.wait_ge(v_moved[k], times * V_SENT[k])
                        nc.scalar.activation(vb[:, t % 2, (c - 4) * HALF:(c - 3) * HALF], src, ACT.Copy)\
                            .then_inc(a_read.sem, 1)
                elif kind == "rope":
                    t, j, hh = i // 4, i // 2 % 2, i % 2
                    r_ps.wait(act, m, i + 1)
                    src = tr.bank(kind, i)[:].rearrange("p (k c) -> p k c", c=P)
                    if j == 0:
                        s_ps.wait(act, m, 2 * t + 2 - 4)
                        dst = qT[:, t % 2, 4 * hh:4 * hh + 4, :]
                    else:
                        s_ps.wait(act, m, min(UNITS, 2 * t + 4) - UNITS)
                        dst = kT[:, 4 * hh:4 * hh + 4, WIN + t * P:WIN + (t + 1) * P]
                    nc.scalar.activation(dst, src, ACT.Copy).then_inc(tr.sem, 1)
                elif kind == "shift":
                    s_shift.wait(act, m, i + 1)
                    pt_ps.wait(act, m, i - 1)
                    den_ready.wait(act, m, i - 1)
                    nc.scalar.activation(pr[:, i % 2], pS[i % 2][:], ACT.Exp).then_inc(p_ready.sem, 1)
                elif kind == "probs":
                    pt_ps.wait(act, m, i + 1)
                    o_ps.wait(act, m, i - 1)
                    nc.scalar.activation(pT[:, i % 2], tr.bank(kind, i)[:], ACT.Copy).then_inc(tr.sem, 1)
                elif kind == "out":
                    ot_ps.wait(act, m, i + 1)
                    if s == 0:
                        y_ps.wait(act, m, t - 1)
                    nc.scalar.activation(oT[:, t % 2, 4 * s:4 * s + 4, :],
                                         tr.bank(kind, i)[:].rearrange("p (k c) -> p k c", c=P), ACT.Copy)\
                        .then_inc(tr.sem, 1)
                elif kind == "ffn_turn":
                    x1T_ps.wait(act, m, 1)
                    shifted(xs2, tr.bank(kind, i))
                elif kind == "ffn_norm":
                    xb_ps.wait(act, m, i + 1)
                    if i == 0:
                        x_done.wait(act, m, 0)
                    nc.scalar.activation(xb[:, 2 * i:2 * i + 2], tr.bank(kind, i)[:, 0:2 * D].rearrange(
                        "p (t d) -> p t d", d=D), ACT.Copy).then_inc(tr.sem, 1)
                elif kind == "ffn_turn2":
                    xnT_ps.wait(act, m, 1)
                    act.wait_ge(ld_f, (m >> 2) * (16 * NLD_F) + 16 * NLD_F)
                    nc.scalar.activation(xnT[:], tr.bank(kind, i)[:], ACT.Identity, bias=lnc[:, 1:2],
                                         scale=lnc[:, 0:1]).then_inc(tr.sem, 1)
                elif kind == "ffn_gate":
                    fn = FT[i][1]
                    g_ps.wait(act, m, i + 1)
                    f_ps.wait(act, m, 0)
                    nc.scalar.activation(uT[0:fn, i], tr.bank(kind, i)[0:fn, :], ACT.Gelu,
                                         bias=b1c[0:fn, 1, i:i + 1]).then_inc(tr.sem, 1)
                    if i == 2:
                        nc.scalar.activation(warm, zero, ACT.Exp)

            act.sem_inc(f_ps.sem, 1)
            act.wait_ge(consts_up, 1)
            turns(act, STEPS, DEPTH * B, step, [tr])

        @block.vector
        def _(dve):
            dve.wait_ge(ld_const, 16)
            nc.vector.memset(zero, 0.0)
            nc.vector.memset(one, 1.0)
            nc.vector.memset(ss[:, 2 * H:], 1.0)
            nc.vector.memset(xs[64:P, 0:1], 0.0)
            nc.vector.memset(xs2[64:P, 0:1], 0.0)
            nc.vector.memset(kT[:, :, 0:WIN], 0.0)
            nc.vector.memset(vp[0:WIN, 0, :], 0.0)
            nc.vector.memset(vp[64:64 + WIN, 0, :], 0.0).then_inc(pads_up, 1)
            nc.vector.tensor_copy(mask[:], mask32)
            nc.vector.tensor_copy(identb[:], ident[:]).then_inc(consts_up, 1)
            dve.wait_ge(consts_up, 1)

            def step(kind, m, i):
                t, s = divmod(i, 2)
                if kind == "x_copy":
                    x_ps.wait(dve, m, 0, alone=tally)
                    x_done.wait(dve, m, -2, alone=tally)
                    nc.vector.tensor_copy(xw[:], xr[:, bass.ds(batch_slot(m), NT), :]).then_inc(xw_ready.sem, 1)
                elif kind == "x_split":
                    tr.copied(dve, m, "x_turn", 0)
                    a_ready.wait(dve, m, 0)
                    nc.vector.tensor_copy(xh[:], xs[:, 0:L]).then_inc(xhl_ready.sem, 1)
                    xhl_ready.wait(dve, m, 1)
                    nc.vector.tensor_tensor(xl[:], xs[:, 0:L], xh[:].bitcast(F32), ALU.subtract)\
                        .then_inc(xhl_ready.sem, 1)
                elif kind == "norm":
                    a_read.wait(dve, m, 6 * t + 2 * s + 2)
                    nc.vector.tensor_reduce(ss[:, s * H:(s + 1) * H],
                                            sq[:, s].rearrange("p (h d) -> p h d", d=DH), AX.X, ALU.add)\
                        .then_inc(sq_read.sem, 1)
                elif kind == "scale":
                    sq_read.wait(dve, m, 2 * i + 2)
                    if i == NT - 1:
                        ffn_ch.start(dve, m, 0)
                        if not isinstance(m, int) or m > 0:
                            ffn_ch.wait()
                    cols = slice(0, 2 * H + (NT if i == NT - 1 else 0))
                    norm_ch.start(dve, m, i * RSQRT_STEPS)
                    rsqrt_steps(nc, norm_ch, rs[:, cols], rh[:, cols], rt[:, cols], ss[:, cols], NORM_FLOOR2, ALU.max)
                    for j in range(2):
                        q = raw[:, i % 2, j].rearrange("p (h d) -> p h d", d=DH)
                        nc.vector.tensor_tensor(q, q, bcast(rs[:, j * H:(j + 1) * H], DH), ALU.mult)\
                            .then_inc(qn_ready.sem, 1)
                elif kind == "rotate":
                    wait_for(dve, tab_ready.sem, (m >> 2) * 4 + 4)
                    for j in range(2):
                        q = raw[:, i % 2, j].rearrange("p (h d) -> p h d", d=DH)
                        qn_ready.wait(dve, m, 2 * i + j + 1)
                        r_ps.wait(dve, m, 4 * (i - 1) + 2 * j + 2)
                        nc.vector.tensor_tensor(t1[:, j].rearrange("p (h d) -> p h d", d=DH), q,
                                                over_heads(tab[:, 2 * j, i], H), ALU.mult).then_inc(t1_ready.sem, 1)
                elif kind == "scores":
                    max_ch.start(dve, m, 2 * i)
                    s_ps.wait(dve, m, i + 1)
                    nm_ready.wait(dve, m, i)
                    max_ch.step(nc.vector.tensor_reduce(mx[:], pS[i % 2][:].rearrange("p (h c) -> p h c", c=64),
                                                        AX.X, ALU.max))
                    s_shift.wait(dve, m, i)
                    max_ch.step(nc.vector.tensor_scalar(nm[:, 0], mx[:], -1.0, None, ALU.mult))
                    nc.vector.scalar_tensor_tensor(nm[:, 1], mx[:], -1.0, nm[:, 0].bitcast(F32), ALU.mult,
                                                   ALU.subtract).then_inc(nm_ready.sem, 1)
                elif kind == "probs":
                    sum_ch.start(dve, m, i)
                    p_ready.wait(dve, m, i + 1)
                    sum_ch.step(nc.vector.tensor_reduce(den[:, i % 2], pr[:, i % 2].rearrange("p (h c) -> p h c", c=64),
                                                        AX.X, ALU.add))
                    nc.vector.reciprocal(den[:, i % 2], den[:, i % 2]).then_inc(den_ready.sem, 1)
                elif kind == "values":
                    if s == 0:
                        return
                    i = t
                    o_ps.wait(dve, m, i + 1)
                    den_ready.wait(dve, m, i + 1)
                    ot_ps.wait(dve, m, i - 1)
                    nc.vector.tensor_tensor(ob[:, i % 2].rearrange("p (h d) -> p h d", d=DH),
                                            ou.bank(kind, 2 * i + 1)[:].rearrange("p (h d) -> p h d", d=DH),
                                            bcast(den[:, i % 2], DH), ALU.mult).then_inc(ou.sem, 1)
                elif kind == "x1":
                    y_ps.wait(dve, m, NT)
                    nc.vector.tensor_tensor(x1w[:], xr[:, bass.ds(batch_slot(m), NT), :],
                                            pY[:].rearrange("p (t d) -> p t d", d=D), ALU.add).then_inc(x1_ready.sem, 1)
                elif kind == "ffn_stats":
                    ffn_ch.start(dve, m)
                    tr.copied(dve, m, "ffn_norm", 1, alone=tally)
                    for j in range(NT):
                        ffn_ch.count(nc.vector.bn_stats(stats[:, j], xb[:, j]))
                    ffn_ch.wait(alone=tally)
                    for j in range(NT):
                        ffn_ch.count(nc.vector.bn_aggr(mv[:, j], stats[:, j]))
                    ffn_ch.wait()
                    ffn_ch.count(nc.vector.tensor_scalar(ss[:, 2 * H:], mv[:, :, 1], LN_EPS, None, ALU.add))
                elif kind == "ffn_apply":
                    cols = slice(2 * H, 2 * H + NT)
                    if isinstance(m, int) and m == DEPTH * B - 1:
                        ffn_ch.start(dve, m, 2 * NT + 1)
                        ffn_ch.wait()
                        last_ch.start(dve, 0)
                        rsqrt_steps(nc, last_ch, rs[:, cols], rh[:, cols], rt[:, cols], ss[:, cols], NORM_FLOOR2,
                                    ALU.max)
                    for j in range(NT):
                        ins = nc.vector.tensor_scalar(xn[:, j], xb[:, j], mv[:, j, 0:1],
                                                      rs[:, 2 * H + j:2 * H + j + 1], ALU.subtract, ALU.mult)
                    ins.then_inc(xn_ready.sem, 1)
                elif kind == "ffn_value":
                    fn = FT[i][1]
                    u_ps.wait(dve, m, i + 1)
                    tr.copied(dve, m, "ffn_gate", i)
                    nc.vector.scalar_tensor_tensor(uT[0:fn, i], ou.bank(kind, i)[0:fn, :], b1c[0:fn, 0, i:i + 1],
                                                   uT[0:fn, i], ALU.add, ALU.mult).then_inc(ou.sem, 1)
                elif kind == "ffn_down":
                    f_ps.wait(dve, m, 1)
                    ou.copied(dve, m, "ffn_value", 2)
                    nc.vector.tensor_tensor(y2[:], ou.bank(kind, i)[:].rearrange("p (t d) -> p t d", d=D),
                                            b2r[:].unsqueeze(1).broadcast_to([P, NT, D]), ALU.add).then_inc(ou.sem, 1)
                    ou.copied(dve, m, kind, i)
                    nc.vector.tensor_tensor(xr[:, bass.ds(batch_slot(m), NT), :], y2[:], x1w[:], ALU.add)\
                        .then_inc(x_done.sem, 1)

            dve.sem_inc(x_done.sem, 1)
            turns(dve, STEPS, DEPTH * B, step, [ou])

        @block.tensor
        def _(pe):
            def transposes(dst, src):
                for t in range(4):
                    last = nc.tensor.transpose(dst[:, t * P:(t + 1) * P], src(t), ident[:])
                return last

            def step(kind, m, i):
                t, s = divmod(i, 2)
                if kind == "x_turn":
                    xw_ready.wait(pe, m, 1)
                    tr.free(pe, m, kind, i)
                    transposes(tr.bank(kind, i), lambda j: xw[:, j]).then_inc(x_ps.sem, 1)
                elif kind == "proj":
                    t, c = divmod(i, 6)
                    xt = slice(t * P, (t + 1) * P)
                    if i == 0:
                        xhl_ready.wait(pe, m, 2)
                    if t == 0:
                        wait_for(pe, w_lo.sem, (m >> 2) * 6 + c + 1)
                    a_read.wait(pe, m, i - 1)
                    for j, (x, w) in enumerate(((xh, whi), (xl, whi), (xh, wlo))):
                        last = nc.tensor.matmul(pA[c % 2][:], x[:, xt], w[:, c * HALF:(c + 1) * HALF],
                                                start=(j == 0), stop=(j == 2))
                    last.then_inc(a_ready.sem, 1)
                elif kind == "rope":
                    t, j, hh = i // 4, i // 2 % 2, i % 2
                    rope_ready.wait(pe, m, 2 * t + j + 1)
                    tr.free(pe, m, kind, i)
                    transposes(tr.bank(kind, i),
                               lambda k: t1[:, j, (4 * hh + k) * P:(4 * hh + k + 1) * P]).then_inc(r_ps.sem, 1)
                elif kind == "scores":
                    bank = pS[i % 2]
                    if s == 0:
                        tr.copied(pe, m, "rope", 4 * t + 3)
                    p_ready.wait(pe, m, i - 1)
                    nc.tensor.matmul(bank[:].rearrange("p (h c) -> p h c", c=64), identb[:],
                                     over_heads(mask[:, min(t, 1)], 8), start=True, stop=True)
                    part = slice(64 * s, 64 * s + 64)
                    for g in range(HP):
                        for j in range(WPT):
                            k0 = t * P + j * WIN
                            last = nc.tensor.matmul(bank[WIN * j:WIN * (j + 1), 64 * g:64 * (g + 1)],
                                                    qT[part, t % 2, g, WIN * j:WIN * (j + 1)],
                                                    kT[part, g, k0:k0 + 2 * WIN], start=False, stop=True,
                                                    skip_group_check=True)
                    last.then_inc(s_ps.sem, 1)
                elif kind == "shift":
                    dst = pS[i % 2][:].rearrange("p (h c) -> p h c", c=64)
                    nm_ready.wait(pe, m, i + 1)
                    for j in range(2):
                        last = nc.tensor.matmul(dst, identr[:], bcast(nm[:, j], 64), start=False, stop=True,
                                                skip_group_check=True)
                    last.then_inc(s_shift.sem, 1)
                elif kind == "probs":
                    p_ready.wait(pe, m, i + 1)
                    tr.free(pe, m, kind, i)
                    transposes(tr.bank(kind, i), lambda j: pr[:, i % 2, j * P:(j + 1) * P]).then_inc(pt_ps.sem, 1)
                elif kind == "values":
                    i, c = divmod(i, 2)
                    t, s = divmod(i, 2)
                    bank = ou.bank(kind, 2 * i)
                    if c == 0:
                        tr.copied(pe, m, "probs", i)
                        if s == 0:
                            pe.wait_ge(v_moved[t], m * V_SENT[t] + V_SENT[t])
                        ou.free(pe, m, kind, 2 * i, alone=tally)
                    else:
                        o_half.wait(pe, m, i + 1, alone=tally)
                    part = slice(64 * c, 64 * c + 64)
                    for k in range(4):
                        g, v = 2 * k + c, 2 * k + s
                        for j in range(WPT):
                            last = nc.tensor.matmul(bank[WIN * j:WIN * (j + 1), 64 * g:64 * (g + 1)],
                                                    pT[part, i % 2, k * P + WIN * j:k * P + WIN * (j + 1)],
                                                    vp[part, WPT * t + j, 64 * v:64 * (v + 1)],
                                                    start=True, stop=True)
                    last.then_inc((o_half, o_ps)[c].sem, 1)
                elif kind == "out":
                    ou.copied(pe, m, "values", 2 * i + 1)
                    tr.free(pe, m, kind, i)
                    transposes(tr.bank(kind, i), lambda j: ob[:, i % 2, j * P:(j + 1) * P]).then_inc(ot_ps.sem, 1)
                elif kind == "project_out":
                    tr.copied(pe, m, "out", 2 * i + 1)
                    if i == 0:
                        pe.wait_ge(ld_wo, (m >> 2) * 64 + 64)
                        x1_ready.wait(pe, m, 0)
                    for g in range(HP):
                        last = nc.tensor.matmul(pY[:, i * D:(i + 1) * D], oT[:, i % 2, g, :], wo[:, g, :],
                                                start=(g == 0), stop=(g == HP - 1))
                    last.then_inc(y_ps.sem, 1)
                elif kind == "ffn_turn":
                    x1_ready.wait(pe, m, 1)
                    tr.free(pe, m, kind, i)
                    transposes(tr.bank(kind, i), lambda j: x1w[:, j]).then_inc(x1T_ps.sem, 1)
                elif kind == "ffn_norm":
                    if i == 0:
                        tr.copied(pe, m, "ffn_turn", 0)
                    tr.free(pe, m, kind, i)
                    for j in range(2):
                        last = nc.tensor.transpose(tr.bank(kind, i)[:, j * P:(j + 1) * P],
                                                   xs2[:, (2 * i + j) * P:(2 * i + j + 1) * P], ident[:])
                    last.then_inc(xb_ps.sem, 1)
                elif kind == "ffn_turn2":
                    xn_ready.wait(pe, m, 1)
                    tr.free(pe, m, kind, i)
                    transposes(tr.bank(kind, i), lambda j: xn[:, j]).then_inc(xnT_ps.sem, 1)
                elif kind == "ffn_gate":
                    f0, fn = FT[i]
                    if i == 0:
                        pe.wait_ge(ld_f, (m >> 2) * (16 * NLD_F) + 16 * NLD_F)
                        tr.copied(pe, m, "ffn_turn2", 0)
                    tr.free(pe, m, kind, i)
                    nc.tensor.matmul(tr.bank(kind, i)[0:fn, :], w1[:, FF + f0:FF + f0 + fn], xnT[:],
                                     start=True, stop=True).then_inc(g_ps.sem, 1)
                elif kind == "ffn_value":
                    f0, fn = FT[i]
                    ou.free(pe, m, kind, i)
                    nc.tensor.matmul(ou.bank(kind, i)[0:fn, :], w1[:, f0:f0 + fn], xnT[:], start=True, stop=True)\
                        .then_inc(u_ps.sem, 1)
                elif kind == "ffn_down":
                    ou.free(pe, m, kind, i)
                    for j in range(NT):
                        for k, (f0, fn) in enumerate(FT):
                            last = nc.tensor.matmul(ou.bank(kind, i)[:, j * D:(j + 1) * D],
                                                    uT[0:fn, k, j * P:(j + 1) * P], w2[0:fn, k, :],
                                                    start=(k == 0), stop=(k == 2))
                    last.then_inc(f_ps.sem, 1)

            pe.wait_ge(consts_up, 1)
            turns(pe, STEPS, DEPTH * B, step)


def final_block(nc, xr, x1_dram, out, mod, consts):
    ident = consts["ident"]
    with ExitStack() as ctx:
        def sem(name):
            return ctx.enter_context(nc.semaphore(name))

        x1 = ctx.enter_context(nc.sbuf_tensor("x1f", [P, B, NT, D], F32))
        xc = ctx.enter_context(nc.sbuf_tensor("xcf", [P, B, NT, D], F32))
        gT = ctx.enter_context(nc.sbuf_tensor("gTf", [P, B, L], F32))
        res = ctx.enter_context(nc.sbuf_tensor("resf", [P, B, NT, D], F32))
        ps = [ctx.enter_context(nc.psum_tensor(f"f{i}", [P, 512], F32)) for i in range(8)]
        loaded, turned, gated, back, done, stored = (sem(n) for n in ("x1_loaded", "turned", "gated", "turned_back",
                                                                      "out_ready", "out_stored"))
        block = ctx.enter_context(nc.Block())

        @block.sync
        def _(sp):
            for b in range(B):
                sp.dma_start(x1[:, b], x1_dram[b]).then_inc(loaded, 16)
            for b in range(B):
                sp.wait_ge(done, b + 1)
                sp.dma_start(out[b].rearrange("(t p) d -> p t d", p=P), res[:, b]).then_inc(stored, 16)
            sp.wait_ge(stored, 16 * B)

        @block.tensor
        def _(pe):
            for b in range(B):
                for t in range(NT):
                    last = nc.tensor.transpose(ps[b][:, t * P:(t + 1) * P], xr[:, b * NT + t, :], ident[:])
                last.then_inc(turned, 1)
            for b in range(B):
                pe.wait_ge(gated, b + 1)
                for t in range(NT):
                    last = nc.tensor.transpose(ps[4 + b][:, t * P:(t + 1) * P], gT[:, b, t * P:(t + 1) * P], ident[:])
                last.then_inc(back, 1)

        @block.scalar
        def _(act):
            for b in range(B):
                act.wait_ge(turned, b + 1)
                nc.scalar.activation(gT[:, b], ps[b][:], ACT.Copy, scale=mod[:, 5, b:b + 1]).then_inc(gated, 1)

        @block.vector
        def _(dve):
            dve.wait_ge(loaded, 16 * B)
            for b in range(B):
                dve.wait_ge(back, b + 1)
                nc.vector.tensor_tensor(res[:, b], ps[4 + b][:].rearrange("p (t d) -> p t d", d=D), x1[:, b], ALU.add)\
                    .then_inc(done, 1)


def build(nc, a, out):
    with ExitStack() as ctx:
        xr = ctx.enter_context(nc.sbuf_tensor("xr", [P, B * NT, D], F32))
        mod = ctx.enter_context(nc.sbuf_tensor("mod", [P, 6, B], F32))
        consts = {n: ctx.enter_context(nc.sbuf_tensor(n, [P, P], dt)) for n, dt in (("ident", F32), ("identr", F32R))}
        x1_dram = nc.dram_tensor("x1_scratch", (B, P, NT, D), F32).ap()
        attention1_block(nc, a, xr, x1_dram, mod, consts)
        layers_block(nc, a, xr, consts)
        final_block(nc, xr, x1_dram, out, mod, consts)


def constants():
    f = np.float32
    half = np.arange(0, DH, 2, dtype=f)
    inv_freq = (f(1.0) / np.power(f(10000.0), half / f(DH), dtype=f)).astype(f)
    pos = np.arange(L, dtype=f)
    ang = pos[:, None] * inv_freq[None, :]
    base = ((half + f(0.4 * DH)) / f(1.4 * DH)).astype(f)
    power = ((pos - L // 2) / (WIN // 2)).astype(f)
    scale = np.power(base[None, :], power[:, None], dtype=f)
    cos, sin = np.cos(ang).astype(f), np.sin(ang).astype(f)
    rot = np.empty((4, L, DH), f)
    for i, (s, m) in enumerate(((scale, QK_SCALE), (f(1.0) / scale, 1.0))):
        rot[2 * i] = np.concatenate([cos * s, cos * s], -1) * f(m)
        rot[2 * i + 1] = np.concatenate([-sin * s, sin * s], -1) * f(m)
    rot = np.ascontiguousarray(rot.reshape(4, NT, P, DH).transpose(2, 0, 1, 3))
    mask = np.zeros((P, 2, 2 * WIN), f)
    i = np.arange(P)[:, None] % WIN
    j = np.arange(2 * WIN)[None, :] - WIN
    mask[:, :] = np.where((i < j) | (i > j + WIN), f(MASKED), f(0))[:, None]
    mask[0:WIN, 0, 0:WIN] = MASKED
    onesblk = np.kron(np.eye(2, dtype=f), np.ones((64, 64), f))
    selneg = np.kron(np.eye(H1, dtype=f), np.full((DH1, 1), -0.5, f))
    return {"rot": rot, "mask": mask, "ident": np.eye(P, dtype=f), "onesblk": onesblk, "selneg": selneg}


def kernel(**inputs):
    import concourse.bacc as bacc
    from concourse.bass_utils import run_bass_kernel_spmd

    x = {k: np.ascontiguousarray(v) for k, v in inputs.items()}
    arrays = {"x": x["L0_attn_x"], "Wrf": x["L0_attn_Wrf"], "bv": x["L0_attn_bv"], "wmod": x["L0_wmod"],
              "cT": np.ascontiguousarray(x["L0_c"].T)}
    for w in ("Wq", "Wk", "Wv", "Wo"):
        arrays[w + "T"] = np.ascontiguousarray(x["L0_attn_" + w].T)
    arrays["bcol"] = np.ascontiguousarray(np.stack([x["L0_attn_" + n] for n in ("bq", "bk", "bo")], 1))
    for w in ("Wqkv", "q_scale", "k_scale", "Wo", "ln_g", "ln_b", "W1", "b1", "W2", "b2"):
        arrays[w] = x["L0_ffn_" + w]
    arrays.update(constants())
    nc = bacc.Bacc("TRN2", target_bir_lowering=False, num_devices=1)
    a = {k: nc.dram_tensor("in_" + k, v.shape, mybir.dt.from_np(v.dtype), kind="ExternalInput").ap()
         for k, v in arrays.items()}
    out = nc.dram_tensor("out", (B, L, D), F32, kind="ExternalOutput").ap()
    build(nc, a, out)
    r = run_bass_kernel_spmd(nc, [{"in_" + k: v for k, v in arrays.items()}], core_ids=[0])
    return r.results[0]["out"]
```
